# Optimizing a Trainium2 kernel written in Bass

```python
import numpy as np
import jax
import jax.numpy as jnp

def _softmax(x, axis=-1):
    return jax.nn.softmax(x, axis=axis)

def _gelu(x):
    return jax.nn.gelu(x, approximate=True)

def _silu(x):
    return jax.nn.silu(x)

def _sigmoid(x):
    return jax.nn.sigmoid(x)

def _layernorm(x, axis=-1, eps=1e-05):
    m = jnp.mean(x, axis=axis, keepdims=True)
    v = jnp.var(x, axis=axis, keepdims=True)
    return (x - m) / jnp.sqrt(v + eps)

def _scatter_add(tgt, idx, src, axis=0):
    return tgt.at[idx].add(src)

def _segment_sum(src, seg, n):
    return jax.ops.segment_sum(src, seg, n)
kernel_name = 'mk_gnn_preln_d4_gnn_r8_6bb0fb'

def setup_inputs(seed: int=0):
    np.random.seed(seed)
    _w = jnp.asarray

    def _rec_inputs():
        import jax
        import jax.numpy as jnp
        _gk = jax.random.key(seed)
        x = -0.001003 + 1 * jax.random.normal(jax.random.fold_in(_gk, 1), (256, 768), jnp.float32)
        src = jax.random.randint(jax.random.fold_in(_gk, 2), (8192,), 0, 256, jnp.int32)
        dst = jnp.minimum((256 * jax.random.uniform(jax.random.fold_in(_gk, 3), (8192,)) ** 2.0).astype(jnp.int32), 2047)
        _o = jnp.argsort(dst, stable=True)
        src = src[_o]
        dst = dst[_o]
        edge_type_3 = jax.random.randint(jax.random.fold_in(_gk, 12), (8192,), 0, 3, jnp.int32)
        return (x, src, dst, edge_type_3)
    x, src, dst, edge_type_3 = _rec_inputs()

    def _L0_gnn_setup():
        import jax, jax.numpy as jnp
        import numpy as np
        NUM_RELATIONS = 3

        def _rgcn(x, W_rel, W_root, bias, src, dst, etype):
            n = x.shape[0]
            xr = jnp.einsum('ni,rio->rno', x, W_rel)
            msg = xr[etype, src]
            out = x @ W_root + bias
            for r in range(NUM_RELATIONS):
                m = etype == r
                s = jax.ops.segment_sum(jnp.where(m[:, None], msg, 0.0), dst, num_segments=n)
                c = jax.ops.segment_sum(m.astype(x.dtype), dst, num_segments=n)
                out = out + s / jnp.maximum(c, 1.0)[:, None]
            return out

        def _gate(h, q, Wg, bg, Wq, bq):
            B, L, F = q.shape
            N = h.shape[0] // B
            h3 = h.reshape(B, N, F)
            hg = jnp.einsum('bnf,gf->bng', h3, Wg[:, :F])
            qg = jnp.einsum('blf,gf->blg', q, Wg[:, F:]) + bg
            attn = jax.nn.sigmoid(hg[:, :, None, :] + qg[:, None, :, :])
            qi = jnp.einsum('bnlf,blf->bnf', attn, q)
            alpha = jax.nn.sigmoid(jnp.einsum('bnf,gf->bng', h3, Wq[:, :F]) + jnp.einsum('bnf,gf->bng', qi, Wq[:, F:]) + bq)
            hn = alpha * jnp.tanh(qi) + (1.0 - alpha) * h3
            return hn.reshape(B * N, F)
        key = jax.random.key(seed)
        ks = jax.random.split(key, 16)
        F = 768
        BN, E, B, L = (256, 8192, 8, 64)
        s = 0.02
        return {'x': jax.random.normal(ks[0], (BN, F), jnp.float32), 'edge_index': jax.random.randint(ks[1], (2, E), 0, BN), 'edge_type': jax.random.randint(ks[2], (E,), 0, NUM_RELATIONS), 'query_embs': jax.random.normal(ks[3], (B, L, F), jnp.float32), 'W_rel1': jax.random.normal(ks[4], (NUM_RELATIONS, F, F), jnp.float32) * s, 'W_root1': jax.random.normal(ks[5], (F, F), jnp.float32) * s, 'b1': jnp.zeros((F,), jnp.float32), 'W_rel2': jax.random.normal(ks[6], (NUM_RELATIONS, F, F), jnp.float32) * s, 'W_root2': jax.random.normal(ks[7], (F, F), jnp.float32) * s, 'b2': jnp.zeros((F,), jnp.float32), 'Wg': jax.random.normal(ks[8], (F, 2 * F), jnp.float32) * s, 'bg': jnp.zeros((F,), jnp.float32), 'Wq': jax.random.normal(ks[9], (F, 2 * F), jnp.float32) * s, 'bq': jnp.zeros((F,), jnp.float32)}
    _L0_gnn_all = _L0_gnn_setup()
    _L0_gnn_in = {k: v for k, v in _L0_gnn_all.items() if k in ('query_embs', 'W_rel1', 'W_root1', 'b1', 'W_rel2', 'W_root2', 'b2', 'Wg', 'bg', 'Wq', 'bq')}
    del _L0_gnn_all

    def _L1_gnn_setup():
        import jax, jax.numpy as jnp
        import numpy as np
        N = 2500
        E_RAND = 40000
        NEG_SLOPE = 0.2

        def gat_layer(x, W, a_src, a_dst, bias, src, dst, heads, out_c, concat):
            n = x.shape[0]
            h = (x @ W).reshape(n, heads, out_c)
            al_s = jnp.einsum('nhc,hc->nh', h, a_src)
            al_d = jnp.einsum('nhc,hc->nh', h, a_dst)
            e = jax.nn.leaky_relu(al_s[src] + al_d[dst], NEG_SLOPE)
            m = jax.ops.segment_max(e, dst, num_segments=n)
            ex = jnp.exp(e - m[dst])
            z = jax.ops.segment_sum(ex, dst, num_segments=n)
            alpha = ex / (z[dst] + 1e-16)
            msg = h[src] * alpha[:, :, None]
            out = jax.ops.segment_sum(msg, dst, num_segments=n)
            out = out.reshape(n, heads * out_c) if concat else out.mean(axis=1)
            return out + bias
        key = jax.random.key(seed)
        ks = jax.random.split(key, 10)
        x = jax.random.normal(ks[0], (N, 768), dtype=jnp.float32)
        src = jax.random.randint(ks[1], (E_RAND,), 0, N)
        dst = jax.random.randint(ks[2], (E_RAND,), 0, N)
        loop = jnp.arange(N)
        edge_index = jnp.stack([jnp.concatenate([src, loop]), jnp.concatenate([dst, loop])])
        s = 1.0 / np.sqrt(768.0)
        W1 = jax.random.normal(ks[3], (768, 768), dtype=jnp.float32) * s
        a_src1 = jax.random.normal(ks[4], (8, 96), dtype=jnp.float32) * 0.1
        a_dst1 = jax.random.normal(ks[5], (8, 96), dtype=jnp.float32) * 0.1
        b1 = jnp.zeros((768,), dtype=jnp.float32)
        W2 = jax.random.normal(ks[6], (768, 768), dtype=jnp.float32) * s
        a_src2 = jax.random.normal(ks[7], (1, 768), dtype=jnp.float32) * 0.1
        a_dst2 = jax.random.normal(ks[8], (1, 768), dtype=jnp.float32) * 0.1
        b2 = jnp.zeros((768,), dtype=jnp.float32)
        return {'x': x, 'edge_index': edge_index, 'W1': W1, 'a_src1': a_src1, 'a_dst1': a_dst1, 'b1': b1, 'W2': W2, 'a_src2': a_src2, 'a_dst2': a_dst2, 'b2': b2}
    _L1_gnn_all = _L1_gnn_setup()
    _L1_gnn_in = {k: v for k, v in _L1_gnn_all.items() if k in ('W1', 'a_src1', 'a_dst1', 'b1', 'W2', 'a_src2', 'a_dst2', 'b2')}
    del _L1_gnn_all

    def _L2_gnn_setup():
        import jax, jax.numpy as jnp
        import numpy as np
        N_NODES = 1250
        N_EDGES = 20000
        NEG_SLOPE = 0.2

        def _gat_layer(x, src, dst, W, a_src, a_dst, bias, concat):
            N = x.shape[0]
            H, C = a_src.shape
            h = (x @ W).reshape(N, H, C)
            al_s = jnp.einsum('nhc,hc->nh', h, a_src)
            al_d = jnp.einsum('nhc,hc->nh', h, a_dst)
            e = jax.nn.leaky_relu(al_s[src] + al_d[dst], NEG_SLOPE)
            m = jax.ops.segment_max(e, dst, num_segments=N)
            ex = jnp.exp(e - m[dst])
            denom = jax.ops.segment_sum(ex, dst, num_segments=N)
            alpha = ex / (denom[dst] + 1e-16)
            msg = h[src] * alpha[:, :, None]
            out = jax.ops.segment_sum(msg, dst, num_segments=N)
            out = out.reshape(N, H * C) if concat else out.mean(axis=1)
            return out + bias
        key = jax.random.key(seed)
        ks = jax.random.split(key, 10)
        in_dim, hid, out_dim, heads = (768, 512, 768, 4)
        x = jax.random.normal(ks[0], (N_NODES, in_dim), dtype=jnp.float32)
        edge_index = jax.random.randint(ks[1], (2, N_EDGES), 0, N_NODES, dtype=jnp.int64)
        g = lambda k, shape, fan: jax.random.normal(k, shape, jnp.float32) / np.sqrt(fan)
        return {'x': x, 'edge_index': edge_index, 'W1': g(ks[2], (in_dim, heads * hid), in_dim), 'att_src1': g(ks[3], (heads, hid), hid), 'att_dst1': g(ks[4], (heads, hid), hid), 'b1': jnp.zeros((heads * hid,), jnp.float32), 'W2': g(ks[5], (heads * hid, out_dim), heads * hid), 'att_src2': g(ks[6], (1, out_dim), out_dim), 'att_dst2': g(ks[7], (1, out_dim), out_dim), 'b2': jnp.zeros((out_dim,), jnp.float32)}
    _L2_gnn_all = _L2_gnn_setup()
    _L2_gnn_in = {k: v for k, v in _L2_gnn_all.items() if k in ('W1', 'att_src1', 'att_dst1', 'b1', 'W2', 'att_src2', 'att_dst2', 'b2')}
    del _L2_gnn_all

    def _L3_gnn_setup():
        import jax, jax.numpy as jnp
        import numpy as np
        N_NODES = 1250
        key = jax.random.key(seed)
        k1, k2, k3 = jax.random.split(key, 3)
        x = jax.random.normal(k1, (N_NODES, 768), dtype=jnp.float32)
        edge_index = jax.random.randint(k2, (2, 12500), 0, N_NODES, dtype=jnp.int32)
        W = jax.random.normal(k3, (768, 768), dtype=jnp.float32) * (1.0 / np.sqrt(768))
        b = jnp.zeros((768,), dtype=jnp.float32)
        return {'x': x, 'edge_index': edge_index, 'W': W, 'b': b}
    _L3_gnn_all = _L3_gnn_setup()
    _L3_gnn_in = {k: v for k, v in _L3_gnn_all.items() if k in ('W', 'b')}
    del _L3_gnn_all
    return {'x': x, 'src': src, 'dst': dst, 'edge_type_3': edge_type_3, 'L0_gnn_query_embs': _L0_gnn_in['query_embs'], 'L0_gnn_W_rel1': _L0_gnn_in['W_rel1'], 'L0_gnn_W_root1': _L0_gnn_in['W_root1'], 'L0_gnn_b1': _L0_gnn_in['b1'], 'L0_gnn_W_rel2': _L0_gnn_in['W_rel2'], 'L0_gnn_W_root2': _L0_gnn_in['W_root2'], 'L0_gnn_b2': _L0_gnn_in['b2'], 'L0_gnn_Wg': _L0_gnn_in['Wg'], 'L0_gnn_bg': _L0_gnn_in['bg'], 'L0_gnn_Wq': _L0_gnn_in['Wq'], 'L0_gnn_bq': _L0_gnn_in['bq'], 'L1_gnn_W1': _L1_gnn_in['W1'], 'L1_gnn_a_src1': _L1_gnn_in['a_src1'], 'L1_gnn_a_dst1': _L1_gnn_in['a_dst1'], 'L1_gnn_b1': _L1_gnn_in['b1'], 'L1_gnn_W2': _L1_gnn_in['W2'], 'L1_gnn_a_src2': _L1_gnn_in['a_src2'], 'L1_gnn_a_dst2': _L1_gnn_in['a_dst2'], 'L1_gnn_b2': _L1_gnn_in['b2'], 'L2_gnn_W1': _L2_gnn_in['W1'], 'L2_gnn_att_src1': _L2_gnn_in['att_src1'], 'L2_gnn_att_dst1': _L2_gnn_in['att_dst1'], 'L2_gnn_b1': _L2_gnn_in['b1'], 'L2_gnn_W2': _L2_gnn_in['W2'], 'L2_gnn_att_src2': _L2_gnn_in['att_src2'], 'L2_gnn_att_dst2': _L2_gnn_in['att_dst2'], 'L2_gnn_b2': _L2_gnn_in['b2'], 'L3_gnn_W': _L3_gnn_in['W'], 'L3_gnn_b': _L3_gnn_in['b']}

def reference(x, src, dst, edge_type_3, L0_gnn_query_embs, L0_gnn_W_rel1, L0_gnn_W_root1, L0_gnn_b1, L0_gnn_W_rel2, L0_gnn_W_root2, L0_gnn_b2, L0_gnn_Wg, L0_gnn_bg, L0_gnn_Wq, L0_gnn_bq, L1_gnn_W1, L1_gnn_a_src1, L1_gnn_a_dst1, L1_gnn_b1, L1_gnn_W2, L1_gnn_a_src2, L1_gnn_a_dst2, L1_gnn_b2, L2_gnn_W1, L2_gnn_att_src1, L2_gnn_att_dst1, L2_gnn_b1, L2_gnn_W2, L2_gnn_att_src2, L2_gnn_att_dst2, L2_gnn_b2, L3_gnn_W, L3_gnn_b):
    import jax
    import jax.numpy as jnp

    def _L0_gnn_ref(x, edge_index, edge_type, query_embs, W_rel1, W_root1, b1, W_rel2, W_root2, b2, Wg, bg, Wq, bq):
        import jax, jax.numpy as jnp
        import numpy as np
        NUM_RELATIONS = 3

        def _rgcn(x, W_rel, W_root, bias, src, dst, etype):
            n = x.shape[0]
            xr = jnp.einsum('ni,rio->rno', x, W_rel)
            msg = xr[etype, src]
            out = x @ W_root + bias
            for r in range(NUM_RELATIONS):
                m = etype == r
                s = jax.ops.segment_sum(jnp.where(m[:, None], msg, 0.0), dst, num_segments=n)
                c = jax.ops.segment_sum(m.astype(x.dtype), dst, num_segments=n)
                out = out + s / jnp.maximum(c, 1.0)[:, None]
            return out

        def _gate(h, q, Wg, bg, Wq, bq):
            B, L, F = q.shape
            N = h.shape[0] // B
            h3 = h.reshape(B, N, F)
            hg = jnp.einsum('bnf,gf->bng', h3, Wg[:, :F])
            qg = jnp.einsum('blf,gf->blg', q, Wg[:, F:]) + bg
            attn = jax.nn.sigmoid(hg[:, :, None, :] + qg[:, None, :, :])
            qi = jnp.einsum('bnlf,blf->bnf', attn, q)
            alpha = jax.nn.sigmoid(jnp.einsum('bnf,gf->bng', h3, Wq[:, :F]) + jnp.einsum('bnf,gf->bng', qi, Wq[:, F:]) + bq)
            hn = alpha * jnp.tanh(qi) + (1.0 - alpha) * h3
            return hn.reshape(B * N, F)
        src, dst = (edge_index[0], edge_index[1])
        h = jax.nn.relu(_rgcn(x, W_rel1, W_root1, b1, src, dst, edge_type))
        h = _gate(h, query_embs, Wg, bg, Wq, bq)
        h = jax.nn.relu(_rgcn(h, W_rel2, W_root2, b2, src, dst, edge_type))
        h = _gate(h, query_embs, Wg, bg, Wq, bq)
        return h

    def _L1_gnn_ref(x, edge_index, W1, a_src1, a_dst1, b1, W2, a_src2, a_dst2, b2):
        import jax, jax.numpy as jnp
        import numpy as np
        N = 2500
        E_RAND = 40000
        NEG_SLOPE = 0.2

        def gat_layer(x, W, a_src, a_dst, bias, src, dst, heads, out_c, concat):
            n = x.shape[0]
            h = (x @ W).reshape(n, heads, out_c)
            al_s = jnp.einsum('nhc,hc->nh', h, a_src)
            al_d = jnp.einsum('nhc,hc->nh', h, a_dst)
            e = jax.nn.leaky_relu(al_s[src] + al_d[dst], NEG_SLOPE)
            m = jax.ops.segment_max(e, dst, num_segments=n)
            ex = jnp.exp(e - m[dst])
            z = jax.ops.segment_sum(ex, dst, num_segments=n)
            alpha = ex / (z[dst] + 1e-16)
            msg = h[src] * alpha[:, :, None]
            out = jax.ops.segment_sum(msg, dst, num_segments=n)
            out = out.reshape(n, heads * out_c) if concat else out.mean(axis=1)
            return out + bias
        src, dst = (edge_index[0], edge_index[1])
        h = gat_layer(x, W1, a_src1, a_dst1, b1, src, dst, heads=8, out_c=96, concat=True)
        h = jax.nn.elu(h)
        out = gat_layer(h, W2, a_src2, a_dst2, b2, src, dst, heads=1, out_c=768, concat=False)
        return out

    def _L2_gnn_ref(x, edge_index, W1, att_src1, att_dst1, b1, W2, att_src2, att_dst2, b2):
        import jax, jax.numpy as jnp
        import numpy as np
        N_NODES = 1250
        N_EDGES = 20000
        NEG_SLOPE = 0.2

        def _gat_layer(x, src, dst, W, a_src, a_dst, bias, concat):
            N = x.shape[0]
            H, C = a_src.shape
            h = (x @ W).reshape(N, H, C)
            al_s = jnp.einsum('nhc,hc->nh', h, a_src)
            al_d = jnp.einsum('nhc,hc->nh', h, a_dst)
            e = jax.nn.leaky_relu(al_s[src] + al_d[dst], NEG_SLOPE)
            m = jax.ops.segment_max(e, dst, num_segments=N)
            ex = jnp.exp(e - m[dst])
            denom = jax.ops.segment_sum(ex, dst, num_segments=N)
            alpha = ex / (denom[dst] + 1e-16)
            msg = h[src] * alpha[:, :, None]
            out = jax.ops.segment_sum(msg, dst, num_segments=N)
            out = out.reshape(N, H * C) if concat else out.mean(axis=1)
            return out + bias
        N = x.shape[0]
        loops = jnp.arange(N, dtype=edge_index.dtype)
        src = jnp.concatenate([edge_index[0], loops])
        dst = jnp.concatenate([edge_index[1], loops])
        h = jax.nn.elu(_gat_layer(x, src, dst, W1, att_src1, att_dst1, b1, concat=True))
        out = _gat_layer(h, src, dst, W2, att_src2, att_dst2, b2, concat=False)
        return out

    def _L3_gnn_ref(x, edge_index, W, b):
        import jax, jax.numpy as jnp
        import numpy as np
        N_NODES = 1250
        n = x.shape[0]
        loops = jnp.arange(n, dtype=edge_index.dtype)
        row = jnp.concatenate([edge_index[0], loops])
        col = jnp.concatenate([edge_index[1], loops])
        ones = jnp.ones(row.shape[0], dtype=x.dtype)
        deg = jax.ops.segment_sum(ones, col, num_segments=n)
        dinv = jnp.where(deg > 0, jax.lax.rsqrt(deg), 0.0)
        norm = dinv[row] * dinv[col]
        h = x @ W
        msg = h[row] * norm[:, None]
        out = jax.ops.segment_sum(msg, col, num_segments=n) + b
        return out
    edge_index = jnp.stack([src, dst])
    h = jnp.maximum(_layernorm(x, axis=-1), 0.0)
    x = x + _L0_gnn_ref(h, edge_index, edge_type_3, L0_gnn_query_embs, L0_gnn_W_rel1, L0_gnn_W_root1, L0_gnn_b1, L0_gnn_W_rel2, L0_gnn_W_root2, L0_gnn_b2, L0_gnn_Wg, L0_gnn_bg, L0_gnn_Wq, L0_gnn_bq)
    h = jnp.maximum(_layernorm(x, axis=-1), 0.0)
    x = x + _L1_gnn_ref(h, edge_index, L1_gnn_W1, L1_gnn_a_src1, L1_gnn_a_dst1, L1_gnn_b1, L1_gnn_W2, L1_gnn_a_src2, L1_gnn_a_dst2, L1_gnn_b2)
    h = jnp.maximum(_layernorm(x, axis=-1), 0.0)
    x = x + _L2_gnn_ref(h, edge_index, L2_gnn_W1, L2_gnn_att_src1, L2_gnn_att_dst1, L2_gnn_b1, L2_gnn_W2, L2_gnn_att_src2, L2_gnn_att_dst2, L2_gnn_b2)
    h = jnp.maximum(_layernorm(x, axis=-1), 0.0)
    x = x + _L3_gnn_ref(h, edge_index, L3_gnn_W, L3_gnn_b)
    return x

_drawn_inputs = setup_inputs


def setup_inputs(seed=0):
    import zlib

    import numpy as np

    out = dict(_drawn_inputs(seed))
    spreads = {'L0_gnn_b1': (0.0, 0.622),
     'L0_gnn_b2': (0.0, 0.1),
     'L0_gnn_bg': (0.0, 0.522),
     'L0_gnn_bq': (0.0, 0.658),
     'L1_gnn_b1': (0.0, 0.1),
     'L1_gnn_b2': (0.0, 0.1),
     'L2_gnn_b1': (0.0, 0.1),
     'L2_gnn_b2': (0.0, 0.1),
     'L3_gnn_b': (0.0, 0.1)}
    factors = {'L1_gnn_a_dst1': 31.139,
     'L1_gnn_a_src2': 8.0,
     'L1_gnn_a_dst2': 8.0,
     'L2_gnn_att_src1': 3.682,
     'L2_gnn_att_dst1': 8.0,
     'L2_gnn_att_src2': 8.0,
     'L2_gnn_att_dst2': 64.0}
    for name, (base, spread) in spreads.items():
        noise = np.random.default_rng([zlib.crc32(name.encode()), seed]).standard_normal(out[name].shape)
        drawn = base * np.exp(spread * noise) if base else spread * noise
        out[name] = jnp.asarray(drawn.astype(out[name].dtype))
    for name, factor in factors.items():
        out[name] = (out[name] * factor).astype(out[name].dtype)
    return out
```

```python
from contextlib import ExitStack

import concourse.bass as bass
from concourse import mybir

F32 = mybir.dt.float32
F32R = mybir.dt.float32r
BF16 = mybir.dt.bfloat16
FP16 = mybir.dt.float16
I32 = mybir.dt.int32
ALU = mybir.AluOpType
ACT = mybir.ActivationFunctionType
AX = mybir.AxisListType

P = 128
N = 256
NT = N // P
D = 768
KT = D // P
R = 3
E = 8192
ET = E // P
B = 8
NB = N // B
LQ = 64
QT = B * LQ // P
EPS_LN = 1e-5
EPS_SM = 1e-16
NO_EDGE = -1e30
SLOPE = 0.2
BLK = 6 * 256

H1, C1 = 8, 96
H2, C2W = 4, 512
CT2 = H2 * C2W // P

RAW, SPL = 4, 3

QG = 0
REL = (3, 24)
ROOT = (12, 33)
HG = (15, 36)
WQ = (18, 39)
G1A, G1B = 45, 49
G2A, G2B = 53, 61
GCN = 69
NBLK = 72

LAGR = 2
ZR = 3
PR = 3
CH = NB * 32
CPB = 2 * KT
GC = 4


def build(nc, ins, out):
    ctx = ExitStack()
    with ctx:
        def alloc(stack, name, shape, dt=F32):
            return stack.enter_context(nc.sbuf_tensor(name, shape, dt))

        wraw = alloc(ctx, "wraw", [P, RAW, BLK])
        wH = alloc(ctx, "wH", [P, SPL, BLK], F32R)
        wL = alloc(ctx, "wL", [P, SPL, BLK], F32R)
        eye = alloc(ctx, "eye", [P, NT, N])
        ones = alloc(ctx, "ones", [P, P], F32R)
        cnt = alloc(ctx, "cnt", [P, NT, N])
        cntS = alloc(ctx, "cntS", [P, NT, N], F32R)
        mask = alloc(ctx, "mask", [P, 2, NT, N])
        bcol = alloc(ctx, "bcol", [P, 48])
        dinv = alloc(ctx, "dinv", [P, NT])
        stat = alloc(ctx, "stat", [P, NT, 2, 6])
        mv = alloc(ctx, "mv", [P, NT, 2])
        var = alloc(ctx, "var", [P, NT])
        std = alloc(ctx, "std", [P, NT])
        rstd = alloc(ctx, "rstd", [P, NT])
        identity = eye[:, 0, 0:P]

        l0 = ctx.enter_context(ExitStack())
        qgH = alloc(l0, "qgH", [P, QT, D], F32R)
        qgL = alloc(l0, "qgL", [P, QT, D], F32R)
        cnH = alloc(l0, "cnH", [P, NT, R, N], F32R)
        cnL = alloc(l0, "cnL", [P, NT, R, N], F32R)
        sel = alloc(l0, "sel", [P, 2, 512], F32R)
        qT = alloc(l0, "qT", [P, KT, B * LQ])
        hnat0 = alloc(l0, "hnat0", [P, NT, D])
        hs = l0.enter_context(ExitStack())
        hT = [(alloc(hs, "hTH0", [P, KT, N], F32R), alloc(hs, "hTL0", [P, KT, N], F32R))]
        hs.close()
        hgH = alloc(l0, "hgH", [P, NT, D], F32R)
        hgL = alloc(l0, "hgL", [P, NT, D], F32R)
        h32 = hnat0[:, :, :].rearrange("p t (a b) -> p (t a) b", b=N)
        first = l0.enter_context(ExitStack())
        x_in = alloc(first, "x_in", [P, NT, D])
        qTH = alloc(first, "qTH", [P, KT, B * LQ], F32R)
        qTL = alloc(first, "qTL", [P, KT, B * LQ], F32R)
        cr = alloc(first, "cr", [P, NT, R, N], F32R)
        cn32 = alloc(first, "cn32", [P, NT, R, N])
        sel32 = cn32[:, :, :, :].rearrange("p t r n -> p (t r n)")[:, 0:1024]
        iota32 = alloc(first, "iota32", [P, R * N])
        iota = alloc(first, "iota", [P, R * N], FP16)
        edge_i = alloc(first, "edge_i", [P, 3, ET], I32)
        edge_f = alloc(first, "edge_f", [P, 3, ET])
        key = alloc(first, "key", [P, ET])
        ohS = alloc(first, "ohS", [P, 4, N], BF16)
        ohD = alloc(first, "ohD", [P, 4, R, N], BF16)
        first.close()
        h2H = alloc(l0, "h2H", [P, KT, N], F32R)
        h2L = alloc(l0, "h2L", [P, KT, N], F32R)
        qiH = alloc(l0, "qiH", [P, KT, N], F32R)
        qiL = alloc(l0, "qiL", [P, KT, N], F32R)
        rel = l0.enter_context(ExitStack())
        xrH = alloc(rel, "xrH", [P, NT, R * D], F32R)
        xrL = alloc(rel, "xrL", [P, NT, R * D], F32R)
        rel.close()
        gate = l0.enter_context(ExitStack())
        lhs = alloc(gate, "lhs", [P, 2, 2, D], F32R)
        prod = alloc(gate, "prod", [P, PR, CH])
        fold = alloc(gate, "fold", [P, PR, CH // 2])
        th = alloc(gate, "th", [P, KT, N])
        gate.close()
        al32 = prod[:, :, :].rearrange("p a b -> p (a b)")[:, 0:3 * 512].rearrange("p (j n) -> p j n", j=3)
        l0.close()

        gl = ctx.enter_context(ExitStack())
        x = alloc(gl, "x", [P, NT, D])
        brow = alloc(gl, "brow", [P, D])
        arow2 = alloc(gl, "arow2", [P, 2, D])
        gTH = alloc(gl, "gTH", [P, CT2, N], F32R)
        gTL = alloc(gl, "gTL", [P, CT2, N], F32R)
        hH = alloc(gl, "hH", [P, NT, H2 * C2W], F32R)
        hL = alloc(gl, "hL", [P, NT, H2 * C2W], F32R)
        hT.append((alloc(gl, "hTH1", [P, KT, N], F32R), alloc(gl, "hTL1", [P, KT, N], F32R)))
        alp = alloc(gl, "alp", [P, 2, NT, 8])
        al = alloc(gl, "al", [P, 2, NT, 8])
        mx = alloc(gl, "mx", [P, NT, 8])
        xs = alloc(gl, "xs", [P, NT, 8])
        ms = alloc(gl, "ms", [P, NT, 8])
        bb = alloc(gl, "bb", [P, 2, NT, 8])
        als2 = alloc(gl, "als2", [P, NT, 8])
        rz = alloc(gl, "rz", [P, 2, N])
        zr = alloc(gl, "zr", [P, NT])
        ys = gl.enter_context(ExitStack())
        arow1 = alloc(ys, "arow1", [P, 2, H2 * C2W])
        ys.close()
        ys = gl.enter_context(ExitStack())
        e1 = alloc(ys, "e1", [P, 2, NT, N])
        e2 = alloc(ys, "e2", [P, 2, NT, N])
        gmax = alloc(ys, "gmax", [P, NT, N])
        pt = alloc(ys, "pt", [P, 2, NT, N])
        ptH = alloc(ys, "ptH", [P, 2, NT, N], F32R)
        ptL = alloc(ys, "ptL", [P, 2, NT, N], F32R)
        zs = gl.enter_context(ExitStack())
        hnat1 = alloc(zs, "hnat1", [P, NT, D])
        tmp = alloc(zs, "tmp", [P, 4, 384])
        zs.close()
        u = alloc(gl, "u", [P, 2, 4, N])
        ru = alloc(gl, "ru", [P, 2, 4, N])

        ps = ctx.enter_context(nc.psum_tensor("ps", [P, 8, 512], F32))

        def banks(a, n):
            return ps[:, a:a + n, :].rearrange("p a b -> p (a b)")

        def f(ap):
            return ap.bitcast(F32)

        sems = {}
        for name in """ld_x ld_const ld_sel ld_edge ld_q ld_bcol w_hi w_lo w_used chain achain pchain
                ln_var ln_std ln_h lnT lnH lnL edges_ready oh_ready oh_used counts_mm cr_ready cnt_ready
                sel_ready ones_ready colsum_mm cntT_mm mask_ready deg_ready sdeg cn_ready qT_ready qg_hi qg_lo
                rel_hi rel_lo root_h h2_ready hg_hi hg_lo lhs_in lhs_in1 z_ready sig_ready mul_ready fold_ready red_done
                qi_ready sum_step sum_hi th_ready alpha_ready hn_ready hn_lo hnT x_res x_ready arow1_in arow2_in brow_in xb_ready
                gh_hi gh_free gh_lo al_ready als_rows max_ready brows_ready brow_mm exps_ready pt_ready pt_hi pt_lo
                out_mm rz_ready u_ready act_u elu_ready gt_ready fin_mm lay_done stored""".split():
            sems[name] = ctx.enter_context(nc.semaphore(name))
        w_in = [ctx.enter_context(nc.semaphore(f"w_in{s}")) for s in range(RAW)]

        def S(name):
            return sems[name]

        def mm3(pe, dst, a, b, start, stop, **kw):
            pe.matmul(dst, a[0], b[0], start=start, stop=False, **kw)
            pe.matmul(dst, a[0], b[1], start=False, stop=False, **kw)
            return pe.matmul(dst, a[1], b[0], start=False, stop=stop, **kw)

        def wblock(i, k, w, p=P):
            s = i % SPL
            return tuple(t[0:p, s, 0:k * w].rearrange("p (k w) -> p k w", k=k) for t in (wH, wL))

        block = ctx.enter_context(nc.Block())

        @block.sync
        def _(sp):
            sp.dma_start(x_in[:], ins["x"].rearrange("(t p) d -> p t d", p=P)).then_inc(S("ld_x"), 16)
            sp.dma_start(edge_i[:], ins["edges"].rearrange("k p t -> p k t")).then_inc(S("ld_edge"), 16)
            sp.dma_start(iota32[:], ins["iota"]).then_inc(S("ld_const"), 16)
            sp.dma_start(eye[:], ins["eye"]).then_inc(S("ld_const"), 16)

            def weights(i0, i1):
                for i in range(i0, i1):
                    if i >= RAW:
                        sp.wait_ge(S("w_lo"), i - RAW + 1)
                    sp.dma_start(wraw[:, i % RAW, :], ins["weights"][i]).then_inc(w_in[i % RAW], 16)

            weights(0, 2)
            sp.dma_start(sel32, ins["sel"]).then_inc(S("ld_sel"), 16)
            sp.dma_start(qT[:], ins["qT"]).then_inc(S("ld_q"), 16)
            sp.dma_start(bcol[:], ins["bcol"]).then_inc(S("ld_bcol"), 16)

            def rows(g, b, par, wait):
                if wait is not None:
                    sp.wait_ge(S("z_ready"), wait)
                sem = S("lhs_in1") if par else S("lhs_in")
                for part, (hg, qg) in enumerate(((hgH, qgH), (hgL, qgL))):
                    for half in range(2):
                        q0 = (b % 2) * LQ + 32 * half
                        sp.dma_start(f(lhs[32 * part:32 * part + 32, par, half, :]),
                                     f(hg[NB * (b % 4):NB * (b % 4) + NB, b // 4, :])).then_inc(sem, 16)
                        sp.dma_start(f(lhs[64 + 32 * part:96 + 32 * part, par, half, :]),
                                     f(qg[q0:q0 + 32, b // 2, :])).then_inc(sem, 16)

            done = 2
            for g in range(2):
                weights(done, HG[g] + 3 + RAW)
                done = HG[g] + 3 + RAW
                sp.wait_ge(S("qg_lo"), 3)
                sp.wait_ge(S("hg_lo"), 3 * (g + 1))
                for b in range(B):
                    rows(g, b, b % 2, None if b < 2 else g * B * CPB + CPB * (b - 1))
            sp.wait_ge(S("z_ready"), 2 * B * CPB)
            sp.dma_start(x[:], ins["x"].rearrange("(t p) d -> p t d", p=P)).then_inc(S("x_res"), 16)
            weights(done, NBLK)
            sp.wait_ge(S("lay_done"), 3)
            for t in range(NT):
                sp.dma_start(out[t * P:(t + 1) * P, :], x[:, t, :]).then_inc(S("stored"), 16)
            sp.wait_ge(S("stored"), 16 * NT)

        @block.tensor
        def _(pe):
            def w_wait(i):
                pe.wait_ge(S("w_lo"), i + 1)

            def transposes(k):
                src = hnat0 if k == 0 else hnat1
                pe.wait_ge(S("ln_h"), 2 * (k + 1))
                dst = banks(0, 3).rearrange("p (k n) -> p k n", k=KT)
                for t in range(NT):
                    for kt in range(KT):
                        m = pe.transpose(dst[:, kt, t * P:(t + 1) * P], src[:, t, kt * P:(kt + 1) * P], identity)
                m.then_inc(S("lnT"), 1)

            def natural(i, bank, a, w=256, k=KT, kp=P):
                w_wait(i)
                wb = wblock(i, k, w, kp)
                for t in range(NT):
                    for kt in range(k):
                        m = mm3(pe, ps[:, bank, t * w:(t + 1) * w],
                                tuple(h[0:kp, kt, t * P:(t + 1) * P] for h in a),
                                tuple(q[:, kt, :] for q in wb), kt == 0, kt == k - 1)
                m.then_inc(S("w_used"), 1)

            pe.wait_ge(S("ld_const"), 32)
            transposes(0)

            def count_tile(t, k, start, stop):
                pe.wait_ge(S("oh_ready"), t + 1)
                oh = ohD[:, k, :, :].rearrange("p r n -> p (r n)")
                for st in range(NT):
                    s = ohS[:, k, st * P:(st + 1) * P]
                    pe.matmul(ps[:, 4 + 2 * st, :], s, oh[:, 0:512], start=start, stop=stop)
                    m = pe.matmul(ps[:, 5 + 2 * st, 0:256], s, oh[:, 512:768], start=start, stop=stop)
                m.then_inc(S("oh_used"), 1)

            for k in range(4):
                count_tile(k, k, k == 0, False)
            with pe.Fori(1, ET // 4 - 1) as g:
                for k in range(4):
                    count_tile(g * 4 + k, k, False, False)
            for k in range(4):
                count_tile(ET - 4 + k, k, False, k == 3)

            pe.wait_ge(S("lnL"), 1)
            pe.wait_ge(S("qT_ready"), 2)
            for j in range(3):
                i = QG + j
                w_wait(i)
                if j >= 2:
                    pe.wait_ge(S("qg_lo"), j - 1)
                wb = wblock(i, KT, 256)
                for rt in range(QT):
                    for kt in range(KT):
                        m = mm3(pe, ps[:, 2 * (j % 2) + rt // 2, (rt % 2) * 256:(rt % 2) * 256 + 256],
                                (qTH[:, kt, rt * P:(rt + 1) * P], qTL[:, kt, rt * P:(rt + 1) * P]),
                                tuple(q[:, kt, :] for q in wb), kt == 0, kt == KT - 1)
                m.then_inc(S("w_used"), 1)
                if j == 0:
                    pe.wait_ge(S("cnt_ready"), 4)
                    pe.wait_ge(S("cr_ready"), 1)
                    pe.wait_ge(S("ones_ready"), 1)
                    for st in range(NT):
                        c = cr[:, st, :, :].rearrange("p r n -> p (r n)")
                        pe.matmul(ps[:, 4, :], ones[:], c[:, 0:512], start=st == 0, stop=st == 1)
                        m = pe.matmul(ps[:, 5, 0:256], ones[:], c[:, 512:768], start=st == 0, stop=st == 1)
                    m.then_inc(S("colsum_mm"), 1)
                    for st in range(NT):
                        for dt in range(NT):
                            m = pe.transpose(ps[:, 6, dt * N + st * P:dt * N + (st + 1) * P],
                                             cnt[:, st, dt * P:(dt + 1) * P], identity)
                    m.then_inc(S("cntT_mm"), 1)

            for g in range(2):
                ht = hT[0]
                pe.wait_ge(S("qg_lo"), 3)
                if g:
                    pe.wait_ge(S("hn_lo"), 3)
                for j in range(9):
                    if j >= 4:
                        pe.wait_ge(S("rel_lo"), 9 * g + j - 3)
                    natural(REL[g] + j, j % 4, ht)
                pe.wait_ge(S("rel_lo"), 9 * (g + 1))
                pe.wait_ge(S("cn_ready"), 1)
                for j in range(3):
                    i = ROOT[g] + j
                    w_wait(i)
                    wb = wblock(i, KT, 256)
                    for o in range(2):
                        ot = 2 * j + o
                        dst = ps[:, j, o * N:(o + 1) * N]
                        for r in range(R):
                            for st in range(NT):
                                c0 = r * D + ot * P
                                mm3(pe, dst, (xrH[:, st, c0:c0 + P], xrL[:, st, c0:c0 + P]),
                                    (cnH[:, st, r, :], cnL[:, st, r, :]), r == 0 and st == 0, False)
                        for kt in range(KT):
                            m = mm3(pe, dst, tuple(q[:, kt, o * P:(o + 1) * P] for q in wb),
                                    tuple(h[:, kt, :] for h in ht), False, kt == KT - 1)
                    m.then_inc(S("w_used"), 1)
                pe.wait_ge(S("h2_ready"), 3 * (g + 1))
                for j in range(3):
                    natural(HG[g] + j, j, (h2H, h2L))

                base = g * B * CPB
                pe.wait_ge(S("hg_lo"), 3 * (g + 1))
                pe.wait_ge(S("sel_ready"), 1)

                def args(c, k, ring):
                    if ring:
                        pe.wait_ge(S("mul_ready"), c - ZR + 1)
                    par, ft, half = k // CPB, (k % CPB) // 2, k % 2
                    for h in range(2):
                        m = pe.matmul(ps[:, 2 * (k % ZR) + h, :], lhs[:, par, half, ft * P:(ft + 1) * P],
                                      sel[:, h, :], start=True, stop=True)
                    m.then_inc(S("z_ready"), 1)

                def reduce(c, k):
                    ft, half = (k % CPB) // 2, k % 2
                    pe.wait_ge(S("fold_ready"), c + 1)
                    for s in range(2):
                        m = pe.matmul(ps[:, 6 + k // GC % 2, ft % 2 * 256:ft % 2 * 256 + 256], identity,
                                      fold[:, k % PR, s * 256:(s + 1) * 256],
                                      start=half == 0 and s == 0, stop=half == 1 and s == 1)
                    m.then_inc(S("red_done"), 1)

                def pair(c0, b0, first_pair, last_pair):
                    for k in range(2 * CPB):
                        n = k + ZR
                        if n == CPB:
                            pe.wait_ge(S("lhs_in1"), lhs_count(b0))
                        if n == 2 * CPB and not last_pair:
                            pe.wait_ge(S("lhs_in"), lhs_count(b0 + 2))
                        if n < 2 * CPB or not last_pair:
                            args(c0 + n, n % (2 * CPB), True)
                        r = k - LAGR
                        if r >= 0 or not first_pair:
                            if r % GC == 0 and (r >= 2 * GC or not (first_pair and g == 0)):
                                pe.wait_ge(S("qi_ready"), b0 * 3 + (r // GC - 1))
                            reduce(c0 + r, r % (2 * CPB))

                def lhs_count(b):
                    return (b * 64) + 128

                pe.wait_ge(S("lhs_in"), lhs_count(g * B))
                for c in range(ZR):
                    args(base + c, c, False)
                pair(base, g * B, True, False)
                with pe.Fori(1, B // 2 - 1) as bp:
                    pair(bp * (2 * CPB) + base, bp * 2 + g * B, False, False)
                pair(base + 6 * CPB, g * B + 6, False, True)
                for r in range(2 * CPB - LAGR, 2 * CPB):
                    reduce(base + 6 * CPB + r, r)

                pe.wait_ge(S("qi_ready"), 3 * B * (g + 1))
                for j in range(3):
                    for half, b_pair in enumerate(((h2H, h2L), (qiH, qiL))):
                        i = WQ[g] + 2 * j + half
                        w_wait(i)
                        wb = wblock(i, KT, 256)
                        for o in range(2):
                            for kt in range(KT):
                                m = mm3(pe, ps[:, 2 * j + o, 0:N], tuple(q[:, kt, o * P:(o + 1) * P] for q in wb),
                                        tuple(h[:, kt, :] for h in b_pair), half == 0 and kt == 0,
                                        half == 1 and kt == KT - 1)
                        m.then_inc(S("w_used"), 1)

            pe.wait_ge(S("hn_ready"), 6)
            for t in range(NT):
                for kt in range(KT):
                    m = pe.transpose(ps[:, 2 * t + kt // 3, (kt % 3) * P:(kt % 3 + 1) * P],
                                     th[:, kt, t * P:(t + 1) * P], identity)
            m.then_inc(S("hnT"), 1)

            def bcast_row(dst, col):
                return pe.matmul(dst, col.broadcast_to([P, P]), identity, start=True, stop=True)

            hb = [0]

            def attention(a, heads, outputs):
                pe.wait_ge(S("al_ready"), a + 1)
                for h in range(heads):
                    for t in range(NT):
                        m = bcast_row(ps[:, h // 2, (h % 2) * N + t * P:(h % 2) * N + (t + 1) * P], al[:, 0, t, h:h + 1])
                m.then_inc(S("als_rows"), 1)
                pe.wait_ge(S("brows_ready"), a + 1)

                def drows(h):
                    k = hb[0] + h
                    if h >= 2:
                        pe.wait_ge(S("exps_ready"), k - 1)
                    for v in range(2):
                        for t in range(NT):
                            m = bcast_row(ps[:, 4 + h % 2, v * N + t * P:v * N + (t + 1) * P], bb[:, v, t, h:h + 1])
                    m.then_inc(S("brow_mm"), 1)

                drows(0)
                if heads > 1:
                    drows(1)
                for h in range(heads):
                    pe.wait_ge(S("pt_lo"), hb[0] + h + 1)
                    outputs(h)
                    if h + 2 < heads:
                        drows(h + 2)
                hb[0] += heads

            def heads_T(done, cw, nct):
                def outputs(h):
                    s = h % 2
                    if h >= 2:
                        pe.wait_ge(S("u_ready"), done + h - 1)
                    for st in range(NT):
                        pe.matmul(ps[:, 6 + s, 0:N], ones[:], ptH[:, s, st, :], start=st == 0, stop=False)
                        pe.matmul(ps[:, 6 + s, 0:N], ones[:], ptL[:, s, st, :], start=False, stop=st == NT - 1)
                    for ct in range(nct):
                        c0 = (h * nct + ct) * cw
                        dst = ps[0:cw, 2 * s + ct // 2, (ct % 2) * N:(ct % 2 + 1) * N]
                        for st in range(NT):
                            m = mm3(pe, dst, (hH[:, st, c0:c0 + cw], hL[:, st, c0:c0 + cw]),
                                    (ptH[:, s, st, :], ptL[:, s, st, :]), st == 0, st == NT - 1)
                    m.then_inc(S("out_mm"), 1)
                return outputs

            def head_nat(h):
                for dt in range(NT):
                    for st in range(NT):
                        q = ptH[:, 0, st, dt * P:(dt + 1) * P], ptL[:, 0, st, dt * P:(dt + 1) * P]
                        pe.matmul(ps[:, 6, dt * 2:dt * 2 + 2], q[0], ones[:, 0:2], start=st == 0, stop=False)
                        pe.matmul(ps[:, 6, dt * 2:dt * 2 + 2], q[1], ones[:, 0:2], start=False, stop=st == NT - 1)
                for dt in range(NT):
                    for fc in range(2):
                        for st in range(NT):
                            q = ptH[:, 0, st, dt * P:(dt + 1) * P], ptL[:, 0, st, dt * P:(dt + 1) * P]
                            m = mm3(pe, ps[:, 2 * dt + fc, 0:384], q,
                                    (hH[:, st, fc * 384:fc * 384 + 384], hL[:, st, fc * 384:fc * 384 + 384]),
                                    st == 0, st == NT - 1)
                m.then_inc(S("fin_mm"), 1)

            transposes(1)
            pe.wait_ge(S("lnL"), 2)
            for j in range(4):
                natural(G1A + j, j, hT[1], w=192)
            attention(0, H1, heads_T(0, C1, 1))
            pe.wait_ge(S("gt_ready"), H1)
            for j in range(4):
                natural(G1B + j, j, (gTH, gTL), w=192, k=H1, kp=C1)
            attention(1, 1, head_nat)
            transposes(2)
            pe.wait_ge(S("lnL"), 3)
            for j in range(8):
                if j >= 4:
                    pe.wait_ge(S("gh_free"), 8 + j - 3)
                natural(G2A + j, j % 4, hT[1])
            attention(2, H2, heads_T(H1, P, 4))
            pe.wait_ge(S("gt_ready"), H1 + H2)
            for j in range(8):
                i = G2B + j
                w_wait(i)
                wb = wblock(i, 2, D)
                for kt in range(2):
                    for t in range(NT):
                        for fc in range(2):
                            m = mm3(pe, ps[:, 2 * t + fc, 0:384],
                                    tuple(h[:, 2 * j + kt, t * P:(t + 1) * P] for h in (gTH, gTL)),
                                    tuple(q[:, kt, fc * 384:fc * 384 + 384] for q in wb),
                                    j == 0 and kt == 0, j == 7 and kt == 1)
                m.then_inc(S("w_used"), 1)
            attention(3, 1, head_nat)
            transposes(3)
            pe.wait_ge(S("lnL"), 4)
            for j in range(3):
                natural(GCN + j, j, hT[1])
            pe.wait_ge(S("gh_lo"), 20)
            for dt in range(NT):
                for fc in range(2):
                    for st in range(NT):
                        c = cntS[:, st, dt * P:(dt + 1) * P]
                        for k, h in enumerate((hH, hL)):
                            m = pe.matmul(ps[:, 4 + 2 * dt + fc, 0:384], c, h[:, st, fc * 384:fc * 384 + 384],
                                          start=st == 0 and k == 0, stop=st == NT - 1 and k == 1)
            m.then_inc(S("fin_mm"), 1)

        @block.scalar
        def _(act):
            def split_hi(i):
                if i >= NBLK:
                    return
                act.wait_ge(w_in[i % RAW], 16 * (i // RAW + 1))
                if i >= SPL:
                    act.wait_ge(S("w_used"), i - SPL + 1)
                act.copy(wH[:, i % SPL, :], wraw[:, i % RAW, :]).then_inc(S("w_hi"), 1)

            def ln(k):
                act.wait_ge(S("ln_var"), k + 1)
                act.sqrt(std[:], var[:]).then_inc(S("ln_std"), 1)

            def ln_relu(k):
                act.wait_ge(S("lnT"), k + 1)
                act.activation(hT[min(k, 1)][0][:, :, :].rearrange("p k n -> p (k n)"), banks(0, 3),
                               ACT.Relu).then_inc(S("lnH"), 1)

            ln(0)
            split_hi(0)
            ln_relu(0)
            split_hi(1)
            split_hi(2)
            act.wait_ge(S("deg_ready"), 1)
            act.sqrt(dinv[:], var[:]).then_inc(S("sdeg"), 1)
            for j in range(3):
                act.wait_ge(S("w_used"), QG + j + 1)
                act.copy(qgH[:, :, j * 256:(j + 1) * 256],
                         banks(2 * (j % 2), 2).rearrange("p (a b) -> p a b", b=256)).then_inc(S("qg_hi"), 1)
                split_hi(QG + j + 3)
            for g in range(2):
                for j in range(9):
                    act.wait_ge(S("w_used"), REL[g] + j + 1)
                    act.copy(xrH[:, :, j * 256:(j + 1) * 256],
                             ps[:, j % 4, :].rearrange("p (t w) -> p t w", t=NT)).then_inc(S("rel_hi"), 1)
                    split_hi(REL[g] + j + 3)
                act.wait_ge(S("ld_bcol"), 16)
                for j in range(3):
                    act.wait_ge(S("w_used"), ROOT[g] + j + 1)
                    for o in range(2):
                        ot = 2 * j + o
                        act.activation(h32[:, ot, :], ps[:, j, o * N:(o + 1) * N], ACT.Relu,
                                       bias=bcol[:, KT * g + ot:KT * g + ot + 1]).then_inc(S("root_h"), 1)
                    split_hi(ROOT[g] + j + 3)
                for j in range(3):
                    act.wait_ge(S("w_used"), HG[g] + j + 1)
                    act.copy(hgH[:, :, j * 256:(j + 1) * 256],
                             ps[:, j, :].rearrange("p (t w) -> p t w", t=NT)).then_inc(S("hg_hi"), 1)
                    split_hi(HG[g] + j + 3)
                base = g * B * CPB

                with act.Fori(0, B) as b:
                    for k in range(CPB):
                        c = b * CPB + (base + k)
                        ft = k // 2
                        act.wait_ge(S("z_ready"), c + 1)
                        z = banks(2 * (k % ZR), 2)
                        act.activation(z, z, ACT.Sigmoid, bias=bcol[:, 12 + ft:13 + ft]).then_inc(S("sig_ready"), 1)
                act.wait_ge(S("qi_ready"), 3 * B * (g + 1))
                act.activation(th[:, :, :], th[:, :, :], ACT.Tanh).then_inc(S("th_ready"), 1)
                for j in range(3):
                    act.wait_ge(S("w_used"), WQ[g] + 2 * j + 1)
                    split_hi(WQ[g] + 2 * j + 3)
                    act.wait_ge(S("w_used"), WQ[g] + 2 * j + 2)
                    for o in range(2):
                        ot = 2 * j + o
                        act.activation(al32[:, j, o * N:(o + 1) * N], ps[:, 2 * j + o, 0:N], ACT.Sigmoid,
                                       bias=bcol[:, 18 + ot:19 + ot]).then_inc(S("alpha_ready"), 1)
                    split_hi(WQ[g] + 2 * j + 4)

            hb = [0, 0]

            def tile_hi(j_all, i, cols, w):
                act.wait_ge(S("w_used"), i + 1)
                act.copy(hH[:, :, cols:cols + w], ps[:, j_all, 0:2 * w].rearrange("p (t w) -> p t w", t=NT))\
                   .then_inc(S("gh_hi"), 1)
                split_hi(i + 3)

            def exps(h):
                k = hb[0] + h
                act.wait_ge(S("brow_mm"), k + 1)
                if h >= 2:
                    act.wait_ge(S("pt_ready"), k - 1)
                for st in range(NT):
                    act.activation(e1[:, h % 2, st, :], ps[:, 4 + h % 2, 0:N], ACT.Exp, bias=al[:, 0, st, h:h + 1])
                    m = act.activation(e2[:, h % 2, st, :], ps[:, 4 + h % 2, N:2 * N], ACT.Exp,
                                       bias=als2[:, st, h:h + 1])
                m.then_inc(S("exps_ready"), 1)

            def heads_T(heads, cw, nct, b0, done):
                exps(0)
                exps(1)
                for h in range(heads):
                    k = hb[0] + h
                    s = k % 2
                    act.wait_ge(S("u_ready"), done + h + 1)
                    for ct in range(nct):
                        bias = bcol[0:cw, b0 + h * nct + ct:b0 + h * nct + ct + 1]
                        act.activation(ru[0:cw, s, ct, :], u[0:cw, s, ct, :], ACT.Relu, bias=bias)
                        m = act.activation(u[0:cw, s, ct, :], u[0:cw, s, ct, :], ACT.Exp, bias=bias)
                    m.then_inc(S("act_u"), 1)
                    if h + 2 < heads:
                        exps(h + 2)
                hb[0] += heads

            def load_rows(att1, att2, bias):
                if att1 is not None:
                    n = att1.shape[1]
                    act.dma_start(arow1[:, :, 0:n], att1.partition_broadcast(P)).then_inc(S("arow1_in"), 16)
                if att2 is not None:
                    act.dma_start(arow2[:], att2.partition_broadcast(P)).then_inc(S("arow2_in"), 16)
                act.dma_start(brow[:], bias.partition_broadcast(P)).then_inc(S("brow_in"), 16)

            act.wait_ge(S("x_ready"), 1)
            load_rows(ins["att11"], ins["att12"], ins["brow1"])
            ln(1)
            ln_relu(1)
            for j in range(4):
                tile_hi(j, G1A + j, j * 192, 192)
            act.wait_ge(S("brows_ready"), 1)
            heads_T(H1, C1, 1, 24, 0)
            for j in range(4):
                tile_hi(j, G1B + j, j * 192, 192)
            act.wait_ge(S("brows_ready"), 2)
            exps(0)
            hb[0] += 1
            act.wait_ge(S("lay_done"), 1)
            load_rows(ins["att21"], ins["att22"], ins["brow2"])
            ln(2)
            ln_relu(2)
            for j in range(8):
                tile_hi(j % 4, G2A + j, j * 256, 256)
            act.wait_ge(S("brows_ready"), 3)
            heads_T(H2, P, 4, 32, H1)
            for j in range(8):
                act.wait_ge(S("w_used"), G2B + j + 1)
                if j < 7:
                    split_hi(G2B + j + 3)
            act.copy(hH[:, :, 0:D].rearrange("p t (f w) -> p t f w", f=2),
                     ps[:, 0:4, 0:384].rearrange("p (t f) w -> p t f w", f=2))\
               .then_inc(S("gh_hi"), 1)
            split_hi(G2B + 10)
            act.wait_ge(S("brows_ready"), 4)
            exps(0)
            hb[0] += 1
            act.wait_ge(S("lay_done"), 2)
            load_rows(None, None, ins["brow3"])
            ln(3)
            ln_relu(3)
            for j in range(3):
                i = GCN + j
                act.wait_ge(S("w_used"), i + 1)
                for t in range(NT):
                    m = act.activation(hH[:, t, j * 256:(j + 1) * 256], ps[:, j, t * 256:(t + 1) * 256], ACT.Copy,
                                       scale=dinv[:, t:t + 1])
                m.then_inc(S("gh_hi"), 1)

        @block.gpsimd
        def _(pool):
            def split_lo(i):
                if i >= NBLK:
                    return
                pool.wait_ge(S("w_hi"), i + 1)
                pool.tensor_tensor(wL[:, i % SPL, :], wraw[:, i % RAW, :], f(wH[:, i % SPL, :]), ALU.subtract)\
                    .then_inc(S("w_lo"), 1)

            for i in range(0, HG[0] + 6):
                split_lo(i)
            for g in range(2):
                base = g * B * CPB
                if g:
                    for i in range(HG[0] + 6, HG[1] + 6):
                        split_lo(i)

                def folds(c, k, wait):
                    pool.wait_ge(S("mul_ready"), c + 1)
                    if wait:
                        pool.wait_ge(S("red_done"), c - PR + 1)
                    s = k % PR
                    pool.tensor_tensor(fold[:, s, :], prod[:, s, 0:CH // 2], prod[:, s, CH // 2:CH], ALU.add)\
                        .then_inc(S("fold_ready"), 1)

                for k in range(CPB):
                    folds(base + k, k, k >= PR)
                with pool.Fori(1, B) as b:
                    for k in range(CPB):
                        folds(b * CPB + (base + k), k, True)
            for i in range(HG[1] + 6, G1A + 4 + 3):
                split_lo(i)

            def pt_split(k):
                s = slot_of[k]
                pool.wait_ge(S("pt_ready"), k + 1)
                if k in prev_use:
                    pool.wait_ge(S("out_mm"), prev_use[k])
                pool.tensor_copy(ptH[:, s, :, :], pt[:, s, :, :]).then_inc(S("pt_hi"), 1)
                pool.wait_ge(S("pt_hi"), k + 1)
                pool.tensor_tensor(ptL[:, s, :, :], pt[:, s, :, :], f(ptH[:, s, :, :]), ALU.subtract)\
                    .then_inc(S("pt_lo"), 1)

            slot_of, prev_use = {}, {}
            k = 0
            for heads, done in ((H1, 0), (1, H1), (H2, H1), (1, H1 + H2)):
                for h in range(heads):
                    slot_of[k] = h % 2
                    if h >= 2:
                        prev_use[k] = done + h - 1
                    k += 1
            for k in range(H1):
                pt_split(k)
            for i in range(G1A + 7, G1B + 7):
                split_lo(i)
            pt_split(H1)
            for i in range(G1B + 7, G2A + 11):
                split_lo(i)
            for k in range(H1 + 1, H1 + 1 + H2):
                pt_split(k)
            for i in range(G2A + 11, G2B + 11):
                split_lo(i)
            pt_split(H1 + 1 + H2)

        @block.vector
        def _(dve):
            steps = [0]

            def link(ins_):
                steps[0] += 1
                ins_.then_inc(S("chain"), 1)
                dve.wait_ge(S("chain"), steps[0])

            def ln(k, src, dst):
                for t in range(NT):
                    for j in range(2):
                        m = dve.bn_stats(stat[:, t, j, :], src[:, t, 384 * j:384 * j + 384])
                link(m)
                for t in range(NT):
                    m = dve.bn_aggr(mv[:, t, :], stat[:, t, :, :])
                link(m)
                dve.tensor_scalar(var[:], mv[:, :, 1], EPS_LN, None, ALU.add).then_inc(S("ln_var"), 1)
                dve.wait_ge(S("ln_std"), k + 1)
                link(dve.reciprocal(rstd[:], std[:]))
                for t in range(NT):
                    dve.tensor_scalar(dst[:, t, :], src[:, t, :], mv[:, t, 0:1], rstd[:, t:t + 1],
                                      ALU.subtract, ALU.mult).then_inc(S("ln_h"), 1)

            def ln_lo(k):
                dve.wait_ge(S("lnH"), k + 1)
                hh, hl = (t[:, :, :].rearrange("p k n -> p (k n)") for t in hT[min(k, 1)])
                dve.scalar_tensor_tensor(hl, banks(0, 3), 0.0, f(hh), ALU.max, ALU.subtract).then_inc(S("lnL"), 1)

            def split(dst, src, hi_sem=None, lo_sem=None):
                link(dve.tensor_copy(dst[0], src))
                return dve.tensor_tensor(dst[1], src, f(dst[0]), ALU.subtract)

            dve.wait_ge(S("ld_edge"), 16)
            dve.wait_ge(S("ld_const"), 32)
            dve.tensor_copy(iota[:], iota32[:])
            link(dve.tensor_copy(edge_f[:], edge_i[:]))
            dve.scalar_tensor_tensor(key[:], edge_f[:, 2, :], float(N), edge_f[:, 1, :], ALU.mult, ALU.add)\
               .then_inc(S("edges_ready"), 1)
            dve.wait_ge(S("edges_ready"), 1)
            dve.wait_ge(S("ld_x"), 16)
            ln(0, x_in, hnat0)

            def onehot(t, k):
                dve.tensor_scalar(ohS[:, k, :], iota[:, 0:N], edge_f[:, 0, bass.ds(t, 1)], None, ALU.is_equal)
                dve.tensor_scalar(ohD[:, k, :, :].rearrange("p r n -> p (r n)"), iota[:], key[:, bass.ds(t, 1)],
                                  None, ALU.is_equal).then_inc(S("oh_ready"), 1)

            for k in range(4):
                onehot(k, k)
            ln_lo(0)
            with dve.Fori(1, ET // 4) as g:
                for k in range(4):
                    dve.wait_ge(S("oh_used"), g * 4 + (k - 3))
                    onehot(g * 4 + k, k)
            dve.wait_ge(S("ld_sel"), 16)
            dve.tensor_copy(sel[:, :, :].rearrange("p a b -> p (a b)"), sel32).then_inc(S("sel_ready"), 1)
            link(dve.memset(iota32[:], 1.0))
            dve.tensor_copy(ones[:], iota32[:, 0:P]).then_inc(S("ones_ready"), 1)
            dve.wait_ge(S("ld_q"), 16)
            dve.tensor_copy(qTH[:], qT[:]).then_inc(S("qT_ready"), 1)
            dve.wait_ge(S("qT_ready"), 1)
            dve.tensor_tensor(qTL[:], qT[:], f(qTH[:]), ALU.subtract).then_inc(S("qT_ready"), 1)
            dve.wait_ge(S("oh_used"), ET)
            for st in range(NT):
                c = cr[:, st, :, :].rearrange("p r n -> p (r n)")
                dve.tensor_copy(c[:, 0:512], ps[:, 4 + 2 * st, :]).then_inc(S("cnt_ready"), 1)
                dve.tensor_copy(c[:, 512:768], ps[:, 5 + 2 * st, 0:256]).then_inc(S("cnt_ready"), 1)
            dve.wait_ge(S("cnt_ready"), 4)
            link(dve.tensor_tensor(cnt[:], f(cr[:, :, 0, :]), f(cr[:, :, 1, :]), ALU.add))
            dve.tensor_tensor(cnt[:], cnt[:], f(cr[:, :, 2, :]), ALU.add).then_inc(S("cr_ready"), 1)
            dve.wait_ge(S("cr_ready"), 1)
            dve.tensor_tensor(cntS[:], cnt[:], eye[:], ALU.add).then_inc(S("cr_ready"), 1)
            dve.wait_ge(S("colsum_mm"), 1)
            dve.wait_ge(S("sel_ready"), 1)
            inv = cn32[:, 0, :, :].rearrange("p r n -> p (r n)")
            link(dve.tensor_scalar(inv, banks(4, 2)[:, 0:768], 1.0, None, ALU.max))
            inv2 = x_in[:, 0, :]
            link(dve.reciprocal(inv2, inv))
            link(dve.tensor_tensor(cn32[:, :, :, :].rearrange("p t r n -> p t (r n)"),
                                   f(cr[:, :, :, :].rearrange("p t r n -> p t (r n)")),
                                   inv2.unsqueeze(1).broadcast_to([P, NT, R * N]), ALU.mult))
            link(dve.tensor_copy(cnH[:], cn32[:]))
            dve.tensor_tensor(cnL[:], cn32[:], f(cnH[:]), ALU.subtract).then_inc(S("cn_ready"), 1)
            dve.wait_ge(S("cntT_mm"), 1)
            cT = ps[:, 6, :].rearrange("p (t n) -> p t n", t=NT)
            link(dve.tensor_tensor(mask[:, 1, :, :], cT, eye[:], ALU.add))
            dve.tensor_reduce(var[:], mask[:, 1, :, :], AX.X, ALU.add).then_inc(S("deg_ready"), 1)
            dve.wait_ge(S("deg_ready"), 1)
            dve.tensor_scalar(mask[:, 0, :, :], cT, 0.0, NO_EDGE, ALU.is_equal, ALU.mult).then_inc(S("mask_ready"), 1)
            dve.tensor_scalar(mask[:, 1, :, :], mask[:, 1, :, :], 0.0, NO_EDGE, ALU.is_equal, ALU.mult)\
               .then_inc(S("mask_ready"), 1)
            dve.wait_ge(S("sdeg"), 1)
            link(dve.reciprocal(dinv[:], dinv[:]))
            for j in range(3):
                dve.wait_ge(S("qg_hi"), j + 1)
                q = banks(2 * (j % 2), 2).rearrange("p (a b) -> p a b", b=256)
                cs = slice(j * 256, (j + 1) * 256)
                dve.tensor_tensor(qgL[:, :, cs], q, f(qgH[:, :, cs]), ALU.subtract).then_inc(S("qg_lo"), 1)

            for g in range(2):
                for j in range(9):
                    dve.wait_ge(S("rel_hi"), 9 * g + j + 1)
                    cs = slice(j * 256, (j + 1) * 256)
                    dve.tensor_tensor(xrL[:, :, cs], ps[:, j % 4, :].rearrange("p (t w) -> p t w", t=NT),
                                      f(xrH[:, :, cs]), ALU.subtract).then_inc(S("rel_lo"), 1)
                for j in range(3):
                    dve.wait_ge(S("root_h"), 6 * g + 2 * j + 2)
                    o = slice(2 * j, 2 * j + 2)
                    split((h2H[:, o, :], h2L[:, o, :]), h32[:, o, :]).then_inc(S("h2_ready"), 1)
                for j in range(3):
                    dve.wait_ge(S("hg_hi"), 3 * g + j + 1)
                    cs = slice(j * 256, (j + 1) * 256)
                    dve.tensor_tensor(hgL[:, :, cs], ps[:, j, :].rearrange("p (t w) -> p t w", t=NT),
                                      f(hgH[:, :, cs]), ALU.subtract).then_inc(S("hg_lo"), 1)
                base = g * B * CPB

                def mul(c, k, b, wait):
                    ft, half = (k % CPB) // 2, k % 2
                    dve.wait_ge(S("sig_ready"), c + 1)
                    if wait:
                        dve.wait_ge(S("fold_ready"), c - PR + 1)
                    q = qT[:, ft, bass.ds(b * LQ + half * 32, 32)]
                    dve.tensor_tensor(prod[:, k % PR, :].rearrange("p (l n) -> p l n", n=NB),
                                      banks(2 * (k % ZR), 2).rearrange("p (l n) -> p l n", n=NB),
                                      q.unsqueeze(2).broadcast_to([P, 32, NB]), ALU.mult).then_inc(S("mul_ready"), 1)

                def sums(b, q, red, n, par):
                    o = slice(2 * q, 2 * q + 2)
                    dst, hi, lo = (t[:, o, bass.ds(b * NB, NB)] for t in (th, qiH, qiL))
                    dve.wait_ge(S("red_done"), red)
                    dve.tensor_reduce(dst, ps[:, 6 + par, :]
                                      .rearrange("p (f l n) -> p f n l", l=8, n=NB), AX.X, ALU.add)\
                       .then_inc(S("sum_step"), 1)
                    dve.wait_ge(S("sum_step"), n)
                    dve.tensor_copy(hi, dst).then_inc(S("sum_hi"), 1)
                    dve.wait_ge(S("sum_hi"), n)
                    dve.tensor_tensor(lo, dst, f(hi), ALU.subtract).then_inc(S("qi_ready"), 1)

                def graph_pair(c0, b0, first_pair):
                    for k in range(2 * CPB):
                        mul(c0 + k, k, b0 + k // CPB, not (first_pair and k < PR))
                        grp = (k - 7) // GC
                        if k % GC == GC - 1 and (grp >= 0 or not first_pair):
                            sums(b0 + grp // 3, grp % 3, c0 + GC * (grp + 1), b0 * 3 + (grp + 1 + 3 * g * B), grp % 2)

                graph_pair(base, 0, True)
                with dve.Fori(1, B // 2) as bp:
                    graph_pair(bp * (2 * CPB) + base, bp * 2, False)
                sums(B - 1, 2, base + B * CPB, 3 * B * (g + 1), 1)
                dve.wait_ge(S("th_ready"), g + 1)
                for j in range(3):
                    o = slice(2 * j, 2 * j + 2)
                    dve.wait_ge(S("alpha_ready"), 6 * g + 2 * j + 2)
                    t2 = th[:, o, :]
                    link(dve.tensor_tensor(t2, t2, h32[:, o, :], ALU.subtract))
                    link(dve.tensor_tensor(t2, t2, al32[:, j, :].rearrange("p (o n) -> p o n", o=2), ALU.mult))
                    dve.tensor_tensor(t2, t2, h32[:, o, :], ALU.add).then_inc(S("hn_ready"), 1)
                    if g == 0:
                        dve.wait_ge(S("hn_ready"), j + 1)
                        split((hT[0][0][:, o, :], hT[0][1][:, o, :]), t2).then_inc(S("hn_lo"), 1)

            dve.wait_ge(S("hnT"), 1)
            dve.wait_ge(S("x_res"), 16)
            x4 = x[:, :, :].rearrange("p t (f w) -> p (t f) w", f=2)
            dve.tensor_tensor(x4, x4, ps[:, 0:4, 0:384], ALU.add).then_inc(S("x_ready"), 1)
            dve.wait_ge(S("x_ready"), 1)

            nt_ = [0, 0]

            def tile_lo(bank, cols, w, arow, a0, per, slot):
                dve.wait_ge(S("gh_hi"), nt_[0] + 1)
                nt_[0] += 1
                q = ps[:, bank, 0:2 * w].rearrange("p (t w) -> p t w", t=NT)
                dve.tensor_tensor(hL[:, :, cols:cols + w], q, f(hH[:, :, cols:cols + w]), ALU.subtract)\
                   .then_inc(S("gh_lo"), 1)
                for v in range(2):
                    t3 = tmp[:, 2 * v:2 * v + 2, 0:w]
                    m = dve.tensor_tensor(t3, q, arow[:, v, a0:a0 + w].unsqueeze(1).broadcast_to([P, NT, w]), ALU.mult)
                    if v == 1:
                        m.then_inc(S("gh_free"), 1)
                dve.wait_ge(S("gh_free"), nt_[0])
                for v in range(2):
                    t3 = tmp[:, 2 * v:2 * v + 2, 0:w].rearrange("p t (a c) -> p t a c", a=per)
                    m = dve.tensor_reduce(alp[:, v, :, slot:slot + per], t3, AX.X, ALU.add)
                link(m)

            def coefficients(a, heads, nparts, msk):
                src = alp[:, :, :, 0:heads * nparts].rearrange("p v t (h k) -> p (v t) h k", k=nparts)
                dst = al[:, :, :, 0:heads].rearrange("p v t h -> p (v t) h")
                if nparts == 1:
                    dve.tensor_copy(dst, alp[:, :, :, 0:heads].rearrange("p v t h -> p (v t) h"))\
                       .then_inc(S("al_ready"), 1)
                else:
                    dve.tensor_reduce(dst, src, AX.X, ALU.add).then_inc(S("al_ready"), 1)
                dve.wait_ge(S("als_rows"), a + 1)
                dve.wait_ge(S("al_ready"), a + 1)
                for h in range(heads):
                    for dt in range(NT):
                        link(dve.tensor_tensor_reduce(gmax[:, dt, :], ps[:, h // 2, (h % 2) * N:(h % 2 + 1) * N],
                                                      mask[:, msk, dt, :], 1.0, -3.0e38, ALU.add, ALU.max,
                                                      mx[:, dt, h:h + 1]))
                hs_ = slice(0, heads)
                link(dve.tensor_tensor(xs[:, :, hs_], mx[:, :, hs_], al[:, 1, :, hs_], ALU.add))
                link(dve.scalar_tensor_tensor(ms[:, :, hs_], xs[:, :, hs_], SLOPE, xs[:, :, hs_], ALU.mult, ALU.max))
                dve.tensor_scalar(als2[:, :, hs_], al[:, 0, :, hs_], SLOPE, None, ALU.mult)
                dve.tensor_tensor(bb[:, 0, :, hs_], al[:, 1, :, hs_], ms[:, :, hs_], ALU.subtract)
                dve.scalar_tensor_tensor(bb[:, 1, :, hs_], al[:, 1, :, hs_], SLOPE, ms[:, :, hs_],
                                         ALU.mult, ALU.subtract).then_inc(S("brows_ready"), 1)

            def weights_of(h, c):
                k = nt_[1] + h
                s = h % 2
                dve.wait_ge(S("exps_ready"), k + 1)
                link(dve.tensor_tensor(e1[:, s, :, :], e1[:, s, :, :], e2[:, s, :, :], ALU.max))
                if h >= 2:
                    dve.wait_ge(S("pt_lo"), k - 1)
                dve.scalar_tensor_tensor(pt[:, s, :, :], e1[:, s, :, :], 1.0, c, ALU.min, ALU.mult)\
                   .then_inc(S("pt_ready"), 1)

            def heads_T(heads, cw, nct, c, done):
                def outputs(h):
                    s = h % 2
                    dve.wait_ge(S("out_mm"), done + h + 1)
                    link(dve.tensor_scalar(rz[:, 0, :], ps[:, 6 + s, 0:N], EPS_SM, None, ALU.add))
                    link(dve.reciprocal(rz[:, 1, :], rz[:, 0, :]))
                    src = banks(2 * s, 2)[0:cw, 0:nct * N].rearrange("p (c n) -> p c n", n=N)
                    dve.tensor_tensor(u[0:cw, (nt_[1] + h) % 2, 0:nct, :], src,
                                      rz[0:cw, 1, :].unsqueeze(1).broadcast_to([cw, nct, N]), ALU.mult)\
                       .then_inc(S("u_ready"), 1)

                def elu(h):
                    k = nt_[1] + h
                    s = k % 2
                    dve.wait_ge(S("act_u"), k + 1 - (nt_[1] - done))
                    uu, rr = u[0:cw, s, 0:nct, :], ru[0:cw, s, 0:nct, :]
                    link(dve.tensor_scalar(uu, uu, 1.0, -1.0, ALU.min, ALU.add))
                    link(dve.tensor_tensor(rr, rr, uu, ALU.add))
                    o = slice(h * nct, (h + 1) * nct)
                    split((gTH[0:cw, o, :], gTL[0:cw, o, :]), rr).then_inc(S("gt_ready"), 1)

                weights_of(0, c)
                for h in range(heads):
                    if h + 1 < heads:
                        weights_of(h + 1, c)
                    outputs(h)
                    if h:
                        elu(h - 1)
                elu(heads - 1)
                nt_[1] += heads

            def finish(k, scale_z):
                dve.wait_ge(S("brow_in"), 16 * (k + 1))
                link(dve.tensor_tensor(x[:], x[:], brow[:].unsqueeze(1).broadcast_to([P, NT, D]), ALU.add))
                dve.wait_ge(S("fin_mm"), k + 1)
                if scale_z:
                    z = ps[:, 6, 0:4].rearrange("p (t k) -> p t k", k=2)[:, :, 0]
                    link(dve.tensor_scalar(zr[:], z, EPS_SM, None, ALU.add))
                    link(dve.reciprocal(zr[:], zr[:]))
                scale, b0 = (zr, 0) if scale_z else (dinv, 4)
                for dt in range(NT):
                    for fc in range(2):
                        cs = slice(fc * 384, fc * 384 + 384)
                        m = dve.scalar_tensor_tensor(x[:, dt, cs], ps[:, b0 + 2 * dt + fc, 0:384], scale[:, dt:dt + 1],
                                                     x[:, dt, cs], ALU.mult, ALU.add)
                m.then_inc(S("lay_done"), 1)
                dve.wait_ge(S("lay_done"), k + 1)

            ln(1, x, hnat1)
            ln_lo(1)
            dve.wait_ge(S("arow1_in"), 16)
            dve.wait_ge(S("arow2_in"), 16)
            dve.wait_ge(S("mask_ready"), 2)
            for j in range(4):
                tile_lo(j, j * 192, 192, arow1, j * 192, 2, 2 * j)
            coefficients(0, H1, 1, 0)
            heads_T(H1, C1, 1, cnt[:], 0)
            for j in range(4):
                tile_lo(j, j * 192, 192, arow2, j * 192, 1, j)
            coefficients(1, 1, 4, 0)
            weights_of(0, cnt[:])
            nt_[1] += 1
            finish(0, True)
            ln(2, x, hnat1)
            ln_lo(2)
            dve.wait_ge(S("arow1_in"), 32)
            dve.wait_ge(S("arow2_in"), 32)
            for j in range(8):
                tile_lo(j % 4, j * 256, 256, arow1, j * 256, 1, j)
            coefficients(2, H2, 2, 1)
            heads_T(H2, P, 4, f(cntS[:]), H1)
            dve.wait_ge(S("gh_hi"), nt_[0] + 1)
            nt_[0] += 1
            h4H, h4L = (t[:, :, 0:D].rearrange("p t (f w) -> p t f w", f=2) for t in (hH, hL))
            dve.tensor_tensor(h4L, ps[:, 0:4, 0:384].rearrange("p (t f) w -> p t f w", f=2), f(h4H), ALU.subtract).then_inc(S("gh_lo"), 1)
            for v in range(2):
                t3 = tmp[:, :, :]
                a3 = arow2[:, v, :].rearrange("p (f w) -> p f w", f=2)
                for t in range(NT):
                    m = dve.tensor_tensor(t3[:, 2 * t:2 * t + 2, :], ps[:, 2 * t:2 * t + 2, 0:384], a3, ALU.mult)
                link(m)
                link(dve.tensor_reduce(alp[:, v, :, 0:2], t3.rearrange("p (t f) w -> p t f w", t=NT), AX.X, ALU.add))
            coefficients(3, 1, 2, 1)
            weights_of(0, f(cntS[:]))
            nt_[1] += 1
            finish(1, True)
            ln(3, x, hnat1)
            ln_lo(3)
            for j in range(3):
                dve.wait_ge(S("gh_hi"), nt_[0] + 1)
                nt_[0] += 1
                for t in range(NT):
                    cs = slice(j * 256, (j + 1) * 256)
                    m = dve.scalar_tensor_tensor(hL[:, t, cs], ps[:, j, t * 256:(t + 1) * 256], dinv[:, t:t + 1],
                                                 f(hH[:, t, cs]), ALU.mult, ALU.subtract)
                m.then_inc(S("gh_lo"), 1)
            finish(2, False)


def kernel(x, src, dst, edge_type_3, L0_gnn_query_embs, L0_gnn_W_rel1, L0_gnn_W_root1, L0_gnn_b1, L0_gnn_W_rel2,
           L0_gnn_W_root2, L0_gnn_b2, L0_gnn_Wg, L0_gnn_bg, L0_gnn_Wq, L0_gnn_bq, L1_gnn_W1, L1_gnn_a_src1,
           L1_gnn_a_dst1, L1_gnn_b1, L1_gnn_W2, L1_gnn_a_src2, L1_gnn_a_dst2, L1_gnn_b2, L2_gnn_W1, L2_gnn_att_src1,
           L2_gnn_att_dst1, L2_gnn_b1, L2_gnn_W2, L2_gnn_att_src2, L2_gnn_att_dst2, L2_gnn_b2, L3_gnn_W, L3_gnn_b):
    import numpy as np
    import concourse.bacc as bacc
    from concourse.bass_utils import run_bass_kernel_spmd

    a = np.asarray

    def blocks(w, rows=P, width=256, kt=KT):
        w = a(w)
        k, m = w.shape[0] // rows, w.shape[1] // width
        v = w.reshape(k // kt, kt, rows, m, width).transpose(0, 3, 2, 1, 4).reshape(k // kt * m, rows, kt * width)
        full = np.zeros((v.shape[0], P, BLK), v.dtype)
        full[:, :rows, :kt * width] = v
        return full

    def interleave(p, q):
        return np.stack([p, q], 1).reshape(-1, P, BLK)

    wg, wq = a(L0_gnn_Wg).T, a(L0_gnn_Wq).T
    stream = [blocks(wg[D:])]
    for w_rel, w_root in ((L0_gnn_W_rel1, L0_gnn_W_root1), (L0_gnn_W_rel2, L0_gnn_W_root2)):
        stream += [blocks(w) for w in a(w_rel)] + [blocks(w_root), blocks(wg[:D]),
                                                   interleave(blocks(wq[:D]), blocks(wq[D:]))]
    stream += [blocks(L1_gnn_W1, width=192), blocks(L1_gnn_W2, rows=C1, width=192, kt=H1),
               blocks(L2_gnn_W1), blocks(L2_gnn_W2, width=D, kt=2), blocks(L3_gnn_W)]

    bcol = np.zeros((P, 48), np.float32)
    for c0, b in ((0, L0_gnn_b1), (6, L0_gnn_b2), (12, L0_gnn_bg), (18, L0_gnn_bq)):
        bcol[:, c0:c0 + KT] = a(b).reshape(KT, P).T
    bcol[:C1, 24:32] = a(L1_gnn_b1).reshape(H1, C1).T
    bcol[:, 32:48] = a(L2_gnn_b1).reshape(CT2, P).T

    eye32 = np.eye(32, dtype=np.float32)
    node = np.tile(eye32, (1, 32))
    token = np.repeat(eye32, NB, axis=1)
    arrays = {
        "x": a(x),
        "edges": np.stack([a(src), a(dst), a(edge_type_3)]).reshape(3, P, ET),
        "iota": np.tile(np.arange(R * N, dtype=np.float32), (P, 1)),
        "eye": np.eye(N, dtype=np.float32).reshape(NT, P, N).transpose(1, 0, 2),
        "sel": np.concatenate([node, node, token, token]),
        "qT": a(L0_gnn_query_embs).reshape(B * LQ, KT, P).transpose(2, 1, 0),
        "bcol": bcol,
        "weights": np.concatenate(stream),
        "att11": np.stack([a(L1_gnn_a_src1).reshape(-1), a(L1_gnn_a_dst1).reshape(-1)]),
        "att12": np.stack([a(L1_gnn_a_src2).reshape(-1), a(L1_gnn_a_dst2).reshape(-1)]),
        "att21": np.stack([a(L2_gnn_att_src1).reshape(-1), a(L2_gnn_att_dst1).reshape(-1)]),
        "att22": np.stack([a(L2_gnn_att_src2).reshape(-1), a(L2_gnn_att_dst2).reshape(-1)]),
        "brow1": a(L1_gnn_b2), "brow2": a(L2_gnn_b2), "brow3": a(L3_gnn_b),
    }
    arrays = {k: np.ascontiguousarray(v) for k, v in arrays.items()}
    nc = bacc.Bacc("TRN2", target_bir_lowering=False, num_devices=1)
    ins = {k: nc.dram_tensor(f"in_{k}", v.shape, mybir.dt.from_np(v.dtype), kind="ExternalInput").ap()
           for k, v in arrays.items()}
    out = nc.dram_tensor("out", (N, D), F32, kind="ExternalOutput").ap()
    build(nc, ins, out)
    res = run_bass_kernel_spmd(nc, [{f"in_{k}": v for k, v in arrays.items()}], core_ids=[0])
    return res.results[0]["out"]
```

```python
from contextlib import ExitStack

import concourse.bass as bass
from concourse import mybir

F32 = mybir.dt.float32
F32R = mybir.dt.float32r
BF16 = mybir.dt.bfloat16
FP16 = mybir.dt.float16
I32 = mybir.dt.int32
ALU = mybir.AluOpType
ACT = mybir.ActivationFunctionType
AX = mybir.AxisListType

P = 128
N = 256
NT = N // P
D = 768
KT = D // P
R = 3
E = 8192
ET = E // P
B = 8
NB = N // B
LQ = 64
QT = B * LQ // P
EPS_LN = 1e-5
EPS_SM = 1e-16
NO_EDGE = -1e30
SLOPE = 0.2
BLK = 6 * 256

H1, C1 = 8, 96
H2, C2W = 4, 512
CT2 = H2 * C2W // P

RAW, SPL = 4, 3

QG = 0
REL = (3, 24)
ROOT = (12, 33)
HG = (15, 36)
WQ = (18, 39)
G1A, G1B = 45, 48
G2A, G2B = 52, 60
GCN = 68
NBLK = 71
UPB = 6

LAGR = 2
ZR = 3
PR = 3
ngroups = (0, 2, 3, 5)
CH = NB * 32
CPB = 2 * KT
GC = 4


def build(nc, ins, out):
    ctx = ExitStack()
    with ctx:
        def alloc(stack, name, shape, dt=F32):
            return stack.enter_context(nc.sbuf_tensor(name, shape, dt))

        wraw = alloc(ctx, "wraw", [P, RAW, BLK])
        wH = alloc(ctx, "wH", [P, SPL, BLK], F32R)
        wL = alloc(ctx, "wL", [P, SPL, BLK], F32R)
        eye = alloc(ctx, "eye", [P, NT, N])
        ones = alloc(ctx, "ones", [P, P], F32R)
        cnt = alloc(ctx, "cnt", [P, NT, N])
        cntS = alloc(ctx, "cntS", [P, NT, N], F32R)
        mask = alloc(ctx, "mask", [P, 2, NT, N])
        bcol = alloc(ctx, "bcol", [P, 48])
        dinv = alloc(ctx, "dinv", [P, NT])
        stat = alloc(ctx, "stat", [P, NT, 2, 6])
        mv = alloc(ctx, "mv", [P, NT, 2])
        var = alloc(ctx, "var", [P, NT])
        std = alloc(ctx, "std", [P, NT])
        rstd = alloc(ctx, "rstd", [P, NT])
        identity = eye[:, 0, 0:P]
        eyeR = alloc(ctx, "eyeR", [P, P], F32R)
        warm = alloc(ctx, "warm", [P, 2])

        l0 = ctx.enter_context(ExitStack())
        qgH = alloc(l0, "qgH", [P, QT, D], F32R)
        qgL = alloc(l0, "qgL", [P, QT, D], F32R)
        cnH = alloc(l0, "cnH", [P, NT, R, N], F32R)
        cnL = alloc(l0, "cnL", [P, NT, R, N], F32R)
        sel = alloc(l0, "sel", [P, 2, 512], F32R)
        qT = alloc(l0, "qT", [P, KT, B * LQ])
        hnat0 = alloc(l0, "hnat0", [P, NT, D])
        hs = l0.enter_context(ExitStack())
        hT = [(alloc(hs, "hTH0", [P, KT, N], F32R), alloc(hs, "hTL0", [P, KT, N], F32R))]
        hs.close()
        hgH = alloc(l0, "hgH", [P, NT, D], F32R)
        hgL = alloc(l0, "hgL", [P, NT, D], F32R)
        h32 = hnat0[:, :, :].rearrange("p t (a b) -> p (t a) b", b=N)
        first = l0.enter_context(ExitStack())
        x_in = alloc(first, "x_in", [P, NT, D])
        qTH = alloc(first, "qTH", [P, KT, B * LQ], F32R)
        qTL = alloc(first, "qTL", [P, KT, B * LQ], F32R)
        cr = alloc(first, "cr", [P, NT, R, N], F32R)
        cn32 = alloc(first, "cn32", [P, NT, R, N])
        sel32 = cn32[:, :, :, :].rearrange("p t r n -> p (t r n)")[:, 0:1024]
        iota = alloc(first, "iota", [P, R * N], FP16)
        edge_i = alloc(first, "edge_i", [P, 3, ET], I32)
        edge_f = alloc(first, "edge_f", [P, 3, ET])
        key = alloc(first, "key", [P, ET])
        ohS = alloc(first, "ohS", [P, 4, N], BF16)
        ohD = alloc(first, "ohD", [P, 4, R, N], BF16)
        first.close()
        h2H = alloc(l0, "h2H", [P, KT, N], F32R)
        h2L = alloc(l0, "h2L", [P, KT, N], F32R)
        qiH = alloc(l0, "qiH", [P, KT, N], F32R)
        qiL = alloc(l0, "qiL", [P, KT, N], F32R)
        rel = l0.enter_context(ExitStack())
        xrH = alloc(rel, "xrH", [P, NT, R * D], F32R)
        xrL = alloc(rel, "xrL", [P, NT, R * D], F32R)
        rel.close()
        gate = l0.enter_context(ExitStack())
        lhs = alloc(gate, "lhs", [P, 2, 2, D], F32R)
        prod = alloc(gate, "prod", [P, PR, CH])
        fold = alloc(gate, "fold", [P, PR, CH // 2])
        th = alloc(gate, "th", [P, KT, N])
        gate.close()
        al32 = prod[:, :, :].rearrange("p a b -> p (a b)")[:, 0:3 * 512].rearrange("p (j n) -> p j n", j=3)
        l0.close()

        gl = ctx.enter_context(ExitStack())
        x = alloc(gl, "x", [P, NT, D])
        brow = alloc(gl, "brow", [P, D])
        arow2 = alloc(gl, "arow2", [P, 2, D])
        gTH = alloc(gl, "gTH", [P, CT2, N], F32R)
        gTL = alloc(gl, "gTL", [P, CT2, N], F32R)
        hH = alloc(gl, "hH", [P, NT, H2 * C2W], F32R)
        hL = alloc(gl, "hL", [P, NT, H2 * C2W], F32R)
        hT.append((alloc(gl, "hTH1", [P, KT, N], F32R), alloc(gl, "hTL1", [P, KT, N], F32R)))
        alp = alloc(gl, "alp", [P, 2, NT, 24])
        al = alloc(gl, "al", [P, 2, NT, 8])
        mx = alloc(gl, "mx", [P, NT, 8])
        xs = alloc(gl, "xs", [P, NT, 8])
        ms = alloc(gl, "ms", [P, NT, 8])
        bb = alloc(gl, "bb", [P, NT, 16])
        zsel = alloc(gl, "zsel", [P, N], F32R)
        aT = tuple(alloc(gl, f"aT{q}", [8, N], F32R) for q in "HL")
        bT = tuple(alloc(gl, f"bT{q}", [8, 2, N], F32R) for q in "HL")
        rzT = tuple(alloc(gl, f"rzT{q}", [8, N], F32R) for q in "HL")
        als2 = alloc(gl, "als2", [P, NT, 8])
        rz = alloc(gl, "rz", [P, 2, N])
        z32 = alloc(gl, "z32", [8, N])
        zr = alloc(gl, "zr", [P, NT])
        ys = gl.enter_context(ExitStack())
        arow1 = alloc(ys, "arow1", [P, 2, H2 * C2W])
        ys.close()
        ys = gl.enter_context(ExitStack())
        e1 = alloc(ys, "e1", [P, 2, NT, N])
        e2 = alloc(ys, "e2", [P, 2, NT, N])
        ptH = alloc(ys, "ptH", [P, 2, NT, N], F32R)
        ptL = alloc(ys, "ptL", [P, 2, NT, N], F32R)
        zs = gl.enter_context(ExitStack())
        hnat1 = alloc(zs, "hnat1", [P, NT, D])
        tmp = alloc(zs, "tmp", [P, 4, 256])
        zs.close()
        u = alloc(gl, "u", [P, 2, 4, N])
        ru = alloc(gl, "ru", [P, 2, 4, N])
        junk = [t[:, a, b, :] for t in (u, ru) for a in range(2) for b in range(4)]

        ps = ctx.enter_context(nc.psum_tensor("ps", [P, 8, 512], F32))

        def banks(a, n):
            return ps[:, a:a + n, :].rearrange("p a b -> p (a b)")

        def f(ap):
            return ap.bitcast(F32)

        sems = {}
        for name in """warm_ready ld_x ld_eye ld_const ld_sel ld_edge ld_q ld_bcol w_hi w_lo w_used chain achain pchain
                ln_var ln_std ln_h lnT lnH lnL edges_ready oh_ready oh_used counts_mm cr_ready cnt_ready
                eyeR_ready zsel_step zsel_ready ones_ready colsum_mm cntT_mm mask_ready deg_ready sdeg cn_ready qT_ready qg_hi qg_lo
                rel_hi rel_lo root_h h2_ready hg_hi hg_lo sel_ready lhs_q lhs_c0 lhs_c1 lhs_c2 lhs_in lhs_in1 z_ready sig_ready mul_ready fold_ready red_done
                qi_ready sum_step sum_hi th_ready alpha_ready hn_ready hn_lo hnT x_res x_ready arow1_in arow2_in brow_in xb_ready
                col_done gh_hi gh_free gh_lo al_ready alT_mm alT_ready als_rows b_ready bT_mm bT_ready brow_mm exps_ready
                pt_ready pt_hi pt_lo out_mm zT_mm rzT_ready rz_mm rz_ready u_ready act_u elu_ready gt_ready fin_mm lay_half lay_done
                stored""".split():
            sems[name] = ctx.enter_context(nc.semaphore(name))
        w_in = [ctx.enter_context(nc.semaphore(f"w_in{s}")) for s in range(RAW)]

        def S(name):
            return sems[name]

        def ubank(cb):
            return (4, 0, 2)[cb]

        def mm3(pe, dst, a, b, start, stop, **kw):
            pe.matmul(dst, a[0], b[0], start=start, stop=False, **kw)
            pe.matmul(dst, a[0], b[1], start=False, stop=False, **kw)
            return pe.matmul(dst, a[1], b[0], start=False, stop=stop, **kw)

        def wblock(i, k, w, p=P):
            s = i % SPL
            return tuple(t[0:p, s, 0:k * w].rearrange("p (k w) -> p k w", k=k) for t in (wH, wL))

        block = ctx.enter_context(nc.Block())

        @block.sync
        def _(sp):
            sp.dma_start(edge_i[:], ins["edges"].rearrange("k p t -> p k t")).then_inc(S("ld_edge"), 16)
            sp.dma_start(iota[:], ins["iota"]).then_inc(S("ld_const"), 16)
            sp.dma_start(x_in[:], ins["x"].rearrange("(t p) d -> p t d", p=P)).then_inc(S("ld_x"), 16)
            sp.dma_start(eye[:], ins["eye"]).then_inc(S("ld_eye"), 16)

            def weights(i0, i1):
                for i in range(i0, i1):
                    if i >= RAW:
                        sp.wait_ge(S("w_lo"), i - RAW + 1)
                    sp.dma_start(wraw[:, i % RAW, :], ins["weights"][i]).then_inc(w_in[i % RAW], 16)

            sp.dma_start(qT[:], ins["qT"]).then_inc(S("ld_q"), 16)
            weights(0, 2)
            sp.dma_start(sel32, ins["sel"]).then_inc(S("ld_sel"), 16)
            sp.dma_start(bcol[:], ins["bcol"]).then_inc(S("ld_bcol"), 16)

            def hg_rows(b, par, cols, sem):
                for part, hg in enumerate((hgH, hgL)):
                    n0 = NB * (b % 4)
                    src = f(hg[n0:n0 + NB, b // 4, cols])
                    w = cols.stop - cols.start
                    sp.dma_start(f(lhs[32 * part:32 * part + 32, par, :, cols]),
                                 src.unsqueeze(1).broadcast_to([NB, 2, w])).then_inc(sem, 16)

            def qg_rows(b, par, sem):
                for part, qg in enumerate((qgH, qgL)):
                    for half in range(2):
                        q0 = (b % 2) * LQ + 32 * half
                        sp.dma_start(f(lhs[64 + 32 * part:96 + 32 * part, par, half, :]),
                                     f(qg[q0:q0 + 32, b // 2, :])).then_inc(sem, 16)

            done = 2
            for g in range(2):
                weights(done, HG[g] + 3 + RAW)
                done = HG[g] + 3 + RAW
                sp.wait_ge(S("qg_lo"), 3)
                qg_rows(0, 0, S("lhs_q"))
                for j in range(3):
                    sp.wait_ge(S("hg_lo"), 3 * g + j + 1)
                    hg_rows(0, 0, slice(j * 256, (j + 1) * 256), S(f"lhs_c{j}"))
                for b in range(1, B):
                    if b >= 2:
                        sp.wait_ge(S("z_ready"), g * B * CPB + CPB * (b - 1))
                    sem = S("lhs_in1") if b % 2 else S("lhs_in")
                    hg_rows(b, b % 2, slice(0, D), sem)
                    qg_rows(b, b % 2, sem)
            sp.wait_ge(S("z_ready"), 2 * B * CPB)
            sp.dma_start(x[:], ins["x"].rearrange("(t p) d -> p t d", p=P)).then_inc(S("x_res"), 16)
            weights(done, NBLK)
            sp.wait_ge(S("lay_done"), 3)
            for t in range(NT):
                sp.dma_start(out[t * P:(t + 1) * P, :], x[:, t, :]).then_inc(S("stored"), 16)
            sp.wait_ge(S("stored"), 16 * NT)

        @block.tensor
        def _(pe):
            def w_wait(i):
                pe.wait_ge(S("w_lo"), i + 1)

            def transposes(k):
                src = hnat0 if k == 0 else hnat1
                pe.wait_ge(S("ln_h"), 2 * (k + 1))
                dst = banks(0, 3).rearrange("p (k n) -> p k n", k=KT)
                for kt in range(KT):
                    for t in range(NT):
                        m = pe.transpose(dst[:, kt, t * P:(t + 1) * P], src[:, t, kt * P:(kt + 1) * P], identity)
                    if kt % 2:
                        m.then_inc(S("lnT"), 1)

            def natural(i, bank, a, fresh=None):
                w_wait(i)
                wb = wblock(i, KT, 256)
                for t in range(NT):
                    for kt in range(KT):
                        if fresh and t == 0 and kt % 2 == 0:
                            pe.wait_ge(S(fresh[0]), fresh[1] + kt // 2 + 1)
                        m = mm3(pe, ps[:, bank, t * 256:(t + 1) * 256],
                                tuple(h[:, kt, t * P:(t + 1) * P] for h in a),
                                tuple(q[:, kt, :] for q in wb), kt == 0, kt == KT - 1)
                m.then_inc(S("w_used"), 1)

            def natural_units(i0, k, kp, ready):
                for unit in range(3 * k):
                    i, cb, kt = i0 + unit // UPB, unit // k, unit % k
                    if unit % UPB == 0:
                        w_wait(i)
                    if cb == 0:
                        pe.wait_ge(S("gt_ready"), ready(kt))
                    elif cb == 1 and kt == 0:
                        pe.wait_ge(S("gt_ready"), ready(k - 1))
                    wb = wblock(i, UPB, 256, kp)
                    for t in range(NT):
                        m = mm3(pe, ps[:, ubank(cb) + t, 0:256], tuple(h[0:kp, kt, t * P:(t + 1) * P] for h in (gTH, gTL)),
                                tuple(q[:, unit % UPB, :] for q in wb), kt == 0, kt == k - 1)
                    if unit % UPB == UPB - 1:
                        m.then_inc(S("w_used"), 1)
                    elif kt == k - 1:
                        m.then_inc(S("col_done"), 1)

            def count_tile(t, k, start, stop):
                pe.wait_ge(S("oh_ready"), t + 1)
                oh = ohD[:, k, :, :].rearrange("p r n -> p (r n)")
                for st in range(NT):
                    s = ohS[:, k, st * P:(st + 1) * P]
                    pe.matmul(ps[:, 4 + 2 * st, :], s, oh[:, 0:512], start=start, stop=stop)
                    m = pe.matmul(ps[:, 5 + 2 * st, 0:256], s, oh[:, 512:768], start=start, stop=stop)
                m.then_inc(S("oh_used"), 1)

            for k in range(4):
                count_tile(k, k, k == 0, False)
            with pe.Fori(1, ET // 4 - 1) as g:
                for k in range(4):
                    count_tile(g * 4 + k, k, False, False)
            for k in range(4):
                count_tile(ET - 4 + k, k, False, k == 3)

            pe.wait_ge(S("ld_eye"), 16)
            transposes(0)
            pe.wait_ge(S("lnL"), 3)
            pe.wait_ge(S("qT_ready"), 2)
            for j in range(3):
                i = QG + j
                w_wait(i)
                if j >= 2:
                    pe.wait_ge(S("qg_lo"), j - 1)
                wb = wblock(i, KT, 256)
                for rt in range(QT):
                    for kt in range(KT):
                        m = mm3(pe, ps[:, 2 * (j % 2) + rt // 2, (rt % 2) * 256:(rt % 2) * 256 + 256],
                                (qTH[:, kt, rt * P:(rt + 1) * P], qTL[:, kt, rt * P:(rt + 1) * P]),
                                tuple(q[:, kt, :] for q in wb), kt == 0, kt == KT - 1)
                m.then_inc(S("w_used"), 1)
                if j == 0:
                    pe.wait_ge(S("cnt_ready"), 4)
                    pe.wait_ge(S("cr_ready"), 1)
                    pe.wait_ge(S("ones_ready"), 1)
                    for st in range(NT):
                        c = cr[:, st, :, :].rearrange("p r n -> p (r n)")
                        pe.matmul(ps[:, 4, :], ones[:], c[:, 0:512], start=st == 0, stop=st == 1)
                        m = pe.matmul(ps[:, 5, 0:256], ones[:], c[:, 512:768], start=st == 0, stop=st == 1)
                    m.then_inc(S("colsum_mm"), 1)
                    for st in range(NT):
                        for dt in range(NT):
                            m = pe.transpose(ps[:, 6, dt * N + st * P:dt * N + (st + 1) * P],
                                             cnt[:, st, dt * P:(dt + 1) * P], identity)
                    m.then_inc(S("cntT_mm"), 1)

            for g in range(2):
                ht = hT[0]
                pe.wait_ge(S("qg_lo"), 3)
                for j in range(9):
                    if j >= 4:
                        pe.wait_ge(S("rel_lo"), 9 * g + j - 3)
                    natural(REL[g] + j, j % 4, ht, ("hn_lo", 0) if g and j == 0 else None)
                pe.wait_ge(S("rel_lo"), 9 * (g + 1))
                pe.wait_ge(S("cn_ready"), 1)
                for j in range(3):
                    i = ROOT[g] + j
                    w_wait(i)
                    wb = wblock(i, KT, 256)
                    for o in range(2):
                        ot = 2 * j + o
                        dst = ps[:, j, o * N:(o + 1) * N]
                        for r in range(R):
                            for st in range(NT):
                                c0 = r * D + ot * P
                                mm3(pe, dst, (xrH[:, st, c0:c0 + P], xrL[:, st, c0:c0 + P]),
                                    (cnH[:, st, r, :], cnL[:, st, r, :]), r == 0 and st == 0, False)
                        for kt in range(KT):
                            m = mm3(pe, dst, tuple(q[:, kt, o * P:(o + 1) * P] for q in wb),
                                    tuple(h[:, kt, :] for h in ht), False, kt == KT - 1)
                    m.then_inc(S("w_used"), 1)
                for j in range(3):
                    natural(HG[g] + j, 3 + j, (h2H, h2L), None if j else ("h2_ready", 3 * g))

                base = g * B * CPB
                pe.wait_ge(S("hg_lo"), 3 * (g + 1))
                pe.wait_ge(S("sel_ready"), 1)

                def args(c, k, ring):
                    if ring:
                        pe.wait_ge(S("mul_ready"), c - ZR + 1)
                    par, ft, half = k // CPB, (k % CPB) // 2, k % 2
                    for h in range(2):
                        m = pe.matmul(ps[:, 2 * (k % ZR) + h, :], lhs[:, par, half, ft * P:(ft + 1) * P],
                                      sel[:, h, :], start=True, stop=True)
                    m.then_inc(S("z_ready"), 1)

                def reduce(c, k):
                    ft, half = (k % CPB) // 2, k % 2
                    pe.wait_ge(S("fold_ready"), c + 1)
                    for s in range(2):
                        m = pe.matmul(ps[:, 6 + k // GC % 2, ft % 2 * 256:ft % 2 * 256 + 256], identity,
                                      fold[:, k % PR, s * 256:(s + 1) * 256],
                                      start=half == 0 and s == 0, stop=half == 1 and s == 1)
                    m.then_inc(S("red_done"), 1)

                def pair(c0, b0, pairs, first_pair, last_pair):
                    for k in range(2 * CPB):
                        n = k + ZR
                        if n == CPB:
                            pe.wait_ge(S("lhs_in1"), lhs_count(pairs + 1))
                        if n == 2 * CPB and not last_pair:
                            pe.wait_ge(S("lhs_in"), lhs_count(pairs + (1 - g)))
                        if first_pair and n in (4, 8):
                            pe.wait_ge(S(f"lhs_c{n // 4}"), 32 * (g + 1))
                        if n < 2 * CPB or not last_pair:
                            args(c0 + n, n % (2 * CPB), True)
                        r = k - LAGR
                        if r >= 0 or not first_pair:
                            if r % GC == 0 and (r >= 2 * GC or not (first_pair and g == 0)):
                                pe.wait_ge(S("qi_ready"), b0 * 3 + (r // GC - 1))
                            reduce(c0 + r, r % (2 * CPB))

                def lhs_count(i):
                    return i * 96

                pe.wait_ge(S("lhs_q"), 64 * (g + 1))
                pe.wait_ge(S("lhs_c0"), 32 * (g + 1))
                for c in range(ZR):
                    args(base + c, c, False)
                pair(base, g * B, 4 * g, True, False)
                with pe.Fori(1, B // 2 - 1) as bp:
                    pair(bp * (2 * CPB) + base, bp * 2 + g * B, bp + 4 * g, False, False)
                pair(base + 6 * CPB, g * B + 6, 4 * g + 3, False, True)
                for r in range(2 * CPB - LAGR, 2 * CPB):
                    reduce(base + 6 * CPB + r, r)

                pe.wait_ge(S("qi_ready"), 3 * B * (g + 1))
                for j in range(3):
                    for half, b_pair in enumerate(((h2H, h2L), (qiH, qiL))):
                        i = WQ[g] + 2 * j + half
                        w_wait(i)
                        wb = wblock(i, KT, 256)
                        for o in range(2):
                            for kt in range(KT):
                                m = mm3(pe, ps[:, 2 * j + o, 0:N], tuple(q[:, kt, o * P:(o + 1) * P] for q in wb),
                                        tuple(h[:, kt, :] for h in b_pair), half == 0 and kt == 0,
                                        half == 1 and kt == KT - 1)
                        m.then_inc(S("w_used"), 1)

            pe.wait_ge(S("hn_ready"), 6)
            for t in range(NT):
                for kt in range(KT):
                    m = pe.transpose(ps[:, 2 * t + kt // 3, (kt % 3) * P:(kt % 3 + 1) * P],
                                     th[:, kt, t * P:(t + 1) * P], identity)
            m.then_inc(S("hnT"), 1)

            nh = [0]

            def row(dst, pair_, rows_, k):
                one = eyeR[0:rows_, k:k + 1].broadcast_to([rows_, P])
                pe.matmul(dst, one, pair_[0], start=True, stop=False)
                return pe.matmul(dst, one, pair_[1], start=False, stop=True)

            def attention_T(a, heads, gs, cw, nct, done, order):
                pe.wait_ge(S("al_ready"), a + 1)
                for t in range(NT):
                    m = pe.transpose(ps[0:heads, 6, t * P:(t + 1) * P], al[:, 0, t, 0:heads], identity)
                m.then_inc(S("alT_mm"), 1)
                pe.wait_ge(S("alT_ready"), a // 2 + 1)
                pe.wait_ge(S("eyeR_ready"), 1)
                for h in range(heads):
                    m = row(ps[:, h // 2, (h % 2) * N:(h % 2 + 1) * N], tuple(q[0:heads, :] for q in aT), heads, h)
                    if h % 2:
                        m.then_inc(S("als_rows"), 1)
                for q in range(2):
                    pe.wait_ge(S("b_ready"), ngroups[a] + q + 1)
                    for t in range(NT):
                        dst = ps[0:2 * gs, 6 + q, (1 - q) * N + t * P:(1 - q) * N + (t + 1) * P]
                        m = pe.transpose(dst, bb[:, t, 2 * gs * q:2 * gs * (q + 1)], identity)
                    m.then_inc(S("bT_mm"), 1)

                def drows(h):
                    q = h // gs
                    pe.wait_ge(S("bT_ready"), 2 * (a // 2) + q + 1)
                    if h >= 2:
                        pe.wait_ge(S("exps_ready"), nh[0] + h - 1)
                    for v in range(2):
                        m = row(ps[:, 4 + h % 2, v * N:(v + 1) * N], tuple(w[0:2 * gs, q, :] for w in bT),
                                2 * gs, v * gs + h % gs)
                    m.then_inc(S("brow_mm"), 1)

                def sums(h):
                    s, q = h % 2, h // gs
                    pe.wait_ge(S("pt_lo"), nh[0] + h + 1)
                    first_h, last_h = h % gs == 0, h % gs == gs - 1
                    if q:
                        pe.wait_ge(S("u_ready"), done + h - gs + 1)
                    for st in range(NT):
                        for k, w in enumerate((ptH, ptL)):
                            m = pe.matmul(ps[:, 6, q * N:(q + 1) * N], zsel[:, P - h:2 * P - h], w[:, s, st, :],
                                          start=first_h and st == 0 and k == 0,
                                          stop=last_h and st == NT - 1 and k == 1, skip_group_check=True)
                    if last_h:
                        m.then_inc(S("zT_mm"), 1)
                    for ct in range(nct):
                        c0 = (h * nct + ct) * cw
                        at = (h % gs) * (8 // gs) + ct
                        dst = ps[0:cw, at // 2, (at % 2) * N:(at % 2 + 1) * N]
                        for st in range(NT):
                            m = mm3(pe, dst, (hH[:, st, c0:c0 + cw], hL[:, st, c0:c0 + cw]),
                                    (ptH[:, s, st, :], ptL[:, s, st, :]), st == 0, st == NT - 1)
                    m.then_inc(S("out_mm"), 1)

                def rzrow(p):
                    pe.wait_ge(S("rzT_ready"), 2 * (a // 2) + 2 * p // gs + 1)
                    if p:
                        pe.wait_ge(S("rz_ready"), done // 2 + p)
                    for k in range(2):
                        m = row(ps[:, 7, k * N:(k + 1) * N], tuple(w[0:heads, :] for w in rzT), heads, 2 * p + k)
                    m.then_inc(S("rz_mm"), 1)

                for step in order.split():
                    {"d": drows, "s": sums, "z": rzrow}[step[0]](int(step[1]))
                nh[0] += heads

            def attention_1(a):
                pe.wait_ge(S("al_ready"), a + 1)
                for t in range(NT):
                    m = pe.matmul(ps[:, 6, t * P:(t + 1) * P], al[:, 0, t, 0:1].broadcast_to([P, P]), identity,
                                  start=True, stop=True)
                m.then_inc(S("als_rows"), 1)
                pe.wait_ge(S("b_ready"), ngroups[a] + 1)
                for v in range(2):
                    for t in range(NT):
                        m = pe.matmul(ps[:, 7, v * N + t * P:v * N + (t + 1) * P],
                                      bb[:, t, v:v + 1].broadcast_to([P, P]), identity, start=True, stop=True)
                m.then_inc(S("brow_mm"), 1)
                pe.wait_ge(S("pt_lo"), nh[0] + 1)
                for dt in range(NT):
                    for fc in range(2):
                        w = 384 + 2 * fc
                        for st in range(NT):
                            q = ptH[:, 0, st, dt * P:(dt + 1) * P], ptL[:, 0, st, dt * P:(dt + 1) * P]
                            m = mm3(pe, ps[:, 2 * dt + fc, 0:w], q,
                                    (hH[:, st, fc * 384:fc * 384 + w], hL[:, st, fc * 384:fc * 384 + w]),
                                    st == 0, st == NT - 1)
                    m.then_inc(S("fin_mm"), 1)
                nh[0] += 1

            pe.wait_ge(S("zsel_ready"), 1)
            transposes(1)
            for j in range(3):
                natural(G1A + j, j, hT[1], None if j else ("lnL", 3))
            attention_T(0, H1, 4, C1, 1, 0, "d0 d1 s0 d2 s1 d3 s2 d4 s3 d5 z0 s4 d6 z1 s5 d7 s6 s7 z2 z3")
            natural_units(G1B, H1, C1, lambda kt: kt + 1)
            attention_1(1)
            transposes(2)
            for j in range(8):
                if j >= 4:
                    pe.wait_ge(S("gh_free"), 6 + j - 3)
                natural(G2A + j, j % 4, hT[1], None if j else ("lnL", 6))
            attention_T(2, H2, 2, P, 4, H1, "d0 d1 s0 d2 s1 d3 z0 s2 s3 z1")
            natural_units(G2B, CT2, P, lambda kt: H1 + kt // 4 + 1)
            attention_1(3)
            transposes(3)
            for j in range(3):
                natural(GCN + j, j, hT[1], None if j else ("lnL", 9))
            pe.wait_ge(S("gh_lo"), 3)
            for dt in range(NT):
                for fc in range(2):
                    for st in range(NT):
                        c = cntS[:, st, dt * P:(dt + 1) * P]
                        for k, h in enumerate((hH, hL)):
                            m = pe.matmul(ps[:, 4 + 2 * dt + fc, 0:384], c, h[:, st, fc * 384:fc * 384 + 384],
                                          start=st == 0 and k == 0, stop=st == NT - 1 and k == 1)
                m.then_inc(S("fin_mm"), 1)

        @block.scalar
        def _(act):
            def split_hi(i):
                if i >= NBLK:
                    return
                act.wait_ge(w_in[i % RAW], 16 * (i // RAW + 1))
                if i >= SPL:
                    act.wait_ge(S("w_used"), i - SPL + 1)
                act.copy(wH[:, i % SPL, :], wraw[:, i % RAW, :]).then_inc(S("w_hi"), 1)

            def table(func):
                act.activation(warm[:, 1:2], warm[:, 0:1], func).then_inc(S("achain"), 1)
                tables[0] += 1
                act.wait_ge(S("achain"), tables[0])

            tables = [0]

            def ln(k):
                table(ACT.Sqrt)
                act.wait_ge(S("ln_var"), k + 1)
                act.sqrt(std[:], var[:]).then_inc(S("ln_std"), 1)

            def ln_relu(k):
                for j in range(3):
                    act.wait_ge(S("lnT"), 3 * k + j + 1)
                    act.activation(hT[min(k, 1)][0][:, 2 * j:2 * j + 2, :].rearrange("p k n -> p (k n)"), ps[:, j, :],
                                   ACT.Relu).then_inc(S("lnH"), 1)

            act.wait_ge(S("warm_ready"), 1)
            act.wait_ge(S("ld_q"), 16)
            act.copy(qTH[:], qT[:]).then_inc(S("qT_ready"), 1)
            split_hi(0)
            split_hi(1)
            split_hi(2)
            ln(0)
            ln_relu(0)
            for j in range(3):
                act.wait_ge(S("w_used"), QG + j + 1)
                act.copy(qgH[:, :, j * 256:(j + 1) * 256],
                         banks(2 * (j % 2), 2).rearrange("p (a b) -> p a b", b=256)).then_inc(S("qg_hi"), 1)
                split_hi(QG + j + 3)
            act.wait_ge(S("deg_ready"), 1)
            act.sqrt(dinv[:], var[:]).then_inc(S("sdeg"), 1)
            for g in range(2):
                for j in range(9):
                    act.wait_ge(S("w_used"), REL[g] + j + 1)
                    act.copy(xrH[:, :, j * 256:(j + 1) * 256],
                             ps[:, j % 4, :].rearrange("p (t w) -> p t w", t=NT)).then_inc(S("rel_hi"), 1)
                    split_hi(REL[g] + j + 3)
                act.wait_ge(S("ld_bcol"), 16)
                for j in range(3):
                    act.wait_ge(S("w_used"), ROOT[g] + j + 1)
                    for o in range(2):
                        ot = 2 * j + o
                        act.activation(h32[:, ot, :], ps[:, j, o * N:(o + 1) * N], ACT.Relu,
                                       bias=bcol[:, KT * g + ot:KT * g + ot + 1]).then_inc(S("root_h"), 1)
                    split_hi(ROOT[g] + j + 3)
                for j in range(3):
                    act.wait_ge(S("w_used"), HG[g] + j + 1)
                    act.copy(hgH[:, :, j * 256:(j + 1) * 256],
                             ps[:, 3 + j, :].rearrange("p (t w) -> p t w", t=NT)).then_inc(S("hg_hi"), 1)
                    split_hi(HG[g] + j + 3)
                table(ACT.Sigmoid)
                base = g * B * CPB

                with act.Fori(0, B) as b:
                    for k in range(CPB):
                        c = b * CPB + (base + k)
                        ft = k // 2
                        act.wait_ge(S("z_ready"), c + 1)
                        z = banks(2 * (k % ZR), 2)
                        act.activation(z, z, ACT.Sigmoid, bias=bcol[:, 12 + ft:13 + ft]).then_inc(S("sig_ready"), 1)
                act.wait_ge(S("qi_ready"), 3 * B * (g + 1))
                act.activation(th[:, :, :], th[:, :, :], ACT.Tanh).then_inc(S("th_ready"), 1)
                for j in range(3):
                    act.wait_ge(S("w_used"), WQ[g] + 2 * j + 1)
                    split_hi(WQ[g] + 2 * j + 3)
                    act.wait_ge(S("w_used"), WQ[g] + 2 * j + 2)
                    for o in range(2):
                        ot = 2 * j + o
                        act.activation(al32[:, j, o * N:(o + 1) * N], ps[:, 2 * j + o, 0:N], ACT.Sigmoid,
                                       bias=bcol[:, 18 + ot:19 + ot]).then_inc(S("alpha_ready"), 1)
                    split_hi(WQ[g] + 2 * j + 4)

            nh = [0]

            def tile_hi(src, cols):
                act.copy(hH[:, :, cols:cols + 256], src).then_inc(S("gh_hi"), 1)

            def tiles_natural(i0, n):
                for j in range(n):
                    act.wait_ge(S("w_used"), i0 + j + 1)
                    tile_hi(ps[:, j % 4, :].rearrange("p (t w) -> p t w", t=NT), j * 256)
                    split_hi(i0 + j + 3)

            def tiles_units(i0, k, cols_done):
                nblk, cb = 3 * k // UPB, 0
                for j in range(nblk):
                    while cb < 2 and k * (cb + 1) <= UPB * (j + 1):
                        act.wait_ge(S("col_done"), cols_done + cb + 1)
                        tile_hi(ps[:, ubank(cb):ubank(cb) + 2, 0:256], cb * 256)
                        cb += 1
                    act.wait_ge(S("w_used"), i0 + j + 1)
                    if j == nblk - 1:
                        tile_hi(ps[:, ubank(2):ubank(2) + 2, 0:256], 512)
                    split_hi(i0 + j + 3)

            def exps(h, bank, slot):
                k = nh[0] + h
                act.wait_ge(S("brow_mm"), k + 1)
                if h >= 2:
                    act.wait_ge(S("pt_lo"), k - 1)
                for st in range(NT):
                    act.activation(e1[:, slot, st, :], ps[:, bank, 0:N], ACT.Exp, bias=al[:, 0, st, h:h + 1])
                    m = act.activation(e2[:, slot, st, :], ps[:, bank, N:2 * N], ACT.Exp,
                                       bias=als2[:, st, h:h + 1])
                m.then_inc(S("exps_ready"), 1)

            def attention_T(heads, cw, nct, b0, done, order):
                def rz_copy(p):
                    act.wait_ge(S("rz_mm"), done // 2 + p + 1)
                    if p:
                        act.wait_ge(S("u_ready"), done + 2 * p)
                    act.copy(rz[:, :, :].rearrange("p k n -> p (k n)"), ps[:, 7, :]).then_inc(S("rz_ready"), 1)

                def branches(h):
                    s = h % 2
                    act.wait_ge(S("u_ready"), done + h + 1)
                    if h >= 2:
                        act.wait_ge(S("gt_ready"), done + h - 1)
                    for ct in range(nct):
                        bias = bcol[0:cw, b0 + h * nct + ct:b0 + h * nct + ct + 1]
                        act.activation(ru[0:cw, s, ct, :], u[0:cw, s, ct, :], ACT.Relu, bias=bias)
                        m = act.activation(u[0:cw, s, ct, :], u[0:cw, s, ct, :], ACT.Exp, bias=bias)
                    m.then_inc(S("act_u"), 1)

                table(ACT.Exp)
                for step in order.split():
                    h = int(step[1])
                    if step[0] == "e":
                        exps(h, 4 + h % 2, h % 2)
                    else:
                        {"z": rz_copy, "b": branches}[step[0]](h)
                nh[0] += heads

            def attention_1():
                table(ACT.Exp)
                exps(0, 7, 0)
                nh[0] += 1

            def load_rows(att1, att2, bias):
                if att1 is not None:
                    n = att1.shape[1]
                    act.dma_start(arow1[:, :, 0:n], att1.partition_broadcast(P)).then_inc(S("arow1_in"), 16)
                if att2 is not None:
                    act.dma_start(arow2[:], att2.partition_broadcast(P)).then_inc(S("arow2_in"), 16)
                act.dma_start(brow[:], bias.partition_broadcast(P)).then_inc(S("brow_in"), 16)

            act.wait_ge(S("x_ready"), 1)
            load_rows(ins["att11"], ins["att12"], ins["brow1"])
            ln(1)
            ln_relu(1)
            tiles_natural(G1A, 3)
            attention_T(H1, C1, 1, 24, 0, "e0 e1 e2 e3 e4 e5 z0 e6 b0 b1 z1 e7 b2 b3 z2 b4 z3 b5 b6 b7")
            tiles_units(G1B, H1, 0)
            attention_1()
            act.wait_ge(S("lay_done"), 1)
            load_rows(ins["att21"], ins["att22"], ins["brow2"])
            ln(2)
            ln_relu(2)
            tiles_natural(G2A, 8)
            attention_T(H2, P, 4, 32, H1, "e0 e1 e2 e3 z0 b0 b1 z1 b2 b3")
            tiles_units(G2B, CT2, 2)
            attention_1()
            act.wait_ge(S("lay_done"), 2)
            load_rows(None, None, ins["brow3"])
            ln(3)
            ln_relu(3)
            for j in range(3):
                act.wait_ge(S("w_used"), GCN + j + 1)
                for t in range(NT):
                    m = act.activation(hH[:, t, j * 256:(j + 1) * 256], ps[:, j, t * 256:(t + 1) * 256], ACT.Copy,
                                       scale=dinv[:, t:t + 1])
                m.then_inc(S("gh_hi"), 1)

        @block.gpsimd
        def _(pool):
            def split_lo(i):
                if i >= NBLK:
                    return
                pool.wait_ge(S("w_hi"), i + 1)
                pool.tensor_tensor(wL[:, i % SPL, :], wraw[:, i % RAW, :], f(wH[:, i % SPL, :]), ALU.subtract)\
                    .then_inc(S("w_lo"), 1)

            pool.wait_ge(S("qT_ready"), 1)
            pool.tensor_tensor(qTL[:], qT[:], f(qTH[:]), ALU.subtract).then_inc(S("qT_ready"), 1)
            for i in range(0, HG[0] + 6):
                split_lo(i)
            for g in range(2):
                base = g * B * CPB
                if g:
                    for i in range(HG[0] + 6, HG[1] + 6):
                        split_lo(i)

                def folds(c, k, wait):
                    pool.wait_ge(S("mul_ready"), c + 1)
                    if wait:
                        pool.wait_ge(S("red_done"), c - PR + 1)
                    s = k % PR
                    pool.tensor_tensor(fold[:, s, :], prod[:, s, 0:CH // 2], prod[:, s, CH // 2:CH], ALU.add)\
                        .then_inc(S("fold_ready"), 1)

                for k in range(CPB):
                    folds(base + k, k, k >= PR)
                with pool.Fori(1, B) as b:
                    for k in range(CPB):
                        folds(b * CPB + (base + k), k, True)
            def pt_low(k, slot):
                pool.wait_ge(S("pt_hi"), k + 1)
                pool.tensor_tensor(ptL[:, slot, :, :], e1[:, slot, :, :], f(ptH[:, slot, :, :]), ALU.subtract)\
                    .then_inc(S("pt_lo"), 1)

            def gt_low(h, cw, nct, done):
                pool.wait_ge(S("elu_ready"), done + h + 1)
                o = slice(h * nct, (h + 1) * nct)
                pool.tensor_tensor(gTL[0:cw, o, :], ru[0:cw, h % 2, 0:nct, :], f(gTH[0:cw, o, :]), ALU.subtract)\
                    .then_inc(S("gt_ready"), 1)

            def attention_T(k0, cw, nct, done, order):
                for step in order.split():
                    h = int(step[1])
                    if step[0] == "p":
                        pt_low(k0 + h, h % 2)
                    else:
                        gt_low(h, cw, nct, done)

            for i in range(HG[1] + 6, G1A + 6):
                split_lo(i)
            attention_T(0, C1, 1, 0, "p0 p1 p2 p3 p4 p5 p6 g0 p7 g1 g2 g3 g4 g5 g6 g7")
            for i in range(G1A + 6, G2A + 3):
                split_lo(i)
            pt_low(H1, 0)
            for i in range(G2A + 3, G2B + 3):
                split_lo(i)
            attention_T(H1 + 1, P, 4, H1, "p0 p1 p2 p3 g0 g1 g2 g3")
            for i in range(G2B + 3, NBLK):
                split_lo(i)
            pt_low(H1 + 1 + H2, 0)

        @block.vector
        def _(dve):
            steps = [0]

            def link(ins_):
                steps[0] += 1
                ins_.then_inc(S("chain"), 1)
                dve.wait_ge(S("chain"), steps[0])

            def ln(k, src, dst):
                for t in range(NT):
                    for j in range(2):
                        m = dve.bn_stats(stat[:, t, j, :], src[:, t, 384 * j:384 * j + 384])
                link(m)
                for t in range(NT):
                    m = dve.bn_aggr(mv[:, t, :], stat[:, t, :, :])
                link(m)
                dve.tensor_scalar(var[:], mv[:, :, 1], EPS_LN, None, ALU.add).then_inc(S("ln_var"), 1)
                dve.wait_ge(S("ln_std"), k + 1)
                link(dve.reciprocal(rstd[:], std[:]))
                for t in range(NT):
                    dve.tensor_scalar(dst[:, t, :], src[:, t, :], mv[:, t, 0:1], rstd[:, t:t + 1],
                                      ALU.subtract, ALU.mult).then_inc(S("ln_h"), 1)

            def ln_lo(k):
                for j in range(3):
                    dve.wait_ge(S("lnH"), 3 * k + j + 1)
                    hh, hl = (t[:, 2 * j:2 * j + 2, :].rearrange("p k n -> p (k n)") for t in hT[min(k, 1)])
                    dve.scalar_tensor_tensor(hl, ps[:, j, :], 0.0, f(hh), ALU.max, ALU.subtract)\
                       .then_inc(S("lnL"), 1)

            def split(dst, src, hi_sem=None, lo_sem=None):
                link(dve.tensor_copy(dst[0], src))
                return dve.tensor_tensor(dst[1], src, f(dst[0]), ALU.subtract)

            dve.memset(warm[:], 1.0).then_inc(S("warm_ready"), 1)
            dve.wait_ge(S("ld_edge"), 16)
            link(dve.tensor_copy(edge_f[:], edge_i[:]))
            link(dve.scalar_tensor_tensor(key[:], edge_f[:, 2, :], float(N), edge_f[:, 1, :], ALU.mult, ALU.add))
            dve.wait_ge(S("ld_const"), 16)

            def onehot(t, k):
                dve.tensor_scalar(ohS[:, k, :], iota[:, 0:N], edge_f[:, 0, bass.ds(t, 1)], None, ALU.is_equal)
                dve.tensor_scalar(ohD[:, k, :, :].rearrange("p r n -> p (r n)"), iota[:], key[:, bass.ds(t, 1)],
                                  None, ALU.is_equal).then_inc(S("oh_ready"), 1)

            for k in range(4):
                onehot(k, k)
            with dve.Fori(1, ET // 4) as g:
                for k in range(4):
                    dve.wait_ge(S("oh_used"), g * 4 + (k - 3))
                    onehot(g * 4 + k, k)
            dve.wait_ge(S("ld_x"), 16)
            ln(0, x_in, hnat0)
            dve.wait_ge(S("ld_sel"), 16)
            dve.tensor_copy(sel[:, :, :].rearrange("p a b -> p (a b)"), sel32).then_inc(S("sel_ready"), 1)
            dve.wait_ge(S("ld_eye"), 16)
            dve.tensor_copy(eyeR[:], identity).then_inc(S("eyeR_ready"), 1)
            dve.tensor_copy(ones[:], warm[:, 0:1].broadcast_to([P, P])).then_inc(S("ones_ready"), 1)
            ln_lo(0)
            dve.wait_ge(S("oh_used"), ET)
            for st in range(NT):
                c = cr[:, st, :, :].rearrange("p r n -> p (r n)")
                dve.tensor_copy(c[:, 0:512], ps[:, 4 + 2 * st, :]).then_inc(S("cnt_ready"), 1)
                dve.tensor_copy(c[:, 512:768], ps[:, 5 + 2 * st, 0:256]).then_inc(S("cnt_ready"), 1)
            dve.wait_ge(S("cnt_ready"), 4)
            link(dve.tensor_tensor(cnt[:], f(cr[:, :, 0, :]), f(cr[:, :, 1, :]), ALU.add))
            dve.tensor_tensor(cnt[:], cnt[:], f(cr[:, :, 2, :]), ALU.add).then_inc(S("cr_ready"), 1)
            dve.wait_ge(S("cr_ready"), 1)
            dve.tensor_tensor(cntS[:], cnt[:], eye[:], ALU.add).then_inc(S("cr_ready"), 1)
            for j in range(3):
                dve.wait_ge(S("qg_hi"), j + 1)
                q = banks(2 * (j % 2), 2).rearrange("p (a b) -> p a b", b=256)
                cs = slice(j * 256, (j + 1) * 256)
                dve.tensor_tensor(qgL[:, :, cs], q, f(qgH[:, :, cs]), ALU.subtract).then_inc(S("qg_lo"), 1)

            dve.wait_ge(S("colsum_mm"), 1)
            dve.wait_ge(S("sel_ready"), 1)
            inv = cn32[:, 0, :, :].rearrange("p r n -> p (r n)")
            link(dve.tensor_scalar(inv, banks(4, 2)[:, 0:768], 1.0, None, ALU.max))
            inv2 = x_in[:, 0, :]
            link(dve.reciprocal(inv2, inv))
            link(dve.tensor_tensor(cn32[:, :, :, :].rearrange("p t r n -> p t (r n)"),
                                   f(cr[:, :, :, :].rearrange("p t r n -> p t (r n)")),
                                   inv2.unsqueeze(1).broadcast_to([P, NT, R * N]), ALU.mult))
            link(dve.tensor_copy(cnH[:], cn32[:]))
            dve.tensor_tensor(cnL[:], cn32[:], f(cnH[:]), ALU.subtract).then_inc(S("cn_ready"), 1)
            dve.wait_ge(S("cntT_mm"), 1)
            cT = ps[:, 6, :].rearrange("p (t n) -> p t n", t=NT)
            link(dve.tensor_tensor(mask[:, 1, :, :], cT, eye[:], ALU.add))
            dve.tensor_reduce(var[:], mask[:, 1, :, :], AX.X, ALU.add).then_inc(S("deg_ready"), 1)
            dve.wait_ge(S("deg_ready"), 1)
            dve.tensor_scalar(mask[:, 0, :, :], cT, 0.0, NO_EDGE, ALU.is_equal, ALU.mult).then_inc(S("mask_ready"), 1)
            dve.tensor_scalar(mask[:, 1, :, :], mask[:, 1, :, :], 0.0, NO_EDGE, ALU.is_equal, ALU.mult)\
               .then_inc(S("mask_ready"), 1)
            dve.wait_ge(S("sdeg"), 1)
            link(dve.reciprocal(dinv[:], dinv[:]))
            for g in range(2):
                for j in range(9):
                    dve.wait_ge(S("rel_hi"), 9 * g + j + 1)
                    cs = slice(j * 256, (j + 1) * 256)
                    dve.tensor_tensor(xrL[:, :, cs], ps[:, j % 4, :].rearrange("p (t w) -> p t w", t=NT),
                                      f(xrH[:, :, cs]), ALU.subtract).then_inc(S("rel_lo"), 1)
                for j in range(3):
                    dve.wait_ge(S("root_h"), 6 * g + 2 * j + 2)
                    o = slice(2 * j, 2 * j + 2)
                    split((h2H[:, o, :], h2L[:, o, :]), h32[:, o, :]).then_inc(S("h2_ready"), 1)
                for j in range(3):
                    dve.wait_ge(S("hg_hi"), 3 * g + j + 1)
                    cs = slice(j * 256, (j + 1) * 256)
                    dve.tensor_tensor(hgL[:, :, cs], ps[:, 3 + j, :].rearrange("p (t w) -> p t w", t=NT),
                                      f(hgH[:, :, cs]), ALU.subtract).then_inc(S("hg_lo"), 1)
                base = g * B * CPB

                def mul(c, k, b, wait):
                    ft, half = (k % CPB) // 2, k % 2
                    dve.wait_ge(S("sig_ready"), c + 1)
                    if wait:
                        dve.wait_ge(S("fold_ready"), c - PR + 1)
                    q = qT[:, ft, bass.ds(b * LQ + half * 32, 32)]
                    dve.tensor_tensor(prod[:, k % PR, :].rearrange("p (l n) -> p l n", n=NB),
                                      banks(2 * (k % ZR), 2).rearrange("p (l n) -> p l n", n=NB),
                                      q.unsqueeze(2).broadcast_to([P, 32, NB]), ALU.mult).then_inc(S("mul_ready"), 1)

                def sums(b, q, red, n, par):
                    o = slice(2 * q, 2 * q + 2)
                    dst, hi, lo = (t[:, o, bass.ds(b * NB, NB)] for t in (th, qiH, qiL))
                    dve.wait_ge(S("red_done"), red)
                    dve.tensor_reduce(dst, ps[:, 6 + par, :]
                                      .rearrange("p (f l n) -> p f n l", l=8, n=NB), AX.X, ALU.add)\
                       .then_inc(S("sum_step"), 1)
                    dve.wait_ge(S("sum_step"), n)
                    dve.tensor_copy(hi, dst).then_inc(S("sum_hi"), 1)
                    dve.wait_ge(S("sum_hi"), n)
                    dve.tensor_tensor(lo, dst, f(hi), ALU.subtract).then_inc(S("qi_ready"), 1)

                def graph_pair(c0, b0, first_pair):
                    for k in range(2 * CPB):
                        mul(c0 + k, k, b0 + k // CPB, not (first_pair and k < PR))
                        grp = (k - 7) // GC
                        if k % GC == GC - 1 and (grp >= 0 or not first_pair):
                            sums(b0 + grp // 3, grp % 3, c0 + GC * (grp + 1), b0 * 3 + (grp + 1 + 3 * g * B), grp % 2)

                graph_pair(base, 0, True)
                with dve.Fori(1, B // 2) as bp:
                    graph_pair(bp * (2 * CPB) + base, bp * 2, False)
                sums(B - 1, 2, base + B * CPB, 3 * B * (g + 1), 1)
                dve.wait_ge(S("th_ready"), g + 1)
                for j in range(3):
                    o = slice(2 * j, 2 * j + 2)
                    dve.wait_ge(S("alpha_ready"), 6 * g + 2 * j + 2)
                    t2 = th[:, o, :]
                    link(dve.tensor_tensor(t2, t2, h32[:, o, :], ALU.subtract))
                    link(dve.tensor_tensor(t2, t2, al32[:, j, :].rearrange("p (o n) -> p o n", o=2), ALU.mult))
                    dve.tensor_tensor(t2, t2, h32[:, o, :], ALU.add).then_inc(S("hn_ready"), 1)
                    if g == 0:
                        dve.wait_ge(S("hn_ready"), j + 1)
                        split((hT[0][0][:, o, :], hT[0][1][:, o, :]), t2).then_inc(S("hn_lo"), 1)

            dve.wait_ge(S("hnT"), 1)
            dve.wait_ge(S("x_res"), 16)
            x4 = x[:, :, :].rearrange("p t (f w) -> p (t f) w", f=2)
            dve.tensor_tensor(x4, x4, ps[:, 0:4, 0:384], ALU.add).then_inc(S("x_ready"), 1)
            dve.wait_ge(S("x_ready"), 1)

            tiles, nh, rows = [0], [0], [0]

            def tile_lo(q, cols, arow, per):
                j = cols // 256
                dve.wait_ge(S("gh_hi"), tiles[0] + 1)
                tiles[0] += 1
                for v in range(2):
                    m = dve.tensor_tensor(tmp[:, 2 * v:2 * v + 2, :], q,
                                          arow[:, v, cols:cols + 256].unsqueeze(1).broadcast_to([P, NT, 256]), ALU.mult)
                dve.tensor_tensor(hL[:, :, cols:cols + 256], q, f(hH[:, :, cols:cols + 256]), ALU.subtract)\
                   .then_inc(S("gh_free"), 1)
                dve.wait_ge(S("gh_free"), tiles[0])
                link(dve.tensor_reduce(alp[:, :, :, per * j:per * (j + 1)].rearrange("p v t a -> p (v t) a"),
                                       tmp[:, :, :].rearrange("p v (a c) -> p v a c", a=per), AX.X, ALU.add))

            def tiles_natural(n, per):
                for j in range(n):
                    tile_lo(ps[:, j % 4, :].rearrange("p (t w) -> p t w", t=NT), j * 256, arow1, per)

            def tiles_units():
                dve.tensor_copy(hH[:, :, D:D + 2], warm[:, 0:1].unsqueeze(1).broadcast_to([P, NT, 2]))
                dve.memset(f(hL[:, :, D:D + 2]), 0.0)
                for cb in range(3):
                    tile_lo(ps[:, ubank(cb):ubank(cb) + 2, 0:256], cb * 256, arow2, 1)

            def coefficients(a, heads, nparts, gs, msk):
                dve.tensor_reduce(al[:, :, :, 0:heads].rearrange("p v t h -> p (v t) h"),
                                  alp[:, :, :, 0:heads * nparts].rearrange("p v t (h k) -> p (v t) h k", k=nparts),
                                  AX.X, ALU.add).then_inc(S("al_ready"), 1)
                dve.wait_ge(S("al_ready"), a + 1)
                dve.tensor_scalar(als2[:, :, 0:heads], al[:, 0, :, 0:heads], SLOPE, None, ALU.mult)
                if heads > 1:
                    dve.wait_ge(S("alT_mm"), a // 2 + 1)
                    split(tuple(q[0:heads, :] for q in aT), ps[0:heads, 6, 0:N]).then_inc(S("alT_ready"), 1)
                for q in range(heads // gs):
                    for h in range(q * gs, (q + 1) * gs):
                        if h % 2 == 0:
                            rows[0] += 1
                            dve.wait_ge(S("als_rows"), rows[0])
                        row = ps[:, h // 2, (h % 2) * N:(h % 2 + 1) * N] if heads > 1 else ps[:, 6, 0:N]
                        for dt in range(NT):
                            m = dve.tensor_tensor_reduce(junk[2 * h + dt], row, mask[:, msk, dt, :], 1.0, -3.0e38,
                                                         ALU.add, ALU.max, mx[:, dt, h:h + 1])
                    link(m)
                    hs_ = slice(q * gs, (q + 1) * gs)
                    link(dve.tensor_tensor(xs[:, :, hs_], mx[:, :, hs_], al[:, 1, :, hs_], ALU.add))
                    link(dve.scalar_tensor_tensor(ms[:, :, hs_], xs[:, :, hs_], SLOPE, xs[:, :, hs_],
                                                  ALU.mult, ALU.max))
                    c0 = 2 * gs * q
                    dve.tensor_tensor(bb[:, :, c0:c0 + gs], al[:, 1, :, hs_], ms[:, :, hs_], ALU.subtract)
                    dve.scalar_tensor_tensor(bb[:, :, c0 + gs:c0 + 2 * gs], al[:, 1, :, hs_], SLOPE, ms[:, :, hs_],
                                             ALU.mult, ALU.subtract).then_inc(S("b_ready"), 1)
                if heads > 1:
                    for q in range(2):
                        dve.wait_ge(S("bT_mm"), 2 * (a // 2) + q + 1)
                        split(tuple(w[0:2 * gs, q, :] for w in bT), ps[0:2 * gs, 6 + q, (1 - q) * N:(2 - q) * N])\
                            .then_inc(S("bT_ready"), 1)

            def weights_of(h, c):
                k = nh[0] + h
                s = h % 2
                dve.wait_ge(S("exps_ready"), k + 1)
                link(dve.tensor_tensor(e1[:, s, :, :], e1[:, s, :, :], e2[:, s, :, :], ALU.max))
                dve.scalar_tensor_tensor(e1[:, s, :, :], e1[:, s, :, :], 1.0, c, ALU.min, ALU.mult)\
                   .then_inc(S("pt_ready"), 1)
                dve.wait_ge(S("pt_ready"), k + 1)
                if h >= 2:
                    dve.wait_ge(S("out_mm"), out_heads[0] + h - 1)
                dve.tensor_copy(ptH[:, s, :, :], e1[:, s, :, :]).then_inc(S("pt_hi"), 1)

            out_heads = [0]

            def attention_T(a, heads, gs, cw, nct, c, order):
                done = out_heads[0]

                def inverse(q):
                    dve.wait_ge(S("zT_mm"), 2 * (a // 2) + q + 1)
                    link(dve.tensor_scalar(z32[0:heads, :], ps[0:heads, 6, q * N:(q + 1) * N], EPS_SM, None, ALU.add))
                    link(dve.reciprocal(z32[0:heads, :], z32[0:heads, :]))
                    if q:
                        dve.wait_ge(S("rz_mm"), (done + gs) // 2)
                    split(tuple(w[0:heads, :] for w in rzT), z32[0:heads, :]).then_inc(S("rzT_ready"), 1)

                def normalise(h):
                    dve.wait_ge(S("out_mm"), done + h + 1)
                    dve.wait_ge(S("rz_ready"), (done + h) // 2 + 1)
                    at = (h % gs) * (8 // gs)
                    src = banks(at // 2, max(nct // 2, 1))[0:cw, (at % 2) * N:(at % 2 + nct) * N]
                    dve.tensor_tensor(u[0:cw, h % 2, 0:nct, :], src.rearrange("p (c n) -> p c n", n=N),
                                      rz[0:cw, h % 2, :].unsqueeze(1).broadcast_to([cw, nct, N]), ALU.mult)\
                       .then_inc(S("u_ready"), 1)

                def elu(h):
                    s = h % 2
                    dve.wait_ge(S("act_u"), done + h + 1)
                    uu, rr = u[0:cw, s, 0:nct, :], ru[0:cw, s, 0:nct, :]
                    link(dve.tensor_scalar(uu, uu, 1.0, -1.0, ALU.min, ALU.add))
                    link(dve.tensor_tensor(rr, rr, uu, ALU.add))
                    o = slice(h * nct, (h + 1) * nct)
                    dve.tensor_copy(gTH[0:cw, o, :], rr).then_inc(S("elu_ready"), 1)

                for step in order.split():
                    k = int(step[1])
                    if step[0] == "w":
                        weights_of(k, c)
                    else:
                        {"i": inverse, "n": normalise, "g": elu}[step[0]](k)
                nh[0] += heads
                out_heads[0] += heads

            def finish(k, scale_z):
                dve.wait_ge(S("brow_in"), 16 * (k + 1))
                link(dve.tensor_tensor(x[:], x[:], brow[:].unsqueeze(1).broadcast_to([P, NT, D]), ALU.add))
                scale, b0 = (zr, 0) if scale_z else (dinv, 4)
                for dt in range(NT):
                    dve.wait_ge(S("fin_mm"), 2 * k + dt + 1)
                    if scale_z:
                        link(dve.tensor_scalar(zr[:, dt:dt + 1], ps[:, 2 * dt + 1, 384:385], EPS_SM, None, ALU.add))
                        link(dve.reciprocal(zr[:, dt:dt + 1], zr[:, dt:dt + 1]))
                    for fc in range(2):
                        cs = slice(fc * 384, fc * 384 + 384)
                        m = dve.scalar_tensor_tensor(x[:, dt, cs], ps[:, b0 + 2 * dt + fc, 0:384], scale[:, dt:dt + 1],
                                                     x[:, dt, cs], ALU.mult, ALU.add)
                    m.then_inc(S("lay_half"), 1)
                dve.engine_nop().then_inc(S("lay_done"), 1)
                dve.wait_ge(S("lay_half"), 2 * k + 2)

            dve.memset(f(gTH[:, 0, :]), 0.0).then_inc(S("zsel_step"), 1)
            dve.wait_ge(S("zsel_step"), 1)
            dve.tensor_copy(zsel[:], f(gTH[:, 0, :])).then_inc(S("zsel_step"), 1)
            dve.wait_ge(S("zsel_step"), 2)
            dve.tensor_copy(zsel[:, P:P + 1], warm[:, 0:1]).then_inc(S("zsel_ready"), 1)
            ln(1, x, hnat1)
            ln_lo(1)
            dve.wait_ge(S("arow1_in"), 16)
            dve.wait_ge(S("arow2_in"), 16)
            dve.wait_ge(S("mask_ready"), 2)
            tiles_natural(3, 8)
            coefficients(0, H1, 3, 4, 0)
            attention_T(0, H1, 4, C1, 1, cnt[:],
                        "w0 w1 w2 w3 w4 i0 w5 n0 n1 w6 g0 w7 n2 g1 n3 g2 g3 i1 n4 n5 g4 n6 g5 n7 g6 g7")
            tiles_units()
            coefficients(1, 1, 3, 1, 0)
            weights_of(0, cnt[:])
            nh[0] += 1
            finish(0, True)
            ln(2, x, hnat1)
            ln_lo(2)
            dve.wait_ge(S("arow1_in"), 32)
            dve.wait_ge(S("arow2_in"), 32)
            tiles_natural(8, 1)
            coefficients(2, H2, 2, 2, 1)
            attention_T(2, H2, 2, P, 4, f(cntS[:]), "w0 w1 w2 i0 w3 n0 n1 g0 g1 i1 n2 n3 g2 g3")
            tiles_units()
            coefficients(3, 1, 3, 1, 1)
            weights_of(0, f(cntS[:]))
            nh[0] += 1
            finish(1, True)
            ln(3, x, hnat1)
            ln_lo(3)
            for j in range(3):
                dve.wait_ge(S("gh_hi"), tiles[0] + 1)
                tiles[0] += 1
                for t in range(NT):
                    cs = slice(j * 256, (j + 1) * 256)
                    m = dve.scalar_tensor_tensor(hL[:, t, cs], ps[:, j, t * 256:(t + 1) * 256], dinv[:, t:t + 1],
                                                 f(hH[:, t, cs]), ALU.mult, ALU.subtract)
                m.then_inc(S("gh_lo"), 1)
            finish(2, False)


def kernel(x, src, dst, edge_type_3, L0_gnn_query_embs, L0_gnn_W_rel1, L0_gnn_W_root1, L0_gnn_b1, L0_gnn_W_rel2,
           L0_gnn_W_root2, L0_gnn_b2, L0_gnn_Wg, L0_gnn_bg, L0_gnn_Wq, L0_gnn_bq, L1_gnn_W1, L1_gnn_a_src1,
           L1_gnn_a_dst1, L1_gnn_b1, L1_gnn_W2, L1_gnn_a_src2, L1_gnn_a_dst2, L1_gnn_b2, L2_gnn_W1, L2_gnn_att_src1,
           L2_gnn_att_dst1, L2_gnn_b1, L2_gnn_W2, L2_gnn_att_src2, L2_gnn_att_dst2, L2_gnn_b2, L3_gnn_W, L3_gnn_b):
    import numpy as np
    import concourse.bacc as bacc
    from concourse.bass_utils import run_bass_kernel_spmd

    a = np.asarray

    def blocks(w):
        w = a(w)
        m = w.shape[1] // 256
        return w.reshape(KT, P, m, 256).transpose(2, 1, 0, 3).reshape(m, P, BLK)

    def interleave(p, q):
        return np.stack([p, q], 1).reshape(-1, P, BLK)

    def units(w, rows):
        w = a(w)
        k = w.shape[0] // rows
        v = w.reshape(k, rows, 3, 256).transpose(2, 0, 1, 3).reshape(3 * k // UPB, UPB, rows, 256)
        full = np.zeros((v.shape[0], P, BLK), v.dtype)
        full[:, :rows] = v.transpose(0, 2, 1, 3).reshape(v.shape[0], rows, BLK)
        return full

    wg, wq = a(L0_gnn_Wg).T, a(L0_gnn_Wq).T
    stream = [blocks(wg[D:])]
    for w_rel, w_root in ((L0_gnn_W_rel1, L0_gnn_W_root1), (L0_gnn_W_rel2, L0_gnn_W_root2)):
        stream += [blocks(w) for w in a(w_rel)] + [blocks(w_root), blocks(wg[:D]),
                                                   interleave(blocks(wq[:D]), blocks(wq[D:]))]
    stream += [blocks(L1_gnn_W1), units(L1_gnn_W2, C1), blocks(L2_gnn_W1), units(L2_gnn_W2, P), blocks(L3_gnn_W)]

    bcol = np.zeros((P, 48), np.float32)
    for c0, b in ((0, L0_gnn_b1), (6, L0_gnn_b2), (12, L0_gnn_bg), (18, L0_gnn_bq)):
        bcol[:, c0:c0 + KT] = a(b).reshape(KT, P).T
    bcol[:C1, 24:32] = a(L1_gnn_b1).reshape(H1, C1).T
    bcol[:, 32:48] = a(L2_gnn_b1).reshape(CT2, P).T

    eye32 = np.eye(32, dtype=np.float32)
    node = np.tile(eye32, (1, 32))
    token = np.repeat(eye32, NB, axis=1)
    arrays = {
        "x": a(x),
        "edges": np.stack([a(src), a(dst), a(edge_type_3)]).reshape(3, P, ET),
        "iota": np.tile(np.arange(R * N, dtype=np.float16), (P, 1)),
        "eye": np.eye(N, dtype=np.float32).reshape(NT, P, N).transpose(1, 0, 2),
        "sel": np.concatenate([node, node, token, token]),
        "qT": a(L0_gnn_query_embs).reshape(B * LQ, KT, P).transpose(2, 1, 0),
        "bcol": bcol,
        "weights": np.concatenate(stream),
        "att11": np.stack([a(L1_gnn_a_src1).reshape(-1), a(L1_gnn_a_dst1).reshape(-1)]),
        "att12": np.stack([a(L1_gnn_a_src2).reshape(-1), a(L1_gnn_a_dst2).reshape(-1)]),
        "att21": np.stack([a(L2_gnn_att_src1).reshape(-1), a(L2_gnn_att_dst1).reshape(-1)]),
        "att22": np.stack([a(L2_gnn_att_src2).reshape(-1), a(L2_gnn_att_dst2).reshape(-1)]),
        "brow1": a(L1_gnn_b2), "brow2": a(L2_gnn_b2), "brow3": a(L3_gnn_b),
    }
    arrays = {k: np.ascontiguousarray(v) for k, v in arrays.items()}
    nc = bacc.Bacc("TRN2", target_bir_lowering=False, num_devices=1)
    ins = {k: nc.dram_tensor(f"in_{k}", v.shape, mybir.dt.from_np(v.dtype), kind="ExternalInput").ap()
           for k, v in arrays.items()}
    out = nc.dram_tensor("out", (N, D), F32, kind="ExternalOutput").ap()
    build(nc, ins, out)
    res = run_bass_kernel_spmd(nc, [{f"in_{k}": v for k, v in arrays.items()}], core_ids=[0])
    return res.results[0]["out"]
```

```python
from contextlib import ExitStack

import concourse.bass as bass
from concourse import mybir

F32 = mybir.dt.float32
F32R = mybir.dt.float32r
BF16 = mybir.dt.bfloat16
FP16 = mybir.dt.float16
I32 = mybir.dt.int32
ALU = mybir.AluOpType
ACT = mybir.ActivationFunctionType
AX = mybir.AxisListType

P = 128
N = 256
NT = N // P
D = 768
KT = D // P
R = 3
E = 8192
ET = E // P
B = 8
NB = N // B
LQ = 64
QT = B * LQ // P
EPTSLN = 1e-5
EPTSSM = 1e-16
NO_EDGE = -1e30
SLOPE = 0.2
BLK = 6 * 256

H1, C1 = 8, 96
H2, C2W = 4, 512
CT2 = H2 * C2W // P

RAW, SPL = 4, 3

QG = 0
REL = (3, 24)
ROOT = (12, 33)
HG = (15, 36)
WQ = (18, 39)
G1A, G1B = 45, 48
G2A, G2B = 52, 60
GCN = 68
NBLK = 71
BYCOL = 5
UPB = 6

ES = 3
W_LN, W_AL, W_ALT, W_B, W_BT, W_F, W_AL1, W_B1, W_PT, W_U = (13, 18), 13, 4, (4, 9), (6, 6), 4, 13, 8, 16, 4
LAGR = 2
ZR = 3
PR = 3
ngroups = (0, 2, 3, 5)
PTS = 3
SU = 4
CH = NB * 32
CPB = 2 * KT
GC = 4


def unit_order(k):
    return ([(kt, cb) for kt in range(k - BYCOL) for cb in range(3)] +
            [(kt, cb) for cb in range(3) for kt in range(k - BYCOL, k)])


def build(nc, ins, out):
    ctx = ExitStack()
    with ctx:
        def alloc(stack, name, shape, dt=F32):
            return stack.enter_context(nc.sbuf_tensor(name, shape, dt))

        wraw = alloc(ctx, "wraw", [P, RAW, BLK])
        wH = alloc(ctx, "wH", [P, SPL, BLK], F32R)
        wL = alloc(ctx, "wL", [P, SPL, BLK], F32R)
        eye = alloc(ctx, "eye", [P, NT, N])
        ones = alloc(ctx, "ones", [P, P], F32R)
        cnt = alloc(ctx, "cnt", [P, NT, N])
        cntS = alloc(ctx, "cntS", [P, NT, N], F32R)
        mask = alloc(ctx, "mask", [P, 2, NT, N])
        bcol = alloc(ctx, "bcol", [P, 48])
        dinv = alloc(ctx, "dinv", [P, NT])
        deg = alloc(ctx, "deg", [P, NT])
        stat = alloc(ctx, "stat", [P, NT, 2, 6])
        mv = alloc(ctx, "mv", [P, NT, 2])
        var = alloc(ctx, "var", [P, NT])
        std = alloc(ctx, "std", [P, NT])
        rstd = alloc(ctx, "rstd", [P, NT])
        identity = eye[:, 0, 0:P]
        eyeR = alloc(ctx, "eyeR", [P, P], F32R)
        warm = alloc(ctx, "warm", [P, 2])

        l0 = ctx.enter_context(ExitStack())
        qgH = alloc(l0, "qgH", [P, QT, D], F32R)
        qgL = alloc(l0, "qgL", [P, QT, D], F32R)
        cr = alloc(l0, "cr", [P, NT, R, N], F32R)
        inv = alloc(l0, "inv", [P, R, N])
        sel = alloc(l0, "sel", [P, 2, 512], F32R)
        qT = alloc(l0, "qT", [P, KT, B * LQ])
        hnat0 = alloc(l0, "hnat0", [P, NT, D])
        hs = l0.enter_context(ExitStack())
        hT = [(alloc(hs, "hTH0", [P, KT, N], F32R), alloc(hs, "hTL0", [P, KT, N], F32R))]
        hs.close()
        hgH = alloc(l0, "hgH", [P, NT, D], F32R)
        hgL = alloc(l0, "hgL", [P, NT, D], F32R)
        h32 = hnat0[:, :, :].rearrange("p t (a b) -> p (t a) b", b=N)
        first = l0.enter_context(ExitStack())
        x_in = alloc(first, "x_in", [P, NT, D])
        sel32 = alloc(first, "sel32", [P, 1024])
        qTH = alloc(first, "qTH", [P, KT, B * LQ], F32R)
        qTL = alloc(first, "qTL", [P, KT, B * LQ], F32R)
        iota = alloc(first, "iota", [P, R * N], FP16)
        edge_i = alloc(first, "edge_i", [P, 3, ET], I32)
        edge_f = alloc(first, "edge_f", [P, 3, ET])
        key = alloc(first, "key", [P, ET])
        ohS = alloc(first, "ohS", [P, 4, N], BF16)
        ohD = alloc(first, "ohD", [P, 4, R, N], BF16)
        first.close()
        h2H = alloc(l0, "h2H", [P, KT, N], F32R)
        h2L = alloc(l0, "h2L", [P, KT, N], F32R)
        messages = l0.enter_context(ExitStack())
        msg = alloc(messages, "msg", [P, R, N])
        upd = alloc(messages, "upd", [P, 2, N])
        messages.close()
        qiH = alloc(l0, "qiH", [P, KT, N], F32R)
        qiL = alloc(l0, "qiL", [P, KT, N], F32R)
        rel = l0.enter_context(ExitStack())
        xrH = alloc(rel, "xrH", [P, NT, R * D], F32R)
        xrL = alloc(rel, "xrL", [P, NT, R * D], F32R)
        rel.close()
        gate = l0.enter_context(ExitStack())
        lhs = alloc(gate, "lhs", [P, 2, 2, D], F32R)
        prod = alloc(gate, "prod", [P, PR, CH])
        fold = alloc(gate, "fold", [P, PR, CH // 2])
        th = alloc(gate, "th", [P, KT, N])
        gate.close()
        al32 = prod[:, :, :].rearrange("p a b -> p (a b)")[:, 0:3 * 512].rearrange("p (j n) -> p j n", j=3)
        l0.close()

        gl = ctx.enter_context(ExitStack())
        x = alloc(gl, "x", [P, NT, D])
        brow = alloc(gl, "brow", [P, D])
        gTH = alloc(gl, "gTH", [P, CT2, N], F32R)
        gTL = alloc(gl, "gTL", [P, CT2, N], F32R)
        hH = alloc(gl, "hH", [P, NT, H2 * C2W], F32R)
        hL = alloc(gl, "hL", [P, NT, H2 * C2W], F32R)
        hT.append((alloc(gl, "hTH1", [P, KT, N], F32R), alloc(gl, "hTL1", [P, KT, N], F32R)))
        alp = alloc(gl, "alp", [P, 2, NT, 24])
        al = alloc(gl, "al", [P, 2, NT, 8])
        mx = alloc(gl, "mx", [P, NT, 8])
        xs = alloc(gl, "xs", [P, NT, 8])
        ms = alloc(gl, "ms", [P, NT, 8])
        bb = alloc(gl, "bb", [P, NT, 16])
        zsel = alloc(gl, "zsel", [P, N], F32R)
        aT = tuple(alloc(gl, f"aT{q}", [P, N], F32R) for q in "HL")
        bT = tuple(alloc(gl, f"bT{q}", [P, 2, N], F32R) for q in "HL")
        rzT = tuple(alloc(gl, f"rzT{q}", [P, N], F32R) for q in "HL")
        als2 = alloc(gl, "als2", [P, NT, 8])
        als8 = alloc(gl, "als8", [P, NT, 8])
        z32 = alloc(gl, "z32", [8, N])
        zr = alloc(gl, "zr", [P, NT])
        ys = gl.enter_context(ExitStack())
        arow1 = alloc(ys, "arow1", [P, 2, H2 * C2W])
        ys.close()
        ys = gl.enter_context(ExitStack())
        e = alloc(ys, "e", [P, ES, NT, N])
        ptH = alloc(ys, "ptH", [P, PTS, NT, N], F32R)
        ptL = alloc(ys, "ptL", [P, PTS, NT, N], F32R)
        rz = alloc(ys, "rz", [P, 2, 2, N])
        zs = gl.enter_context(ExitStack())
        hnat1 = alloc(zs, "hnat1", [P, NT, D])
        tmp = alloc(zs, "tmp", [P, 4, 256])
        arow2 = alloc(zs, "arow2", [P, 2, D])
        zs.close()
        u = alloc(gl, "u", [P, SU, 2, N])
        ru = alloc(gl, "ru", [P, SU, 2, N])
        junk = [t[:, a, b, :] for t in (u, ru) for a in range(SU) for b in range(2)]

        ps = ctx.enter_context(nc.psum_tensor("ps", [P, 8, 512], F32))

        def banks(a, n):
            return ps[:, a:a + n, :].rearrange("p a b -> p (a b)")

        def f(ap):
            return ap.bitcast(F32)

        sems = {}
        for name in """warm_ready ld_x ld_eye ld_const ld_sel ld_edge ld_q ld_bcol w_hi w_lo w_used chain achain 
                ln_var ln_std ln_h lnT lnH lnL  oh_ready oh_used  cr_ready cnt_ready
                eyeR_ready zsel_step zsel_ready zero_step ones_ready colsum_mm cntT_mm mask_ready deg_ready sdeg cn_ready qT_ready qg_hi qg_lo
                rel_hi rel_lo root_mm root_sum root_h h2_ready hg_hi hg_lo sel_ready lhs_q lhs_c0 lhs_c1 lhs_c2 lhs_in lhs_in1 z_ready sig_ready mul_ready fold_ready red_done
                qi_ready sum_step sum_hi row_copied arg_ready th_ready alpha_ready hn_ready hn_lo hnT x_res x_ready arow1_in arow2_in brow_in 
                col_done gh_hi gh_free gh_lo al_ready alT_mm alT_ready als_rows b_ready bT_mm bT_ready brow_mm exps_ready
                pt_ready pt_hi pt_lo out_mm out_half zT_mm rzT_ready rz_mm rz_ready u_ready act_u elu_ready gt_ready fin_mm lay_half
                stored""".split():
            sems[name] = ctx.enter_context(nc.semaphore(name))
        w_in = [ctx.enter_context(nc.semaphore(f"w_in{s}")) for s in range(RAW)]

        def S(name):
            return sems[name]

        def out_at(h, nct):
            return h % 4 * 2 + h // 4 if nct == 1 else h % 2 * nct

        def rz_bank(p, both):
            return 7 - p % 2 if both else 7

        def rel_bank(g, j):
            return (j + 2) % 4 if g == 0 else j % 4

        def root_bank(ot):
            return 2 * (ot % 4)

        def ubank(cb):
            return 4 + cb

        def src_natural(bank):
            return ps[:, bank, :].rearrange("p (t w) -> p t w", t=NT)

        def mm3(pe, dst, a, b, start, stop, **kw):
            pe.matmul(dst, a[0], b[0], start=start, stop=False, **kw)
            pe.matmul(dst, a[0], b[1], start=False, stop=False, **kw)
            return pe.matmul(dst, a[1], b[0], start=False, stop=stop, **kw)

        def wblock(i, k, w, p=P):
            s = i % SPL
            return tuple(t[0:p, s, 0:k * w].rearrange("p (k w) -> p k w", k=k) for t in (wH, wL))

        block = ctx.enter_context(nc.Block())

        @block.sync
        def _(sp):
            sp.dma_start(edge_i[:], ins["edges"].rearrange("k p t -> p k t")).then_inc(S("ld_edge"), 16)
            sp.dma_start(iota[:], ins["iota"]).then_inc(S("ld_const"), 16)
            sp.dma_start(x_in[:], ins["x"].rearrange("(t p) d -> p t d", p=P)).then_inc(S("ld_x"), 16)
            sp.dma_start(eye[:], ins["eye"]).then_inc(S("ld_eye"), 16)

            def weights(i0, i1):
                for i in range(i0, i1):
                    if i >= RAW:
                        sp.wait_ge(S("w_lo"), i - RAW + 1)
                    sp.dma_start(wraw[:, i % RAW, :], ins["weights"][i]).then_inc(w_in[i % RAW], 16)

            sp.dma_start(qT[:], ins["qT"]).then_inc(S("ld_q"), 16)
            weights(0, 2)
            sp.dma_start(sel32[:], ins["sel"]).then_inc(S("ld_sel"), 16)
            sp.dma_start(bcol[:], ins["bcol"]).then_inc(S("ld_bcol"), 16)

            def hg_rows(b, par, cols, sem):
                for part, hg in enumerate((hgH, hgL)):
                    n0 = NB * (b % 4)
                    src = f(hg[n0:n0 + NB, b // 4, cols])
                    w = cols.stop - cols.start
                    sp.dma_start(f(lhs[32 * part:32 * part + 32, par, :, cols]),
                                 src.unsqueeze(1).broadcast_to([NB, 2, w])).then_inc(sem, 16)

            def qg_rows(b, par, sem):
                for part, qg in enumerate((qgH, qgL)):
                    for half in range(2):
                        q0 = (b % 2) * LQ + 32 * half
                        sp.dma_start(f(lhs[64 + 32 * part:96 + 32 * part, par, half, :]),
                                     f(qg[q0:q0 + 32, b // 2, :])).then_inc(sem, 16)

            done = 2
            for g in range(2):
                weights(done, HG[g] + 3 + RAW)
                done = HG[g] + 3 + RAW
                sp.wait_ge(S("qg_lo"), 3)
                qg_rows(0, 0, S("lhs_q"))
                for j in range(3):
                    sp.wait_ge(S("hg_lo"), 3 * g + j + 1)
                    hg_rows(0, 0, slice(j * 256, (j + 1) * 256), S(f"lhs_c{j}"))
                for b in range(1, B):
                    if b >= 2:
                        sp.wait_ge(S("z_ready"), g * B * CPB + CPB * (b - 1))
                    sem = S("lhs_in1") if b % 2 else S("lhs_in")
                    hg_rows(b, b % 2, slice(0, D), sem)
                    qg_rows(b, b % 2, sem)
            sp.wait_ge(S("z_ready"), 2 * B * CPB)
            sp.dma_start(x[:], ins["x"].rearrange("(t p) d -> p t d", p=P)).then_inc(S("x_res"), 16)
            weights(done, NBLK)
            for t in range(NT):
                sp.wait_ge(S("lay_half"), 2 * 2 + t + 1)
                sp.dma_start(out[t * P:(t + 1) * P, :], x[:, t, :]).then_inc(S("stored"), 16)
            sp.wait_ge(S("stored"), 16 * NT)

        @block.tensor
        def _(pe):
            def w_wait(i):
                pe.wait_ge(S("w_lo"), i + 1)

            def transposes(k):
                src = hnat0 if k == 0 else hnat1
                if k:
                    keep_warm(W_LN[k > 1], 5)
                dst = banks(0, 3).rearrange("p (k n) -> p k n", k=KT)
                for t in range(NT):
                    pe.wait_ge(S("ln_h"), 2 * k + t + 1)
                    for kt in range(KT):
                        m = pe.transpose(dst[:, kt, t * P:(t + 1) * P], src[:, t, kt * P:(kt + 1) * P], identity)
                        if t == 1 and kt % 2:
                            m.then_inc(S("lnT"), 1)

            def keep_warm(n, bank):
                for _ in range(n):
                    pe.matmul(ps[:, bank, :], ones[:], cntS[:, :, :].rearrange("p t n -> p (t n)"),
                              start=True, stop=True)

            def natural(i, bank, a, fresh=None):
                w_wait(i)
                wb = wblock(i, KT, 256)
                pairs = [(t, kt) for t in range(NT) for kt in range(KT)]
                if fresh:
                    pairs.sort(key=lambda p: (p[1] // 2, p))
                for n, (t, kt) in enumerate(pairs):
                    if fresh and n % 4 == 0:
                        pe.wait_ge(S(fresh[0]), fresh[1] + n // 4 + 1)
                    m = mm3(pe, ps[:, bank, t * 256:(t + 1) * 256],
                            tuple(h[:, kt, t * P:(t + 1) * P] for h in a), tuple(q[:, kt, :] for q in wb),
                            n == 0 or (kt == 0 and not fresh), kt == KT - 1, skip_group_check=bool(fresh))
                m.then_inc(S("w_used"), 1)

            def natural_units(i0, k, kp, steps0, pairs):
                keep_warm(W_U, 4)
                seen = 0
                pe.wait_ge(S("rz_ready"), pairs)
                for n, (kt, cb) in enumerate(unit_order(k)):
                    i = i0 + n // UPB
                    if n % UPB == 0:
                        w_wait(i)
                    if kt // 2 >= seen:
                        pe.wait_ge(S("gt_ready"), steps0 + kt // 2 + 1)
                        seen = kt // 2 + 1
                    wb = wblock(i, UPB, 256, kp)
                    for t in range(NT):
                        m = mm3(pe, ps[:, ubank(cb), t * 256:(t + 1) * 256],
                                tuple(h[0:kp, kt, t * P:(t + 1) * P] for h in (gTH, gTL)),
                                tuple(q[:, n % UPB, :] for q in wb), kt == 0 and t == 0, kt == k - 1, skip_group_check=True)
                    if n % UPB == UPB - 1:
                        m.then_inc(S("w_used"), 1)
                    elif kt == k - 1:
                        m.then_inc(S("col_done"), 1)

            def count_tile(t, k, start, stop):
                pe.wait_ge(S("oh_ready"), t + 1)
                oh = ohD[:, k, :, :].rearrange("p r n -> p (r n)")
                for st in range(NT):
                    s = ohS[:, k, st * P:(st + 1) * P]
                    pe.matmul(ps[:, 4 + 2 * st, :], s, oh[:, 0:512], start=start, stop=stop)
                    m = pe.matmul(ps[:, 5 + 2 * st, 0:256], s, oh[:, 512:768], start=start, stop=stop)
                m.then_inc(S("oh_used"), 1)

            for k in range(4):
                count_tile(k, k, k == 0, False)
            with pe.Fori(1, ET // 8 + 1) as g:
                for k in range(4):
                    count_tile(g * 4 + k, k, False, False)
            pe.wait_ge(S("ld_eye"), 16)
            transposes(0)
            with pe.Fori(ET // 8 + 1, ET // 4 - 1) as g:
                for k in range(4):
                    count_tile(g * 4 + k, k, False, False)
            for k in range(4):
                count_tile(ET - 4 + k, k, False, k == 3)

            pe.wait_ge(S("lnL"), 3)
            pe.wait_ge(S("qT_ready"), 2)
            for j in range(3):
                i = QG + j
                w_wait(i)
                if j >= 2:
                    pe.wait_ge(S("qg_lo"), j - 1)
                wb = wblock(i, KT, 256)
                for rt in range(QT):
                    for kt in range(KT):
                        m = mm3(pe, ps[:, 2 * (j % 2) + rt // 2, (rt % 2) * 256:(rt % 2) * 256 + 256],
                                (qTH[:, kt, rt * P:(rt + 1) * P], qTL[:, kt, rt * P:(rt + 1) * P]),
                                tuple(q[:, kt, :] for q in wb), kt == 0, kt == KT - 1)
                m.then_inc(S("w_used"), 1)
                if j == 0:
                    pe.wait_ge(S("cnt_ready"), 4)
                    pe.wait_ge(S("cr_ready"), 1)
                    pe.wait_ge(S("ones_ready"), 1)
                    for st in range(NT):
                        c = cr[:, st, :, :].rearrange("p r n -> p (r n)")
                        pe.matmul(ps[:, 4, :], ones[:], c[:, 0:512], start=st == 0, stop=st == 1)
                        m = pe.matmul(ps[:, 5, 0:256], ones[:], c[:, 512:768], start=st == 0, stop=st == 1)
                    m.then_inc(S("colsum_mm"), 1)
                    for st in range(NT):
                        for dt in range(NT):
                            m = pe.transpose(ps[:, 6, dt * N + st * P:dt * N + (st + 1) * P],
                                             cnt[:, st, dt * P:(dt + 1) * P], identity)
                    m.then_inc(S("cntT_mm"), 1)

            for g in range(2):
                ht = hT[0]
                for j in range(9):
                    if g == 0 and j in (0, 2):
                        pe.wait_ge(S("qg_lo"), 2 + j // 2)
                    if j >= 4:
                        pe.wait_ge(S("rel_lo"), 9 * g + j - 3)
                    natural(REL[g] + j, rel_bank(g, j), ht, ("hn_lo", 0) if g and j == 0 else None)
                pe.wait_ge(S("rel_lo"), 9 * (g + 1))
                for j in range(3):
                    i = ROOT[g] + j
                    w_wait(i)
                    wb = wblock(i, KT, 256)
                    for o in range(2):
                        ot = 2 * j + o
                        if ot >= 4:
                            pe.wait_ge(S("root_sum"), KT * g + ot - 3)
                        dst = banks(root_bank(ot), 2)
                        for r in range(R):
                            for st in range(NT):
                                c0 = r * D + ot * P
                                for k, xr in enumerate((xrH, xrL)):
                                    pe.matmul(dst[:, r * N:(r + 1) * N], xr[:, st, c0:c0 + P], cr[:, st, r, :],
                                              start=st == 0 and k == 0, stop=st == NT - 1 and k == 1)
                        for kt in range(KT):
                            m = mm3(pe, dst[:, R * N:(R + 1) * N], tuple(q[:, kt, o * P:(o + 1) * P] for q in wb),
                                    tuple(h[:, kt, :] for h in ht), kt == 0, kt == KT - 1)
                        m.then_inc(S("root_mm" if o == 0 else "w_used"), 1)
                pe.wait_ge(S("h2_ready"), 3 * g + 2)
                for j in range(3):
                    natural(HG[g] + j, 4 + j, (h2H, h2L), None if j else ("h2_ready", 3 * g))

                base = g * B * CPB
                pe.wait_ge(S("sel_ready"), 1)

                def args(c, k, ring):
                    if ring:
                        pe.wait_ge(S("mul_ready"), c - ZR + 1)
                    par, ft, half = k // CPB, (k % CPB) // 2, k % 2
                    for h in range(2):
                        m = pe.matmul(ps[:, 2 * (k % ZR) + h, :], lhs[:, par, half, ft * P:(ft + 1) * P],
                                      sel[:, h, :], start=True, stop=True)
                    m.then_inc(S("z_ready"), 1)

                def reduce(c, k):
                    ft, half = (k % CPB) // 2, k % 2
                    pe.wait_ge(S("fold_ready"), c + 1)
                    for s in range(2):
                        m = pe.matmul(ps[:, 6 + k // GC % 2, ft % 2 * 256:ft % 2 * 256 + 256], identity,
                                      fold[:, k % PR, s * 256:(s + 1) * 256],
                                      start=half == 0 and s == 0, stop=half == 1 and s == 1)
                    m.then_inc(S("red_done"), 1)

                def pair(c0, b0, pairs, first_pair, last_pair):
                    for k in range(2 * CPB):
                        n = k + ZR
                        if n == CPB:
                            pe.wait_ge(S("lhs_in1"), lhs_count(pairs + 1))
                        if n == 2 * CPB and not last_pair:
                            pe.wait_ge(S("lhs_in"), lhs_count(pairs + (1 - g)))
                        if first_pair and n in (4, 8):
                            pe.wait_ge(S(f"lhs_c{n // 4}"), 32 * (g + 1))
                        if n < 2 * CPB or not last_pair:
                            args(c0 + n, n % (2 * CPB), True)
                        r = k - LAGR
                        if r >= 0 or not first_pair:
                            if r % GC == 0 and (r >= 2 * GC or not (first_pair and g == 0)):
                                pe.wait_ge(S("qi_ready"), b0 * 3 + (r // GC - 1))
                            reduce(c0 + r, r % (2 * CPB))

                def lhs_count(i):
                    return i * 96

                pe.wait_ge(S("lhs_q"), 64 * (g + 1))
                pe.wait_ge(S("lhs_c0"), 32 * (g + 1))
                for c in range(ZR):
                    if c == 2:
                        pe.wait_ge(S("hg_lo"), 3 * g + 2)
                    args(base + c, c, False)
                pe.wait_ge(S("hg_lo"), 3 * (g + 1))
                pair(base, g * B, 4 * g, True, False)
                with pe.Fori(1, B // 2 - 1) as bp:
                    pair(bp * (2 * CPB) + base, bp * 2 + g * B, bp + 4 * g, False, False)
                pair(base + 6 * CPB, g * B + 6, 4 * g + 3, False, True)
                for r in range(2 * CPB - LAGR, 2 * CPB):
                    reduce(base + 6 * CPB + r, r)

                for j in range(3):
                    for half, b_pair in enumerate(((h2H, h2L), (qiH, qiL))):
                        i = WQ[g] + 2 * j + half
                        w_wait(i)
                        if j == 0 and half == 1:
                            pe.wait_ge(S("qi_ready"), 3 * B * (g + 1))
                        wb = wblock(i, KT, 256)
                        for o in range(2):
                            for kt in range(KT):
                                m = mm3(pe, ps[:, 2 * j + o, 0:N], tuple(q[:, kt, o * P:(o + 1) * P] for q in wb),
                                        tuple(h[:, kt, :] for h in b_pair), half == 0 and kt == 0,
                                        half == 1 and kt == KT - 1)
                        m.then_inc(S("w_used"), 1)

            pe.wait_ge(S("hn_ready"), 6)
            for t in range(NT):
                for kt in range(KT):
                    m = pe.transpose(ps[:, 2 * t + kt // 3, (kt % 3) * P:(kt % 3 + 1) * P],
                                     th[:, kt, t * P:(t + 1) * P], identity)
                m.then_inc(S("hnT"), 1)

            nh = [0]

            def row(dst, pair_, k):
                one = eyeR[:, k:k + 1].broadcast_to([P, P])
                pe.matmul(dst, one, pair_[0], start=True, stop=False)
                return pe.matmul(dst, one, pair_[1], start=False, stop=True)

            def attention_T(a, heads, gs, zg, cw, nct, done, order):
                heads0, steps0, pairs0, inv0 = done
                keep_warm(W_AL, 5)
                pe.wait_ge(S("al_ready"), a + 1)
                for t in range(NT):
                    m = pe.transpose(ps[0:heads, 6, t * P:(t + 1) * P], al[:, 0, t, 0:heads], identity)
                m.then_inc(S("alT_mm"), 1)
                keep_warm(W_ALT, 5)
                pe.wait_ge(S("alT_ready"), a // 2 + 1)
                pe.wait_ge(S("eyeR_ready"), 1)
                for h in range(heads):
                    m = row(ps[:, h // 2, (h % 2) * N:(h % 2 + 1) * N], tuple(q[:] for q in aT), h)
                    if h % 2:
                        m.then_inc(S("als_rows"), 1)
                for q in range(2):
                    keep_warm(W_B[q], 5 + 2 * q)
                    pe.wait_ge(S("b_ready"), ngroups[a] + q + 1)
                    for t in range(NT):
                        dst = ps[0:2 * gs, 6 + q, (1 - q) * N + t * P:(1 - q) * N + (t + 1) * P]
                        m = pe.transpose(dst, bb[:, t, 2 * gs * q:2 * gs * (q + 1)], identity)
                    m.then_inc(S("bT_mm"), 1)
                    keep_warm(W_BT[q], 5 + q)
                    if q == 0:
                        for h in range(2):
                            drows(a, h, gs)

                def sums(h):
                    q = h // zg
                    pe.wait_ge(S("pt_lo"), nh[0] + h + 1)
                    first_h, last_h = h % zg == 0, h % zg == zg - 1
                    for st in range(NT):
                        for k, w in enumerate((ptH, ptL)):
                            m = pe.matmul(ps[:, 6, q * N:(q + 1) * N], zsel[:, P - h:2 * P - h], w[:, h % PTS, st, :],
                                          start=first_h and st == 0 and k == 0,
                                          stop=last_h and st == NT - 1 and k == 1, skip_group_check=True)
                    if last_h:
                        m.then_inc(S("zT_mm"), 1)

                def outputs(h):
                    s = h % PTS
                    if h >= zg:
                        pe.wait_ge(S("u_ready"), steps0 + (h - zg + 1) * nct // 2)
                    for ct in range(nct):
                        c0 = (h * nct + ct) * cw
                        at = out_at(h, nct) + ct
                        dst = ps[0:cw, at // 2, (at % 2) * N:(at % 2 + 1) * N]
                        for st in range(NT):
                            m = mm3(pe, dst, (hH[:, st, c0:c0 + cw], hL[:, st, c0:c0 + cw]),
                                    (ptH[:, s, st, :], ptL[:, s, st, :]), st == 0, st == NT - 1)
                        if nct == 4 and ct == 1:
                            m.then_inc(S("out_half"), 1)
                    m.then_inc(S("out_mm"), 1)

                def rzrow(p):
                    pe.wait_ge(S("rzT_ready"), inv0 + 2 * p // zg + 1)
                    step_ = 2 if zg == heads else 1
                    if p >= step_:
                        pe.wait_ge(S("rz_ready"), pairs0 + p - step_ + 1)
                    for k in range(2):
                        m = row(ps[:, rz_bank(p, zg == heads), k * N:(k + 1) * N], tuple(w[:] for w in rzT), 2 * p + k)
                    m.then_inc(S("rz_mm"), 1)

                for step in order.split():
                    k = int(step[1])
                    if step[0] == "d":
                        drows(a, k, gs)
                    elif step[0] == "f":
                        keep_warm(W_F, k)
                    else:
                        {"s": sums, "o": outputs, "z": rzrow}[step[0]](k)
                nh[0] += heads

            def drows(a, h, gs):
                q = h // gs
                pe.wait_ge(S("bT_ready"), 2 * (a // 2) + q + 1)
                if h >= 2:
                    pe.wait_ge(S("arg_ready"), nh[0] + h - 1)
                for v in range(2):
                    m = row(ps[:, 4 + h % 2, v * N:(v + 1) * N], tuple(w[:, q, :] for w in bT), v * gs + h % gs)
                m.then_inc(S("brow_mm"), 1)

            def attention_1(a):
                keep_warm(W_AL1, 7)
                pe.wait_ge(S("al_ready"), a + 1)
                for t in range(NT):
                    m = pe.matmul(ps[:, 0, t * P:(t + 1) * P], al[:, 0, t, 0:1].broadcast_to([P, P]), identity,
                                  start=True, stop=True)
                m.then_inc(S("als_rows"), 1)
                keep_warm(W_B1, 7)
                pe.wait_ge(S("b_ready"), ngroups[a] + 1)
                for v in range(2):
                    for t in range(NT):
                        m = pe.matmul(ps[:, 7, v * N + t * P:v * N + (t + 1) * P],
                                      bb[:, t, v:v + 1].broadcast_to([P, P]), identity, start=True, stop=True)
                m.then_inc(S("brow_mm"), 1)
                keep_warm(W_PT, 5)
                pe.wait_ge(S("pt_lo"), nh[0] + 1)
                for dt in range(NT):
                    for fc in range(2):
                        w = 384 + 2 * fc
                        for st in range(NT):
                            q = ptH[:, 0, st, dt * P:(dt + 1) * P], ptL[:, 0, st, dt * P:(dt + 1) * P]
                            m = mm3(pe, ps[:, 2 * dt + fc, 0:w], q,
                                    (hH[:, st, fc * 384:fc * 384 + w], hL[:, st, fc * 384:fc * 384 + w]),
                                    st == 0, st == NT - 1)
                    m.then_inc(S("fin_mm"), 1)
                nh[0] += 1

            transposes(1)
            for j in range(3):
                natural(G1A + j, j, hT[1], None if j else ("lnL", 3))
            pe.wait_ge(S("zsel_ready"), 1)
            attention_T(0, H1, 4, H1, C1, 1, (0, 0, 0, 0),
                        "d2 f0 d3 f0 f0 s0 o0 f1 d4 s1 o1 f2 d5 s2 o2 f3 d6 s3 o3 d7 s4 o4 s5 o5 s6 o6 s7 o7 "
                        "f4 f4 f4 z0 z1 f4 z2 f4 f4 z3 f4 f4")
            natural_units(G1B, H1, C1, 0, H1 // 2)
            attention_1(1)
            transposes(2)
            for j in range(8):
                if j >= 4:
                    pe.wait_ge(S("gh_free"), 6 + j - 3)
                natural(G2A + j, j % 4, hT[1], None if j else ("lnL", 6))
            attention_T(2, H2, 2, 2, P, 4, (H1, H1 // 2, H1 // 2, 1),
                        "d2 f0 d3 f0 s0 f0 s1 o0 z0 s2 o1 s3 o2 z1 o3")
            natural_units(G2B, CT2, P, H1 // 2, (H1 + H2) // 2)
            attention_1(3)
            transposes(3)
            for j in range(3):
                natural(GCN + j, j, hT[1], None if j else ("lnL", 9))
            pe.wait_ge(S("gh_lo"), 3)
            for dt in range(NT):
                for fc in range(2):
                    for st in range(NT):
                        c = cntS[:, st, dt * P:(dt + 1) * P]
                        for k, h in enumerate((hH, hL)):
                            m = pe.matmul(ps[:, 4 + 2 * dt + fc, 0:384], c, h[:, st, fc * 384:fc * 384 + 384],
                                          start=st == 0 and k == 0, stop=st == NT - 1 and k == 1)
                m.then_inc(S("fin_mm"), 1)

        @block.scalar
        def _(act):
            def split_hi(i):
                if i >= NBLK or i < split_next[0]:
                    return
                split_next[0] = i + 1
                act.wait_ge(w_in[i % RAW], 16 * (i // RAW + 1))
                if i >= SPL:
                    act.wait_ge(S("w_used"), i - SPL + 1)
                act.copy(wH[:, i % SPL, :], wraw[:, i % RAW, :]).then_inc(S("w_hi"), 1)

            split_next = [0]

            def table(func):
                act.activation(warm[:, 1:2], warm[:, 0:1], func).then_inc(S("achain"), 1)
                tables[0] += 1
                act.wait_ge(S("achain"), tables[0])

            tables = [0]

            def ln(k):
                for t in range(NT):
                    act.wait_ge(S("ln_var"), 2 * k + t + 1)
                    act.sqrt(std[:, t:t + 1], var[:, t:t + 1]).then_inc(S("ln_std"), 1)

            def ln_relu(k):
                for j in range(3):
                    act.wait_ge(S("lnT"), 3 * k + j + 1)
                    act.activation(hT[min(k, 1)][0][:, 2 * j:2 * j + 2, :].rearrange("p k n -> p (k n)"), ps[:, j, :],
                                   ACT.Relu).then_inc(S("lnH"), 1)

            act.wait_ge(S("warm_ready"), 1)
            act.wait_ge(S("ld_q"), 16)
            act.copy(qTH[:], qT[:]).then_inc(S("qT_ready"), 1)
            split_hi(0)
            split_hi(1)
            split_hi(2)
            table(ACT.Sqrt)
            ln(0)
            ln_relu(0)
            for j in range(3):
                act.wait_ge(S("w_used"), QG + j + 1)
                act.copy(qgH[:, :, j * 256:(j + 1) * 256],
                         banks(2 * (j % 2), 2).rearrange("p (a b) -> p a b", b=256)).then_inc(S("qg_hi"), 1)
                split_hi(QG + j + 3)
            for g in range(2):
                for j in range(9):
                    if g == 0 and j == 7:
                        act.wait_ge(S("deg_ready"), 1)
                        act.sqrt(dinv[:], deg[:]).then_inc(S("sdeg"), 1)
                    act.wait_ge(S("w_used"), REL[g] + j + 1)
                    act.copy(xrH[:, :, j * 256:(j + 1) * 256],
                             src_natural(rel_bank(g, j))).then_inc(S("rel_hi"), 1)
                    split_hi(REL[g] + j + 3)
                act.wait_ge(S("ld_bcol"), 16)
                for j in range(3):
                    for o in range(2):
                        ot = 2 * j + o
                        act.wait_ge(S("root_sum"), KT * g + ot + 1)
                        act.activation(h32[:, ot, :], upd[:, o, :], ACT.Relu,
                                       bias=bcol[:, KT * g + ot:KT * g + ot + 1]).then_inc(S("root_h"), 1)
                    split_hi(ROOT[g] + j + 3)
                table(ACT.Sigmoid)
                for j in range(3):
                    act.wait_ge(S("w_used"), HG[g] + j + 1)
                    act.copy(hgH[:, :, j * 256:(j + 1) * 256],
                             ps[:, 4 + j, :].rearrange("p (t w) -> p t w", t=NT)).then_inc(S("hg_hi"), 1)
                    split_hi(HG[g] + j + 3)
                base = g * B * CPB

                with act.Fori(0, B) as b:
                    for k in range(CPB):
                        c = b * CPB + (base + k)
                        ft = k // 2
                        act.wait_ge(S("z_ready"), c + 1)
                        z = banks(2 * (k % ZR), 2)
                        act.activation(z, z, ACT.Sigmoid, bias=bcol[:, 12 + ft:13 + ft]).then_inc(S("sig_ready"), 1)
                act.wait_ge(S("qi_ready"), 3 * B * (g + 1))
                act.activation(th[:, :, :], th[:, :, :], ACT.Tanh).then_inc(S("th_ready"), 1)
                for j in range(3):
                    act.wait_ge(S("w_used"), WQ[g] + 2 * j + 1)
                    split_hi(WQ[g] + 2 * j + 3)
                    act.wait_ge(S("w_used"), WQ[g] + 2 * j + 2)
                    for o in range(2):
                        ot = 2 * j + o
                        act.activation(al32[:, j, o * N:(o + 1) * N], ps[:, 2 * j + o, 0:N], ACT.Sigmoid,
                                       bias=bcol[:, 18 + ot:19 + ot]).then_inc(S("alpha_ready"), 1)
                    split_hi(WQ[g] + 2 * j + 4)

            nh = [0]

            def tile_hi(src, cols):
                act.copy(hH[:, :, cols:cols + 256], src).then_inc(S("gh_hi"), 1)

            def tiles_natural(i0, n):
                for j in range(n):
                    act.wait_ge(S("w_used"), i0 + j + 1)
                    tile_hi(ps[:, j % 4, :].rearrange("p (t w) -> p t w", t=NT), j * 256)
                    split_hi(i0 + j + 3)

            def tiles_units(i0, k, cols_done):
                nblk = 3 * k // UPB
                ends = [n // UPB for n, (kt, cb) in enumerate(unit_order(k)) if kt == k - 1]
                for j in range(nblk):
                    for cb in range(3):
                        if ends[cb] == j and cb < 2:
                            act.wait_ge(S("col_done"), cols_done + cb + 1)
                            tile_hi(src_natural(ubank(cb)), cb * 256)
                    act.wait_ge(S("w_used"), i0 + j + 1)
                    if j == nblk - 1:
                        tile_hi(src_natural(ubank(2)), 512)
                    split_hi(i0 + j + 3)

            def row_copy(h, bank):
                act.wait_ge(S("brow_mm"), nh[0] + h + 1)
                if h >= ES:
                    act.wait_ge(S("pt_lo"), nh[0] + h - ES + 1)
                act.copy(e[:, h % ES, 1, :], ps[:, bank, N:2 * N]).then_inc(S("row_copied"), 1)

            def exps(h):
                act.wait_ge(S("arg_ready"), nh[0] + h + 1)
                s = h % ES
                for st in range(NT):
                    m = act.activation(e[:, s, st, :], e[:, s, st, :], ACT.Exp, bias=als2[:, st, h:h + 1])
                m.then_inc(S("exps_ready"), 1)

            def pt_high(h, used=None):
                act.wait_ge(S("pt_ready"), nh[0] + h + 1)
                if used is not None:
                    act.wait_ge(S("out_mm"), used)
                act.copy(ptH[:, h % PTS, :, :], e[:, h % ES, :, :]).then_inc(S("pt_hi"), 1)

            def attention_T(heads, both, cw, b0, done, i0, order):
                heads0, steps0, pairs0, inv0 = done

                def rz_copy(p):
                    act.wait_ge(S("rz_mm"), pairs0 + p + 1)
                    if p >= 2:
                        act.wait_ge(S("u_ready"), steps0 + p - 1)
                    act.copy(rz[:, p % 2, :, :].rearrange("p k n -> p (k n)"),
                             ps[:, rz_bank(p, both), :]).then_inc(S("rz_ready"), 1)

                def branches(p):
                    s = p % SU
                    act.wait_ge(S("u_ready"), steps0 + p + 1)
                    if p >= SU:
                        act.wait_ge(S("gt_ready"), steps0 + p - SU + 1)
                    for ct in range(2):
                        bias = bcol[0:cw, b0 + 2 * p + ct:b0 + 2 * p + ct + 1]
                        act.activation(ru[0:cw, s, ct, :], u[0:cw, s, ct, :], ACT.Relu, bias=bias)
                        m = act.activation(u[0:cw, s, ct, :], u[0:cw, s, ct, :], ACT.Exp, bias=bias)
                    m.then_inc(S("act_u"), 1)

                table(ACT.Exp)
                for step in order.split():
                    k = int(step[1])
                    if step[0] == "c":
                        pt_high(k, heads0 + k - PTS + 1 if k >= PTS else None)
                    else:
                        {"r": lambda h: row_copy(h, 4 + h % 2), "W": lambda j: split_hi(i0 + j), "e": exps, "z": rz_copy, "b": branches}[step[0]](k)
                nh[0] += heads

            def attention_1():
                table(ACT.Exp)
                row_copy(0, 7)
                exps(0)
                nh[0] += 1

            def load_att1(att):
                n = att.shape[1]
                act.dma_start(arow1[:, :, 0:n], att.partition_broadcast(P)).then_inc(S("arow1_in"), 16)

            def load_att2(att, steps_done):
                act.wait_ge(S("gt_ready"), steps_done)
                act.dma_start(arow2[:], att.partition_broadcast(P)).then_inc(S("arow2_in"), 16)

            def load_bias(bias):
                act.dma_start(brow[:], bias.partition_broadcast(P)).then_inc(S("brow_in"), 16)

            table(ACT.Sqrt)
            act.wait_ge(S("x_ready"), 2)
            load_att1(ins["att11"])
            load_bias(ins["brow1"])
            ln(1)
            ln_relu(1)
            tiles_natural(G1A, 3)
            attention_T(H1, True, C1, 24, (0, 0, 0, 0), G1B,
                        "r0 r1 e0 r2 e1 c0 r3 c1 e2 e3 r4 c2 e4 r5 c3 e5 r6 c4 e6 r7 c5 e7 c6 c7 "
                        "z0 z1 z2 b0 z3 b1 b2 b3 W3")
            load_att2(ins["att12"], H1 // 2)
            tiles_units(G1B, H1, 0)
            attention_1()
            table(ACT.Sqrt)
            act.wait_ge(S("fin_mm"), 2)
            load_att1(ins["att21"])
            ln(2)
            act.wait_ge(S("lay_half"), 2)
            load_bias(ins["brow2"])
            ln_relu(2)
            tiles_natural(G2A, 8)
            attention_T(H2, False, P, 32, (H1, H1 // 2, H1 // 2, 1), G2B,
                        "r0 r1 e0 r2 e1 c0 c1 r3 e2 c2 e3 c3 z0 b0 b1 b2 b3 z1 b4 b5 W3 b6 b7 W4 W5")
            load_att2(ins["att22"], H1 // 2 + CT2 // 2)
            tiles_units(G2B, CT2, 2)
            attention_1()
            table(ACT.Sqrt)
            ln(3)
            act.wait_ge(S("lay_half"), 4)
            load_bias(ins["brow3"])
            ln_relu(3)
            for j in range(3):
                act.wait_ge(S("w_used"), GCN + j + 1)
                for t in range(NT):
                    m = act.activation(hH[:, t, j * 256:(j + 1) * 256], ps[:, j, t * 256:(t + 1) * 256], ACT.Copy,
                                       scale=dinv[:, t:t + 1])
                m.then_inc(S("gh_hi"), 1)

        @block.gpsimd
        def _(pool):
            def split_lo(i):
                if i >= NBLK:
                    return
                pool.wait_ge(S("w_hi"), i + 1)
                pool.tensor_tensor(wL[:, i % SPL, :], wraw[:, i % RAW, :], f(wH[:, i % SPL, :]), ALU.subtract)\
                    .then_inc(S("w_lo"), 1)

            pool.wait_ge(S("qT_ready"), 1)
            pool.tensor_tensor(qTL[:], qT[:], f(qTH[:]), ALU.subtract).then_inc(S("qT_ready"), 1)
            for i in range(0, HG[0] + 5):
                split_lo(i)
            for g in range(2):
                base = g * B * CPB
                if g:
                    for i in range(HG[0] + 5, HG[1] + 5):
                        split_lo(i)

                def folds(c, k, wait):
                    pool.wait_ge(S("mul_ready"), c + 1)
                    if wait:
                        pool.wait_ge(S("red_done"), c - PR + 1)
                    s = k % PR
                    pool.tensor_tensor(fold[:, s, :], prod[:, s, 0:CH // 2], prod[:, s, CH // 2:CH], ALU.add)\
                        .then_inc(S("fold_ready"), 1)

                for k in range(CPB):
                    folds(base + k, k, k >= PR)
                with pool.Fori(1, B) as b:
                    for k in range(CPB):
                        folds(b * CPB + (base + k), k, True)
            def pt_low(k, h):
                s = h % PTS
                pool.wait_ge(S("pt_hi"), k + 1)
                pool.tensor_tensor(ptL[:, s, :, :], e[:, h % ES, :, :], f(ptH[:, s, :, :]), ALU.subtract)\
                    .then_inc(S("pt_lo"), 1)

            def gt_low(p, cw, steps0):
                pool.wait_ge(S("elu_ready"), steps0 + p + 1)
                o = slice(2 * p, 2 * p + 2)
                pool.tensor_tensor(gTL[0:cw, o, :], ru[0:cw, p % SU, :, :], f(gTH[0:cw, o, :]), ALU.subtract)\
                    .then_inc(S("gt_ready"), 1)

            def attention_T(k0, cw, steps0, i0, order):
                for step in order.split():
                    k = int(step[1])
                    if step[0] == "p":
                        pt_low(k0 + k, k)
                    elif step[0] == "W":
                        split_lo(i0 + k)
                    else:
                        gt_low(k, cw, steps0)

            for i in range(HG[1] + 5, G1A + 3):
                split_lo(i)
            pool.wait_ge(S("x_ready"), 2)
            pool.memset(f(gTH[:, 2:4, :]), 0.0).then_inc(S("zero_step"), 1)
            pool.wait_ge(S("zero_step"), 1)
            zeros = f(gTH[:, 2:4, :])
            for pair_ in (bT, aT, rzT):
                for w in pair_:
                    m = pool.tensor_copy(w[:], zeros if pair_ is bT else zeros[:, 0, :])
            m.then_inc(S("zero_step"), 1)
            pool.tensor_copy(zsel[:], zeros[:, 0, :]).then_inc(S("zsel_step"), 1)
            pool.wait_ge(S("zsel_step"), 1)
            pool.tensor_copy(zsel[:, P:P + 1], warm[:, 0:1]).then_inc(S("zsel_ready"), 1)
            for i in range(G1A + 3, G1A + 6):
                split_lo(i)
            attention_T(0, C1, 0, G1B, "p0 p1 p2 p3 p4 p5 p6 p7 g0 g1 g2 g3")
            for i in range(G1A + 6, G2A + 3):
                split_lo(i)
            for i in range(G2A + 3, G2B + 3):
                split_lo(i)
            attention_T(H1 + 1, P, H1 // 2, G2B, "p0 p1 p2 p3 g0 g1 g2 g3 W3 g4 g5 W4 g6 g7 W5")
            for i in range(G2B + 6, NBLK):
                split_lo(i)

        @block.vector
        def _(dve):
            steps = [0]

            def link(ins_):
                steps[0] += 1
                ins_.then_inc(S("chain"), 1)
                dve.wait_ge(S("chain"), steps[0])

            def ln_stats(k, t, src):
                for j in range(2):
                    m = dve.bn_stats(stat[:, t, j, :], src[:, t, 384 * j:384 * j + 384])
                link(m)
                link(dve.bn_aggr(mv[:, t, :], stat[:, t, :, :]))
                dve.tensor_scalar(var[:, t:t + 1], mv[:, t, 1:2], EPTSLN, None, ALU.add).then_inc(S("ln_var"), 1)

            def ln_norm(k, t, src, dst):
                dve.wait_ge(S("ln_std"), 2 * k + t + 1)
                link(dve.reciprocal(rstd[:, t:t + 1], std[:, t:t + 1]))
                dve.tensor_scalar(dst[:, t, :], src[:, t, :], mv[:, t, 0:1], rstd[:, t:t + 1],
                                  ALU.subtract, ALU.mult).then_inc(S("ln_h"), 1)

            def ln_lo(k):
                for j in range(3):
                    dve.wait_ge(S("lnH"), 3 * k + j + 1)
                    hh, hl = (t[:, 2 * j:2 * j + 2, :].rearrange("p k n -> p (k n)") for t in hT[min(k, 1)])
                    dve.scalar_tensor_tensor(hl, ps[:, j, :], 0.0, f(hh), ALU.max, ALU.subtract)\
                       .then_inc(S("lnL"), 1)

            def split(dst, src, hi_sem=None, lo_sem=None):
                link(dve.tensor_copy(dst[0], src))
                return dve.tensor_tensor(dst[1], src, f(dst[0]), ALU.subtract)

            dve.memset(warm[:], 1.0).then_inc(S("warm_ready"), 1)
            dve.wait_ge(S("ld_edge"), 16)
            link(dve.tensor_copy(edge_f[:], edge_i[:]))
            link(dve.scalar_tensor_tensor(key[:], edge_f[:, 2, :], float(N), edge_f[:, 1, :], ALU.mult, ALU.add))
            dve.wait_ge(S("ld_const"), 16)

            def onehot(t, k):
                dve.tensor_scalar(ohS[:, k, :], iota[:, 0:N], edge_f[:, 0, bass.ds(t, 1)], None, ALU.is_equal)
                dve.tensor_scalar(ohD[:, k, :, :].rearrange("p r n -> p (r n)"), iota[:], key[:, bass.ds(t, 1)],
                                  None, ALU.is_equal).then_inc(S("oh_ready"), 1)

            for k in range(4):
                onehot(k, k)
            with dve.Fori(1, ET // 8) as g:
                for k in range(4):
                    dve.wait_ge(S("oh_used"), g * 4 + (k - 3))
                    onehot(g * 4 + k, k)
            dve.wait_ge(S("ld_x"), 16)
            for t in range(NT):
                ln_stats(0, t, x_in)
                for k in (2 * t, 2 * t + 1):
                    dve.wait_ge(S("oh_used"), ET // 2 + (k - 3))
                    onehot(ET // 2 + k, k)
            for t in range(NT):
                ln_norm(0, t, x_in, hnat0)
            with dve.Fori(ET // 8 + 1, ET // 4) as g:
                for k in range(4):
                    dve.wait_ge(S("oh_used"), g * 4 + (k - 3))
                    onehot(g * 4 + k, k)
            dve.wait_ge(S("ld_sel"), 16)
            dve.tensor_copy(sel[:, :, :].rearrange("p a b -> p (a b)"), sel32[:]).then_inc(S("sel_ready"), 1)
            dve.wait_ge(S("ld_eye"), 16)
            dve.tensor_copy(eyeR[:], identity).then_inc(S("eyeR_ready"), 1)
            dve.tensor_copy(ones[:], warm[:, 0:1].broadcast_to([P, P])).then_inc(S("ones_ready"), 1)
            ln_lo(0)
            dve.wait_ge(S("oh_used"), ET)
            for st in range(NT):
                c = cr[:, st, :, :].rearrange("p r n -> p (r n)")
                dve.tensor_copy(c[:, 0:512], ps[:, 4 + 2 * st, :]).then_inc(S("cnt_ready"), 1)
                dve.tensor_copy(c[:, 512:768], ps[:, 5 + 2 * st, 0:256]).then_inc(S("cnt_ready"), 1)
            dve.wait_ge(S("cnt_ready"), 4)
            link(dve.tensor_tensor(cnt[:], f(cr[:, :, 0, :]), f(cr[:, :, 1, :]), ALU.add))
            dve.tensor_tensor(cnt[:], cnt[:], f(cr[:, :, 2, :]), ALU.add).then_inc(S("cr_ready"), 1)
            dve.wait_ge(S("cr_ready"), 1)
            dve.tensor_tensor(cntS[:], cnt[:], eye[:], ALU.add).then_inc(S("cr_ready"), 1)
            for j in range(3):
                dve.wait_ge(S("qg_hi"), j + 1)
                q = banks(2 * (j % 2), 2).rearrange("p (a b) -> p a b", b=256)
                cs = slice(j * 256, (j + 1) * 256)
                dve.tensor_tensor(qgL[:, :, cs], q, f(qgH[:, :, cs]), ALU.subtract).then_inc(S("qg_lo"), 1)

            def relation_weights():
                dve.wait_ge(S("colsum_mm"), 1)
                w = inv[:, :, :].rearrange("p r n -> p (r n)")
                link(dve.tensor_scalar(w, banks(4, 2)[:, 0:768], 1.0, None, ALU.max))
                dve.reciprocal(w, w).then_inc(S("cn_ready"), 1)

            def update(g, ot):
                if ot % 2 == 0:
                    dve.wait_ge(S("root_mm"), 3 * g + ot // 2 + 1)
                else:
                    dve.wait_ge(S("w_used"), ROOT[g] + ot // 2 + 1)
                if ot == 0:
                    dve.wait_ge(S("cn_ready"), 1)
                if ot:
                    dve.wait_ge(S("root_sum"), KT * g + ot)
                src = banks(root_bank(ot), 2).rearrange("p (r n) -> p r n", n=N)
                link(dve.tensor_tensor(msg[:], src[:, 0:R, :], inv[:], ALU.mult))
                link(dve.tensor_tensor(msg[:, 2, :], msg[:, 2, :], src[:, R, :], ALU.add))
                link(dve.tensor_tensor(msg[:, 0, :], msg[:, 0, :], msg[:, 1, :], ALU.add))
                if ot >= 2:
                    dve.wait_ge(S("root_h"), KT * g + ot - 1)
                dve.tensor_tensor(upd[:, ot % 2, :], msg[:, 0, :], msg[:, 2, :], ALU.add).then_inc(S("root_sum"), 1)

            def node_split(g, j):
                dve.wait_ge(S("root_h"), KT * g + 2 * j + 2)
                o = slice(2 * j, 2 * j + 2)
                split((h2H[:, o, :], h2L[:, o, :]), h32[:, o, :]).then_inc(S("h2_ready"), 1)

            def edge_masks():
                dve.wait_ge(S("cntT_mm"), 1)
                cT = ps[:, 6, :].rearrange("p (t n) -> p t n", t=NT)
                link(dve.tensor_tensor(mask[:, 1, :, :], cT, eye[:], ALU.add))
                dve.tensor_reduce(deg[:], mask[:, 1, :, :], AX.X, ALU.add).then_inc(S("deg_ready"), 1)
                dve.wait_ge(S("deg_ready"), 1)
                dve.tensor_scalar(mask[:, 0, :, :], cT, 0.0, NO_EDGE, ALU.is_equal, ALU.mult).then_inc(S("mask_ready"), 1)
                dve.tensor_scalar(mask[:, 1, :, :], mask[:, 1, :, :], 0.0, NO_EDGE, ALU.is_equal, ALU.mult)\
                   .then_inc(S("mask_ready"), 1)

            for g in range(2):
                for j in range(9):
                    dve.wait_ge(S("rel_hi"), 9 * g + j + 1)
                    cs = slice(j * 256, (j + 1) * 256)
                    dve.tensor_tensor(xrL[:, :, cs], src_natural(rel_bank(g, j)),
                                      f(xrH[:, :, cs]), ALU.subtract).then_inc(S("rel_lo"), 1)
                    if g == 0 and j == 3:
                        relation_weights()
                    if g == 0 and j == 5:
                        edge_masks()
                if g == 0:
                    dve.wait_ge(S("sdeg"), 1)
                    link(dve.reciprocal(dinv[:], dinv[:]))
                for ot in range(KT):
                    update(g, ot)
                    if ot % 2 == 0 and ot:
                        node_split(g, ot // 2 - 1)
                node_split(g, 2)
                for j in range(3):
                    dve.wait_ge(S("hg_hi"), 3 * g + j + 1)
                    cs = slice(j * 256, (j + 1) * 256)
                    dve.tensor_tensor(hgL[:, :, cs], ps[:, 4 + j, :].rearrange("p (t w) -> p t w", t=NT),
                                      f(hgH[:, :, cs]), ALU.subtract).then_inc(S("hg_lo"), 1)
                base = g * B * CPB

                def mul(c, k, b, wait):
                    ft, half = (k % CPB) // 2, k % 2
                    dve.wait_ge(S("sig_ready"), c + 1)
                    if wait:
                        dve.wait_ge(S("fold_ready"), c - PR + 1)
                    q = qT[:, ft, bass.ds(b * LQ + half * 32, 32)]
                    dve.tensor_tensor(prod[:, k % PR, :].rearrange("p (l n) -> p l n", n=NB),
                                      banks(2 * (k % ZR), 2).rearrange("p (l n) -> p l n", n=NB),
                                      q.unsqueeze(2).broadcast_to([P, 32, NB]), ALU.mult).then_inc(S("mul_ready"), 1)

                def sums(b, q, red, n, par):
                    o = slice(2 * q, 2 * q + 2)
                    dst, hi, lo = (t[:, o, bass.ds(b * NB, NB)] for t in (th, qiH, qiL))
                    dve.wait_ge(S("red_done"), red)
                    dve.tensor_reduce(dst, ps[:, 6 + par, :]
                                      .rearrange("p (f l n) -> p f n l", l=8, n=NB), AX.X, ALU.add)\
                       .then_inc(S("sum_step"), 1)
                    dve.wait_ge(S("sum_step"), n)
                    dve.tensor_copy(hi, dst).then_inc(S("sum_hi"), 1)
                    dve.wait_ge(S("sum_hi"), n)
                    dve.tensor_tensor(lo, dst, f(hi), ALU.subtract).then_inc(S("qi_ready"), 1)

                def graph_pair(c0, b0, first_pair):
                    for k in range(2 * CPB):
                        mul(c0 + k, k, b0 + k // CPB, not (first_pair and k < PR))
                        grp = (k - 7) // GC
                        if k % GC == GC - 1 and (grp >= 0 or not first_pair):
                            sums(b0 + grp // 3, grp % 3, c0 + GC * (grp + 1), b0 * 3 + (grp + 1 + 3 * g * B), grp % 2)

                graph_pair(base, 0, True)
                with dve.Fori(1, B // 2) as bp:
                    graph_pair(bp * (2 * CPB) + base, bp * 2, False)
                sums(B - 1, 2, base + B * CPB, 3 * B * (g + 1), 1)
                dve.wait_ge(S("th_ready"), g + 1)
                for j in range(3):
                    o = slice(2 * j, 2 * j + 2)
                    dve.wait_ge(S("alpha_ready"), 6 * g + 2 * j + 2)
                    t2 = th[:, o, :]
                    link(dve.tensor_tensor(t2, t2, h32[:, o, :], ALU.subtract))
                    link(dve.tensor_tensor(t2, t2, al32[:, j, :].rearrange("p (o n) -> p o n", o=2), ALU.mult))
                    dve.tensor_tensor(t2, t2, h32[:, o, :], ALU.add).then_inc(S("hn_ready"), 1)
                    if g == 0:
                        dve.wait_ge(S("hn_ready"), j + 1)
                        split((hT[0][0][:, o, :], hT[0][1][:, o, :]), t2).then_inc(S("hn_lo"), 1)

            dve.wait_ge(S("x_res"), 16)
            for t in range(NT):
                dve.wait_ge(S("hnT"), t + 1)
                x2 = x[:, t, :].rearrange("p (f w) -> p f w", f=2)
                dve.tensor_tensor(x2, x2, ps[:, 2 * t:2 * t + 2, 0:384], ALU.add).then_inc(S("x_ready"), 1)
                dve.wait_ge(S("x_ready"), t + 1)
                ln_stats(1, t, x)

            tiles, nh, rows = [0], [0], [0]

            def tile_al(q, cols, arow, per):
                j = cols // 256
                dve.wait_ge(S("gh_hi"), tiles[0] + 1)
                tiles[0] += 1
                for v in range(2):
                    m = dve.tensor_tensor(tmp[:, 2 * v:2 * v + 2, :], q,
                                          arow[:, v, cols:cols + 256].unsqueeze(1).broadcast_to([P, NT, 256]), ALU.mult)
                link(m)
                link(dve.tensor_reduce(alp[:, :, :, per * j:per * (j + 1)].rearrange("p v t a -> p (v t) a"),
                                       tmp[:, :, :].rearrange("p v (a c) -> p v a c", a=per), AX.X, ALU.add))

            def tile_lo(q, cols):
                dve.tensor_tensor(hL[:, :, cols:cols + 256], q, f(hH[:, :, cols:cols + 256]), ALU.subtract)\
                   .then_inc(S("gh_free"), 1)

            def tiles_of(n, src, arow, per, *rest):
                for j in range(n):
                    tile_al(src(j), j * 256, arow, per)
                    if j < n - 1:
                        tile_lo(src(j), j * 256)
                begin(*rest, lambda: tile_lo(src(n - 1), (n - 1) * 256))

            def src_units(j):
                return src_natural(ubank(j))

            def ones_column():
                dve.tensor_copy(hH[:, :, D:D + 2], warm[:, 0:1].unsqueeze(1).broadcast_to([P, NT, 2]))
                dve.memset(f(hL[:, :, D:D + 2]), 0.0)

            def begin(a, heads, nparts, last_low):
                dve.tensor_reduce(al[:, :, :, 0:heads].rearrange("p v t h -> p (v t) h"),
                                  alp[:, :, :, 0:heads * nparts].rearrange("p v t (h k) -> p (v t) h k", k=nparts),
                                  AX.X, ALU.add).then_inc(S("al_ready"), 1)
                last_low()
                dve.wait_ge(S("al_ready"), a + 1)
                if heads > 1:
                    dve.wait_ge(S("alT_mm"), a // 2 + 1)
                    split(tuple(q[0:heads, :] for q in aT), ps[0:heads, 6, 0:N]).then_inc(S("alT_ready"), 1)
                dve.tensor_scalar(als2[:, :, 0:heads], al[:, 0, :, 0:heads], SLOPE, None, ALU.mult)
                link(dve.tensor_scalar(als8[:, :, 0:heads], al[:, 0, :, 0:heads], 1.0 - SLOPE, None, ALU.mult))

            def maxima(h, heads, msk):
                if h % 2 == 0:
                    rows[0] += 1
                    dve.wait_ge(S("als_rows"), rows[0])
                row = ps[:, h // 2, (h % 2) * N:(h % 2 + 1) * N] if heads > 1 else ps[:, 0, 0:N]
                for dt in range(NT):
                    m = dve.tensor_tensor_reduce(junk[2 * h + dt], row, mask[:, msk, dt, :], 1.0, -3.0e38,
                                                 ALU.add, ALU.max, mx[:, dt, h:h + 1])
                steps[0] += 1
                m.then_inc(S("chain"), 1)
                last_max[0] = steps[0]

            def terms(q, gs):
                dve.wait_ge(S("chain"), last_max[0])
                hs_ = slice(q * gs, (q + 1) * gs)
                link(dve.tensor_tensor(xs[:, :, hs_], mx[:, :, hs_], al[:, 1, :, hs_], ALU.add))
                link(dve.scalar_tensor_tensor(ms[:, :, hs_], xs[:, :, hs_], SLOPE, xs[:, :, hs_], ALU.mult, ALU.max))
                c0 = 2 * gs * q
                dve.tensor_tensor(bb[:, :, c0:c0 + gs], al[:, 1, :, hs_], ms[:, :, hs_], ALU.subtract)
                dve.scalar_tensor_tensor(bb[:, :, c0 + gs:c0 + 2 * gs], al[:, 1, :, hs_], SLOPE, ms[:, :, hs_],
                                         ALU.mult, ALU.subtract).then_inc(S("b_ready"), 1)

            last_max = [None]

            def exponents(h, bank):
                k, s = nh[0] + h, h % ES
                dve.wait_ge(S("row_copied"), k + 1)
                for st in range(NT):
                    m = dve.scalar_tensor_tensor(e[:, s, st, :], ps[:, bank, 0:N], als8[:, st, h:h + 1],
                                                 e[:, s, 1, :], ALU.add, ALU.max)
                m.then_inc(S("arg_ready"), 1)

            def weights_of(h, c):
                s = h % ES
                dve.wait_ge(S("exps_ready"), nh[0] + h + 1)
                dve.scalar_tensor_tensor(e[:, s, :, :], e[:, s, :, :], 1.0, c, ALU.min, ALU.mult)\
                   .then_inc(S("pt_ready"), 1)

            def attention_T(a, heads, gs, zg, cw, nct, msk, c, done, order):
                heads0, steps0, pairs0, inv0 = done

                def split_terms(q):
                    dve.wait_ge(S("bT_mm"), 2 * (a // 2) + q + 1)
                    split(tuple(w[0:2 * gs, q, :] for w in bT), ps[0:2 * gs, 6 + q, (1 - q) * N:(2 - q) * N])\
                        .then_inc(S("bT_ready"), 1)

                def inverse(q):
                    dve.wait_ge(S("zT_mm"), inv0 + q + 1)
                    link(dve.tensor_scalar(z32[0:heads, :], ps[0:heads, 6, q * N:(q + 1) * N], EPTSSM, None, ALU.add))
                    link(dve.reciprocal(z32[0:heads, :], z32[0:heads, :]))
                    if q:
                        dve.wait_ge(S("rz_mm"), pairs0 + zg // 2)
                    split(tuple(w[0:heads, :] for w in rzT), z32[0:heads, :]).then_inc(S("rzT_ready"), 1)

                def normalise(p):
                    h = 2 * p // nct
                    if nct == 1:
                        dve.wait_ge(S("out_mm"), heads0 + h + 2)
                    elif p % 2:
                        dve.wait_ge(S("out_mm"), heads0 + h + 1)
                    else:
                        dve.wait_ge(S("out_half"), h + 1)
                    dve.wait_ge(S("rz_ready"), pairs0 + h // 2 + 1)
                    b, half = divmod(out_at(h, nct), 2)
                    if nct == 1:
                        src, by = ps[0:cw, b:b + 2, half * N:(half + 1) * N], rz[0:cw, h // 2 % 2, :, :]
                    else:
                        src = ps[:, b + p % 2, :].rearrange("p (c n) -> p c n", n=N)
                        by = rz[:, h // 2 % 2, h % 2, :].unsqueeze(1).broadcast_to([P, 2, N])
                    dve.tensor_tensor(u[0:cw, p % SU, :, :], src, by, ALU.mult).then_inc(S("u_ready"), 1)

                def elu(p):
                    s = p % SU
                    dve.wait_ge(S("act_u"), steps0 + p + 1)
                    uu, rr = u[0:cw, s, :, :], ru[0:cw, s, :, :]
                    link(dve.tensor_scalar(uu, uu, 1.0, -1.0, ALU.min, ALU.add))
                    link(dve.tensor_tensor(rr, rr, uu, ALU.add))
                    dve.tensor_copy(gTH[0:cw, 2 * p:2 * p + 2, :], rr).then_inc(S("elu_ready"), 1)

                for step in order.split():
                    k = int(step[1])
                    {"x": lambda k: maxima(k, heads, msk), "B": lambda k: terms(k, gs), "T": split_terms,
                     "m": lambda k: exponents(k, 4 + k % 2), "w": lambda k: weights_of(k, c),
                     "i": inverse, "n": normalise, "g": elu}[step[0]](k)
                nh[0] += heads

            def attention_1(msk, c):
                maxima(0, 1, msk)
                terms(0, 1)
                exponents(0, 7)
                weights_of(0, c)
                k = nh[0]
                dve.wait_ge(S("pt_ready"), k + 1)
                dve.tensor_copy(ptH[:, 0, :, :], e[:, 0, :, :]).then_inc(S("pt_hi"), 1)
                dve.wait_ge(S("pt_hi"), k + 1)
                dve.tensor_tensor(ptL[:, 0, :, :], e[:, 0, :, :], f(ptH[:, 0, :, :]), ALU.subtract)\
                   .then_inc(S("pt_lo"), 1)
                nh[0] += 1

            def finish(k, scale_z):
                dve.wait_ge(S("brow_in"), 16 * (k + 1))
                link(dve.tensor_tensor(x[:], x[:], brow[:].unsqueeze(1).broadcast_to([P, NT, D]), ALU.add))
                scale, b0 = (zr, 0) if scale_z else (dinv, 4)
                for dt in range(NT):
                    dve.wait_ge(S("fin_mm"), 2 * k + dt + 1)
                    if scale_z:
                        link(dve.tensor_scalar(zr[:, dt:dt + 1], ps[:, 2 * dt + 1, 384:385], EPTSSM, None, ALU.add))
                        link(dve.reciprocal(zr[:, dt:dt + 1], zr[:, dt:dt + 1]))
                    for fc in range(2):
                        cs = slice(fc * 384, fc * 384 + 384)
                        m = dve.scalar_tensor_tensor(x[:, dt, cs], ps[:, b0 + 2 * dt + fc, 0:384], scale[:, dt:dt + 1],
                                                     x[:, dt, cs], ALU.mult, ALU.add)
                    m.then_inc(S("lay_half"), 1)
                    if scale_z:
                        dve.wait_ge(S("lay_half"), 2 * k + dt + 1)
                        ln_stats(k + 2, dt, x)

            for t in range(NT):
                ln_norm(1, t, x, hnat1)
            ln_lo(1)
            dve.wait_ge(S("arow1_in"), 16)
            dve.wait_ge(S("mask_ready"), 2)
            dve.wait_ge(S("zero_step"), 2)
            tiles_of(3, src_natural, arow1, 8, 0, H1, 3)
            attention_T(0, H1, 4, H1, C1, 1, 0, cnt[:], (0, 0, 0, 0),
                        "x0 x1 x2 x3 B0 x4 x5 T0 x6 m0 m1 x7 B1 w0 w1 m2 T1 m3 w2 m4 w3 m5 w4 m6 w5 m7 w6 w7 "
                        "i0 n0 n1 g0 n2 g1 n3 g2 g3")
            ones_column()
            dve.wait_ge(S("arow2_in"), 16)
            tiles_of(3, src_units, arow2, 1, 1, 1, 3)
            attention_1(0, cnt[:])
            finish(0, True)
            for t in range(NT):
                ln_norm(2, t, x, hnat1)
            ln_lo(2)
            dve.wait_ge(S("arow1_in"), 32)
            tiles_of(8, lambda j: src_natural(j % 4), arow1, 1, 2, H2, 2)
            attention_T(2, H2, 2, 2, P, 4, 1, f(cntS[:]), (H1, H1 // 2, H1 // 2, 1),
                        "x0 x1 B0 x2 x3 T0 B1 m0 m1 T1 w0 w1 m2 m3 w2 i0 w3 n0 n1 n2 n3 i1 g0 g1 n4 n5 g2 g3 "
                        "n6 n7 g4 g5 g6 g7")
            ones_column()
            dve.wait_ge(S("arow2_in"), 32)
            tiles_of(3, src_units, arow2, 1, 3, 1, 3)
            attention_1(1, f(cntS[:]))
            finish(1, True)
            for t in range(NT):
                ln_norm(3, t, x, hnat1)
            ln_lo(3)
            for j in range(3):
                dve.wait_ge(S("gh_hi"), tiles[0] + 1)
                tiles[0] += 1
                for t in range(NT):
                    cs = slice(j * 256, (j + 1) * 256)
                    m = dve.scalar_tensor_tensor(hL[:, t, cs], ps[:, j, t * 256:(t + 1) * 256], dinv[:, t:t + 1],
                                                 f(hH[:, t, cs]), ALU.mult, ALU.subtract)
                m.then_inc(S("gh_lo"), 1)
            finish(2, False)


def kernel(x, src, dst, edge_type_3, L0_gnn_query_embs, L0_gnn_W_rel1, L0_gnn_W_root1, L0_gnn_b1, L0_gnn_W_rel2,
           L0_gnn_W_root2, L0_gnn_b2, L0_gnn_Wg, L0_gnn_bg, L0_gnn_Wq, L0_gnn_bq, L1_gnn_W1, L1_gnn_a_src1,
           L1_gnn_a_dst1, L1_gnn_b1, L1_gnn_W2, L1_gnn_a_src2, L1_gnn_a_dst2, L1_gnn_b2, L2_gnn_W1, L2_gnn_att_src1,
           L2_gnn_att_dst1, L2_gnn_b1, L2_gnn_W2, L2_gnn_att_src2, L2_gnn_att_dst2, L2_gnn_b2, L3_gnn_W, L3_gnn_b):
    import numpy as np
    import concourse.bacc as bacc
    from concourse.bass_utils import run_bass_kernel_spmd

    a = np.asarray

    def blocks(w):
        w = a(w)
        m = w.shape[1] // 256
        return w.reshape(KT, P, m, 256).transpose(2, 1, 0, 3).reshape(m, P, BLK)

    def interleave(p, q):
        return np.stack([p, q], 1).reshape(-1, P, BLK)

    def units(w, rows):
        w = a(w)
        k = w.shape[0] // rows
        v = w.reshape(k, rows, 3, 256)
        v = np.stack([v[kt, :, cb] for kt, cb in unit_order(k)]).reshape(3 * k // UPB, UPB, rows, 256)
        full = np.zeros((v.shape[0], P, BLK), v.dtype)
        full[:, :rows] = v.transpose(0, 2, 1, 3).reshape(v.shape[0], rows, BLK)
        return full

    wg, wq = a(L0_gnn_Wg).T, a(L0_gnn_Wq).T
    stream = [blocks(wg[D:])]
    for w_rel, w_root in ((L0_gnn_W_rel1, L0_gnn_W_root1), (L0_gnn_W_rel2, L0_gnn_W_root2)):
        stream += [blocks(w) for w in a(w_rel)] + [blocks(w_root), blocks(wg[:D]),
                                                   interleave(blocks(wq[:D]), blocks(wq[D:]))]
    stream += [blocks(L1_gnn_W1), units(L1_gnn_W2, C1), blocks(L2_gnn_W1), units(L2_gnn_W2, P), blocks(L3_gnn_W)]

    bcol = np.zeros((P, 48), np.float32)
    for c0, b in ((0, L0_gnn_b1), (6, L0_gnn_b2), (12, L0_gnn_bg), (18, L0_gnn_bq)):
        bcol[:, c0:c0 + KT] = a(b).reshape(KT, P).T
    bcol[:C1, 24:32] = a(L1_gnn_b1).reshape(H1, C1).T
    bcol[:, 32:48] = a(L2_gnn_b1).reshape(CT2, P).T

    eye32 = np.eye(32, dtype=np.float32)
    node = np.tile(eye32, (1, 32))
    token = np.repeat(eye32, NB, axis=1)
    arrays = {
        "x": a(x),
        "edges": np.stack([a(src), a(dst), a(edge_type_3)]).reshape(3, P, ET),
        "iota": np.tile(np.arange(R * N, dtype=np.float16), (P, 1)),
        "eye": np.eye(N, dtype=np.float32).reshape(NT, P, N).transpose(1, 0, 2),
        "sel": np.concatenate([node, node, token, token]),
        "qT": a(L0_gnn_query_embs).reshape(B * LQ, KT, P).transpose(2, 1, 0),
        "bcol": bcol,
        "weights": np.concatenate(stream),
        "att11": np.stack([a(L1_gnn_a_src1).reshape(-1), a(L1_gnn_a_dst1).reshape(-1)]),
        "att12": np.stack([a(L1_gnn_a_src2).reshape(-1), a(L1_gnn_a_dst2).reshape(-1)]),
        "att21": np.stack([a(L2_gnn_att_src1).reshape(-1), a(L2_gnn_att_dst1).reshape(-1)]),
        "att22": np.stack([a(L2_gnn_att_src2).reshape(-1), a(L2_gnn_att_dst2).reshape(-1)]),
        "brow1": a(L1_gnn_b2), "brow2": a(L2_gnn_b2), "brow3": a(L3_gnn_b),
    }
    arrays = {k: np.ascontiguousarray(v) for k, v in arrays.items()}
    nc = bacc.Bacc("TRN2", target_bir_lowering=False, num_devices=1)
    ins = {k: nc.dram_tensor(f"in_{k}", v.shape, mybir.dt.from_np(v.dtype), kind="ExternalInput").ap()
           for k, v in arrays.items()}
    out = nc.dram_tensor("out", (N, D), F32, kind="ExternalOutput").ap()
    build(nc, ins, out)
    res = run_bass_kernel_spmd(nc, [{f"in_{k}": v for k, v in arrays.items()}], core_ids=[0])
    return res.results[0]["out"]
```
